# Optimizing a Trainium2 kernel written in Bass

```python
import numpy as np
import jax
import jax.numpy as jnp

def _softmax(x, axis=-1):
    return jax.nn.softmax(x, axis=axis)

def _gelu(x):
    return jax.nn.gelu(x, approximate=True)

def _silu(x):
    return jax.nn.silu(x)

def _sigmoid(x):
    return jax.nn.sigmoid(x)

def _layernorm(x, axis=-1, eps=1e-05):
    m = jnp.mean(x, axis=axis, keepdims=True)
    v = jnp.var(x, axis=axis, keepdims=True)
    return (x - m) / jnp.sqrt(v + eps)

def _scatter_add(tgt, idx, src, axis=0):
    return tgt.at[idx].add(src)

def _segment_sum(src, seg, n):
    return jax.ops.segment_sum(src, seg, n)
kernel_name = 'mk_vit_tower_d1_tok_img256_r4_f95d22'

def setup_inputs(seed: int=0):
    np.random.seed(seed)
    _w = jnp.asarray

    def _rec_inputs():
        import jax
        import jax.numpy as jnp
        _rk = jax.random.key(seed)
        x = -0.000125008 + 0.999885 * jax.random.normal(jax.random.fold_in(_rk, 1), (4, 64, 64, 64), jnp.float32)
        return x
    x = _rec_inputs()

    def _L0_tok_setup():
        import jax, jax.numpy as jnp
        import numpy as np
        DIM = 64
        NH = 8
        WH, WW = (8, 8)

        def _rope_axis(x, axis):
            half = x.shape[-1]
            inv_freq = 1.0 / 10000.0 ** (jnp.arange(0, half, 2, dtype=jnp.float32) / half)
            pos = jnp.arange(x.shape[axis], dtype=jnp.float32)
            ang = pos[:, None] * inv_freq
            cos, sin = (jnp.cos(ang), jnp.sin(ang))
            shape = [1, 1, 1, ang.shape[-1]]
            shape[axis] = ang.shape[0]
            cos = cos.reshape(shape).astype(x.dtype)
            sin = sin.reshape(shape).astype(x.dtype)
            x1, x2 = (x[..., 0::2], x[..., 1::2])
            r1 = x1 * cos - x2 * sin
            r2 = x1 * sin + x2 * cos
            return jnp.stack([r1, r2], axis=-1).reshape(x.shape)

        def _rope2(x):
            half = x.shape[-1] // 2
            return jnp.concatenate([_rope_axis(x[..., :half], 1), _rope_axis(x[..., half:], 2)], axis=-1)
        key = jax.random.key(seed)
        ks = jax.random.split(key, 5)
        B, H, W, C = (32, 64, 64, DIM)
        s = 1.0 / np.sqrt(C)
        return {'x': jax.random.normal(ks[0], (B, H, W, C), dtype=jnp.float32), 'qkv_w': jax.random.uniform(ks[1], (3 * C, C), jnp.float32, -s, s), 'qkv_b': jax.random.uniform(ks[2], (3 * C,), jnp.float32, -s, s), 'proj_w': jax.random.uniform(ks[3], (C, C), jnp.float32, -s, s), 'proj_b': jax.random.uniform(ks[4], (C,), jnp.float32, -s, s)}
    _L0_tok_all = _L0_tok_setup()
    _L0_tok_in = {k: v for k, v in _L0_tok_all.items() if k in ('qkv_w', 'qkv_b', 'proj_w', 'proj_b')}
    del _L0_tok_all

    def _L0_attn_setup():
        import jax, jax.numpy as jnp
        import numpy as np
        I, H, O, L = (64, 128, 64, 2)
        B, S = (16, 512)
        EPS = 1e-05

        def _layernorm(x, w, b):
            mu = jnp.mean(x, axis=-1, keepdims=True)
            var = jnp.mean(jnp.square(x - mu), axis=-1, keepdims=True)
            return (x - mu) * jax.lax.rsqrt(var + EPS) * w + b
        key = jax.random.key(seed)
        ks = jax.random.split(key, 16)
        s_in = 1.0 / np.sqrt(I)
        s_h = 1.0 / np.sqrt(H)
        return {'x': jax.random.normal(ks[0], (B, S, I), dtype=jnp.float32), 'in_W': jax.random.uniform(ks[1], (H, I), minval=-s_in, maxval=s_in, dtype=jnp.float32), 'in_b': jax.random.uniform(ks[2], (H,), minval=-s_in, maxval=s_in, dtype=jnp.float32), 'A_W': jax.random.uniform(ks[3], (L, H, H), minval=-s_h, maxval=s_h, dtype=jnp.float32), 'B_W': jax.random.uniform(ks[4], (L, H, H), minval=-s_h, maxval=s_h, dtype=jnp.float32), 'B_b': jax.random.uniform(ks[5], (L, H), minval=-s_h, maxval=s_h, dtype=jnp.float32), 'C_W': jax.random.uniform(ks[6], (L, H, H), minval=-s_h, maxval=s_h, dtype=jnp.float32), 'C_b': jax.random.uniform(ks[7], (L, H), minval=-s_h, maxval=s_h, dtype=jnp.float32), 'D_W': jax.random.uniform(ks[8], (L, H, H), minval=-s_h, maxval=s_h, dtype=jnp.float32), 'D_b': jax.random.uniform(ks[9], (L, H), minval=-s_h, maxval=s_h, dtype=jnp.float32), 'ln_w': jnp.ones((L, H), dtype=jnp.float32), 'ln_b': jnp.zeros((L, H), dtype=jnp.float32), 'out_W': jax.random.uniform(ks[10], (O, H), minval=-s_h, maxval=s_h, dtype=jnp.float32), 'out_b': jax.random.uniform(ks[11], (O,), minval=-s_h, maxval=s_h, dtype=jnp.float32)}
    _L0_attn_all = _L0_attn_setup()
    _L0_attn_in = {k: v for k, v in _L0_attn_all.items() if k in ('in_W', 'in_b', 'A_W', 'B_W', 'B_b', 'C_W', 'C_b', 'D_W', 'D_b', 'ln_w', 'ln_b', 'out_W', 'out_b')}
    del _L0_attn_all

    def _L0_ffn_setup():
        import jax, jax.numpy as jnp
        import numpy as np
        B, T, IN_DIM = (64, 64, 64)
        HID, OUT_DIM = (128, 64)
        N_LAYERS, N_EXPERTS, N_SHARED = (2, 16, 1)
        key = jax.random.key(seed)
        ks = jax.random.split(key, 10)
        s = 0.02
        x = jax.random.normal(ks[0], (B, T, IN_DIM), dtype=jnp.float32)
        route_id = jax.random.randint(ks[1], (B,), 0, N_EXPERTS)
        Wi = jax.random.normal(ks[2], (HID, IN_DIM), dtype=jnp.float32) * s
        bi = jnp.zeros((HID,), dtype=jnp.float32)
        Wr = jax.random.normal(ks[3], (N_LAYERS, N_EXPERTS, HID, HID), dtype=jnp.float32) * s
        br = jax.random.normal(ks[4], (N_LAYERS, N_EXPERTS, HID), dtype=jnp.float32) * s
        Ws = jax.random.normal(ks[5], (N_LAYERS, N_SHARED, HID, HID), dtype=jnp.float32) * s
        bs = jax.random.normal(ks[6], (N_LAYERS, N_SHARED, HID), dtype=jnp.float32) * s
        Wo = jax.random.normal(ks[7], (OUT_DIM, HID), dtype=jnp.float32) * s
        bo = jnp.zeros((OUT_DIM,), dtype=jnp.float32)
        return {'x': x, 'route_id': route_id, 'Wi': Wi, 'bi': bi, 'Wr': Wr, 'br': br, 'Ws': Ws, 'bs': bs, 'Wo': Wo, 'bo': bo}
    _L0_ffn_all = _L0_ffn_setup()
    _L0_ffn_in = {k: v for k, v in _L0_ffn_all.items() if k in ('route_id', 'Wi', 'bi', 'Wr', 'br', 'Ws', 'bs', 'Wo', 'bo')}
    del _L0_ffn_all
    return {'x': x, 'L0_tok_qkv_w': _L0_tok_in['qkv_w'], 'L0_tok_qkv_b': _L0_tok_in['qkv_b'], 'L0_tok_proj_w': _L0_tok_in['proj_w'], 'L0_tok_proj_b': _L0_tok_in['proj_b'], 'L0_attn_in_W': _L0_attn_in['in_W'], 'L0_attn_in_b': _L0_attn_in['in_b'], 'L0_attn_A_W': _L0_attn_in['A_W'], 'L0_attn_B_W': _L0_attn_in['B_W'], 'L0_attn_B_b': _L0_attn_in['B_b'], 'L0_attn_C_W': _L0_attn_in['C_W'], 'L0_attn_C_b': _L0_attn_in['C_b'], 'L0_attn_D_W': _L0_attn_in['D_W'], 'L0_attn_D_b': _L0_attn_in['D_b'], 'L0_attn_ln_w': _L0_attn_in['ln_w'], 'L0_attn_ln_b': _L0_attn_in['ln_b'], 'L0_attn_out_W': _L0_attn_in['out_W'], 'L0_attn_out_b': _L0_attn_in['out_b'], 'L0_ffn_route_id': _L0_ffn_in['route_id'], 'L0_ffn_Wi': _L0_ffn_in['Wi'], 'L0_ffn_bi': _L0_ffn_in['bi'], 'L0_ffn_Wr': _L0_ffn_in['Wr'], 'L0_ffn_br': _L0_ffn_in['br'], 'L0_ffn_Ws': _L0_ffn_in['Ws'], 'L0_ffn_bs': _L0_ffn_in['bs'], 'L0_ffn_Wo': _L0_ffn_in['Wo'], 'L0_ffn_bo': _L0_ffn_in['bo']}

def reference(x, L0_tok_qkv_w, L0_tok_qkv_b, L0_tok_proj_w, L0_tok_proj_b, L0_attn_in_W, L0_attn_in_b, L0_attn_A_W, L0_attn_B_W, L0_attn_B_b, L0_attn_C_W, L0_attn_C_b, L0_attn_D_W, L0_attn_D_b, L0_attn_ln_w, L0_attn_ln_b, L0_attn_out_W, L0_attn_out_b, L0_ffn_route_id, L0_ffn_Wi, L0_ffn_bi, L0_ffn_Wr, L0_ffn_br, L0_ffn_Ws, L0_ffn_bs, L0_ffn_Wo, L0_ffn_bo):
    import jax
    import jax.numpy as jnp

    def _L0_tok_ref(x, qkv_w, qkv_b, proj_w, proj_b):
        import jax, jax.numpy as jnp
        import numpy as np
        DIM = 64
        NH = 8
        WH, WW = (8, 8)

        def _rope_axis(x, axis):
            half = x.shape[-1]
            inv_freq = 1.0 / 10000.0 ** (jnp.arange(0, half, 2, dtype=jnp.float32) / half)
            pos = jnp.arange(x.shape[axis], dtype=jnp.float32)
            ang = pos[:, None] * inv_freq
            cos, sin = (jnp.cos(ang), jnp.sin(ang))
            shape = [1, 1, 1, ang.shape[-1]]
            shape[axis] = ang.shape[0]
            cos = cos.reshape(shape).astype(x.dtype)
            sin = sin.reshape(shape).astype(x.dtype)
            x1, x2 = (x[..., 0::2], x[..., 1::2])
            r1 = x1 * cos - x2 * sin
            r2 = x1 * sin + x2 * cos
            return jnp.stack([r1, r2], axis=-1).reshape(x.shape)

        def _rope2(x):
            half = x.shape[-1] // 2
            return jnp.concatenate([_rope_axis(x[..., :half], 1), _rope_axis(x[..., half:], 2)], axis=-1)
        B, H, W, C = x.shape
        hd = C // NH
        N = WH * WW
        xw = x.reshape(B, H // WH, WH, W // WW, WW, C).transpose(0, 1, 3, 2, 4, 5).reshape(-1, N, C)
        qkv = xw @ qkv_w.T + qkv_b
        qkv = qkv.reshape(-1, N, 3, NH, hd).transpose(2, 0, 3, 1, 4)
        q, k, v = (qkv[0], qkv[1], qkv[2])
        q = _rope2(q.reshape(-1, WH, WW, hd)).reshape(-1, NH, N, hd)
        k = _rope2(k.reshape(-1, WH, WW, hd)).reshape(-1, NH, N, hd)
        scale = hd ** (-0.5)
        attn = jax.nn.softmax(q * scale @ jnp.swapaxes(k, -2, -1), axis=-1)
        out = (attn @ v).transpose(0, 2, 1, 3).reshape(-1, N, C)
        out = out.reshape(B, H // WH, W // WW, WH, WW, C).transpose(0, 1, 3, 2, 4, 5).reshape(B, H * W, C)
        return out @ proj_w.T + proj_b

    def _L0_attn_ref(x, in_W, in_b, A_W, B_W, B_b, C_W, C_b, D_W, D_b, ln_w, ln_b, out_W, out_b):
        import jax, jax.numpy as jnp
        import numpy as np
        I, H, O, L = (64, 128, 64, 2)
        B, S = (16, 512)
        EPS = 1e-05

        def _layernorm(x, w, b):
            mu = jnp.mean(x, axis=-1, keepdims=True)
            var = jnp.mean(jnp.square(x - mu), axis=-1, keepdims=True)
            return (x - mu) * jax.lax.rsqrt(var + EPS) * w + b
        x = jnp.einsum('bsi,hi->bsh', x, in_W) + in_b
        bsz = x.shape[0]
        for l in range(L):
            bx = jnp.einsum('bsh,gh->bsg', x, B_W[l]) + B_b[l]
            dx = jnp.einsum('bsh,gh->bsg', x, D_W[l]) + D_b[l]
            Al = A_W[l]

            def step(h, bxt):
                h = jnp.tanh(h @ Al.T + bxt)
                return (h, h)
            h0 = jnp.zeros((bsz, H), dtype=x.dtype)
            _, hs = jax.lax.scan(step, h0, jnp.swapaxes(bx, 0, 1))
            hs = jnp.swapaxes(hs, 0, 1)
            y = jnp.einsum('bsh,gh->bsg', hs, C_W[l]) + C_b[l] + dx
            x = _layernorm(x + y, ln_w[l], ln_b[l])
        return jnp.einsum('bsh,oh->bso', x, out_W) + out_b

    def _L0_ffn_ref(x, route_id, Wi, bi, Wr, br, Ws, bs, Wo, bo):
        import jax, jax.numpy as jnp
        import numpy as np
        B, T, IN_DIM = (64, 64, 64)
        HID, OUT_DIM = (128, 64)
        N_LAYERS, N_EXPERTS, N_SHARED = (2, 16, 1)
        flat = x.reshape(-1, x.shape[-1])
        n_tok = flat.shape[0]
        route = jnp.repeat(route_id, n_tok // route_id.shape[0])
        h = jax.nn.relu(flat @ Wi.T + bi)
        n_layers, n_experts = (Wr.shape[0], Wr.shape[1])
        for l in range(n_layers):
            shared = (jnp.einsum('nd,shd->snh', h, Ws[l]) + bs[l][:, None, :]).mean(axis=0)
            routed = jnp.zeros_like(h)
            for e in range(n_experts):
                ye = h @ Wr[l, e].T + br[l, e]
                routed = routed + jnp.where((route == e)[:, None], ye, 0.0)
            h = jax.nn.relu(shared + routed + h)
        out = h @ Wo.T + bo
        return out.reshape(*x.shape[:-1], out.shape[-1])
    h = _L0_tok_ref(x, L0_tok_qkv_w, L0_tok_qkv_b, L0_tok_proj_w, L0_tok_proj_b)
    h = h + _L0_attn_ref(_layernorm(h, axis=-1), L0_attn_in_W, L0_attn_in_b, L0_attn_A_W, L0_attn_B_W, L0_attn_B_b, L0_attn_C_W, L0_attn_C_b, L0_attn_D_W, L0_attn_D_b, L0_attn_ln_w, L0_attn_ln_b, L0_attn_out_W, L0_attn_out_b)
    h = h + _L0_ffn_ref(_layernorm(h, axis=-1), L0_ffn_route_id, L0_ffn_Wi, L0_ffn_bi, L0_ffn_Wr, L0_ffn_br, L0_ffn_Ws, L0_ffn_bs, L0_ffn_Wo, L0_ffn_bo)
    return h

_drawn_inputs = setup_inputs


def setup_inputs(seed=0):
    import zlib

    import numpy as np

    out = dict(_drawn_inputs(seed))
    spreads = {'L0_attn_ln_w': (1.0, 0.2),
     'L0_attn_ln_b': (0.0, 0.1),
     'L0_ffn_bi': (0.0, 0.1),
     'L0_ffn_bo': (0.0, 0.1)}
    factors = {'L0_ffn_Wr': 3.959, 'L0_ffn_br': 6.664, 'L0_ffn_Ws': 3.732, 'L0_ffn_bs': 5.904}
    for name, (base, spread) in spreads.items():
        noise = np.random.default_rng([zlib.crc32(name.encode()), seed]).standard_normal(out[name].shape)
        drawn = base * np.exp(spread * noise) if base else spread * noise
        out[name] = jnp.asarray(drawn.astype(out[name].dtype))
    for name, factor in factors.items():
        out[name] = (out[name] * factor).astype(out[name].dtype)
    return out
```

```python
import numpy as np
import concourse.bass as bass
from concourse import mybir
from contextlib import ExitStack


class Names:
    pass


BATCH, ROWS, COLS, FEAT = 4, 64, 64, 64
HALF = 2
BROWS = (BATCH // HALF) * ROWS
WIN = 8
NPOS = WIN * WIN
HEADS, HD = 8, 8
PAIRS = (BROWS // WIN) * (COLS // WIN)
TILES = BROWS // WIN
PPT = PAIRS // TILES
HID = 128
LAYERS = 2
EXPERTS = 16
CHUNKS = BATCH * ROWS
WARM = 24
TOL = 2.0 ** -20
SEGS = 64
SEG = BATCH * ROWS * COLS // SEGS
SEG_ROWS = SEG // COLS
EPS = 1e-5
NT = 512

C_IDENT, C_CENT64, C_MEAN64, C_CENT128, C_MEAN128, C_SWAP = (128 * n for n in range(6))
C_STACK = 768
C_MASK = C_STACK + NPOS
C_COSQ = C_MASK + HEADS
C_SINQ, C_COSK, C_SINK = C_COSQ + 64, C_COSQ + 128, C_COSQ + 192
C_END = C_COSQ + 256


def shape_constants():
    c = np.zeros((128, C_END), np.float32)
    eye = np.eye(128, dtype=np.float32)
    bd = np.kron(np.eye(2), np.ones((64, 64))).astype(np.float32) / 64
    c[:, C_IDENT:C_IDENT + 128] = eye
    c[:, C_CENT64:C_CENT64 + 128] = eye - bd
    c[:, C_MEAN64:C_MEAN64 + 128] = bd
    c[:, C_CENT128:C_CENT128 + 128] = eye - 1.0 / 128
    c[:, C_MEAN128:C_MEAN128 + 128] = 1.0 / 128
    c[np.arange(128), C_SWAP + (np.arange(128) ^ 1)] = 1.0
    c[:, C_STACK:C_STACK + 64] = np.vstack([np.eye(64), np.eye(64)])
    f = np.arange(128) % 64
    c[np.arange(128), C_MASK + f // HD] = 1.0
    half = HD // 2
    inv = (1.0 / np.float32(10000.0) ** (np.arange(0, half, 2, dtype=np.float32) / half)).astype(np.float32)
    pos = np.arange(NPOS)
    d = f % HD
    where = np.where((d // half)[:, None] == 0, (pos // WIN)[None, :], (pos % WIN)[None, :]).astype(np.float32)
    ang = where * inv[(d % half) // 2][:, None]
    cos, sin = np.cos(ang), np.sin(ang) * np.where(d % 2 == 0, -1.0, 1.0)[:, None]
    scale = HD ** -0.5
    c[:, C_COSQ:C_COSQ + 64] = cos * scale
    c[:, C_SINQ:C_SINQ + 64] = sin * scale
    c[:, C_COSK:C_COSK + 64] = cos
    c[:, C_SINK:C_SINK + 64] = sin
    return c


(W_Q, W_K, W_V, W_PROJ, W_FIN0, W_FIN1, W_OUT0, W_OUT1, W_FOUT, W_IN, W_A0, W_A1, W_B0, W_B1, W_C0, W_C1,
 W_D0, W_D1, W_QS, W_KS, W_S0, W_S1) = range(22)
NW = 24
(V_BQ, V_BK, V_BV, V_PROJ, V_IN, V_BB0, V_BB1, V_CB0, V_CB1, V_DB0, V_DB1, V_LW0, V_LW1, V_LB0, V_LB1,
 V_OUT, V_FI, V_BS0, V_BS1, V_BR) = range(20)
NV = V_BR + LAYERS * EXPERTS
(D_PROJ, D_C0, D_C1, D_B1, D_OUT, D_WC0, D_WC1, D_QS, D_KS) = range(9)


def at_least(eng, sem, count):
    if isinstance(count, int) and count <= 0:
        return
    eng.wait_ge(sem, count)


def stand_apart(eng, sem):
    eng.sem_inc(sem, 1)


def program(nc, a, out):
    F32, I32 = mybir.dt.float32, mybir.dt.int32
    ctx = ExitStack()
    with ctx:
        def sb(name, shape, dt=F32):
            return ctx.enter_context(nc.sbuf_tensor(name, shape, dt))

        def sem(name):
            return ctx.enter_context(nc.semaphore(name))

        m = Names()
        m.nc, m.a, m.out, m.sem, m.F32, m.I32 = nc, a, out, sem, F32, I32
        m.ALU, m.ACT, m.AX = mybir.AluOpType, mybir.ActivationFunctionType, mybir.AxisListType
        m.apart = sem("apart")
        m.const = sb("const", [128, C_END])
        m.wt = sb("wt", [128, NW, 128])
        m.experts = sb("experts", [128, LAYERS, EXPERTS + 1, HID + 1])
        m.route = sb("route", [1, SEGS], I32)
        m.entry = sb("entry", [128, BATCH, ROWS + 1])
        m.vec = sb("vec", [128, 64])
        m.dvec = sb("dvec", [128, 12])
        m.eps = sb("eps", [128, 1])
        m.bo = sb("bo", [128, FEAT])
        m.h = sb("h", [128, BROWS, COLS])
        m.big1 = sb("big1", [128, CHUNKS * COLS])
        m.big2 = sb("big2", [128, CHUNKS * COLS])
        m.bank = [ctx.enter_context(nc.psum_tensor(f"bank{n}", [128, NT], F32)) for n in range(8)]
        m.warm = sb("warm", [128, 2, CHUNKS])
        m.gap = sb("gap", [128, CHUNKS])
        m.agree = sb("agree", [128, 1])
        m.ones = sb("ones", [128, 1])
        m.flag = sb("flag", [1, 1], I32)
        m.ring = sb("ring", [128, 4, NT])
        prepare(m)
        transpose_input(m)
        window_attention(m)
        norm_and_project(m, "in")
        for layer in range(LAYERS):
            recurrence(m, layer)
            mix_and_norm(m, layer)
        add_recurrent_output(m)
        norm_and_project(m, "ffn")
        routed_ffn(m)


def prepare(m):
    nc, a, sem, ALU, ACT = m.nc, m.a, m.sem, m.ALU, m.ACT
    NRAW = 20 + LAYERS * EXPERTS
    raw = m.big2[:, 0:NRAW * 128].rearrange("p (n c) -> p n c", c=128)
    rows = m.big2[0:64, NRAW * 128:NRAW * 128 + 128]
    x_tok = m.big1[:, 0:HALF * COLS * FEAT].rearrange("p (c h f) -> p c h f", h=HALF, f=FEAT)
    R_S, R_R = 18, 20
    ident = m.const[:, C_IDENT:C_IDENT + 128]
    swap = m.const[:, C_SWAP:C_SWAP + 128]
    cent = m.const[:, C_CENT128:C_CENT128 + 128]
    cleared, const_in, raw_in, vec_in, x_in = (sem(n) for n in ("cleared", "const_in", "raw_in", "vec_in", "x_in"))
    turned, taken, small, small_out = (sem(n) for n in ("turned", "taken", "small", "small_out"))
    m.x_in = x_in
    N_RAW, N_VEC = [0], [0]
    off = (NRAW + 1) * 128
    route_raw = m.big2[0:1, off:off + SEGS].bitcast(m.I32)
    route_f = m.big2[0:1, off + SEGS:off + 2 * SEGS]
    valid = m.big2[0:1, off + 2 * SEGS:off + 3 * SEGS]
    valid2 = m.big2[0:1, off + 3 * SEGS:off + 4 * SEGS]
    routed = sem("routed")

    with nc.Block() as block:
        @block.sync
        def _(sp):
            sp.dma_start(m.const[:, :], a["consts"]).then_inc(const_in, 16)
            sp.wait_ge(cleared, 2)

            def load(slot, src, rows_at=0, cols_at=0):
                n, c = src.shape
                sp.dma_start(raw[rows_at:rows_at + n, slot, cols_at:cols_at + c], src).then_inc(raw_in, 16)
                N_RAW[0] += 16

            def vector(row, src, at=0):
                c = src.shape[1]
                sp.dma_start(rows[row:row + src.shape[0], at:at + c], src).then_inc(vec_in, 16)
                N_VEC[0] += 16

            for p in range(HALF):
                for n, slot in enumerate((W_Q, W_K, W_V)):
                    load(slot, a["L0_tok_qkv_w"][64 * n:64 * n + 64, :], 64 * p, 64 * p)
                load(W_PROJ, a["L0_tok_proj_w"], 64 * p, 64 * p)
                load(W_IN, a["L0_attn_in_W"], 0, 64 * p)
                load(W_FIN0 + p, a["L0_ffn_Wi"], 0, 64 * p)
                load(W_OUT0 + p, a["L0_attn_out_W"], 64 * p, 0)
            load(W_FOUT, a["L0_ffn_Wo"])
            for p in range(HALF):
                for n, row in enumerate((V_BQ, V_BK, V_BV)):
                    vector(row, a["L0_tok_qkv_b"][64 * n:64 * n + 64].rearrange("(a n) -> a n", a=1), 64 * p)
                vector(V_PROJ, a["L0_tok_proj_b"].rearrange("(a n) -> a n", a=1), 64 * p)
                vector(V_OUT, a["L0_attn_out_b"].rearrange("(a n) -> a n", a=1), 64 * p)
            for row, name in ((V_IN, "L0_attn_in_b"), (V_FI, "L0_ffn_bi")):
                vector(row, a[name].rearrange("(a n) -> a n", a=1))
            for row, name in ((V_BB0, "B_b"), (V_CB0, "C_b"), (V_DB0, "D_b"), (V_LW0, "ln_w"), (V_LB0, "ln_b")):
                vector(row, a["L0_attn_" + name])
            vector(V_BS0, a["L0_ffn_bs"].rearrange("l s h -> (l s) h"))
            vector(V_BR, a["L0_ffn_br"].rearrange("l e h -> (l e) h"))
            sp.dma_start(m.bo[:, :], a["L0_ffn_bo"].rearrange("(a n) -> a n", a=1).broadcast_to([128, FEAT]))\
                .then_inc(vec_in, 16)
            sp.dma_start(route_raw, a["L0_ffn_route_id"].rearrange("(a n) -> a n", a=1)).then_inc(vec_in, 16)
            N_VEC[0] += 32

        @block.scalar
        def _(act):
            act.wait_ge(cleared, 2)
            for l in range(LAYERS):
                for slot, name in ((W_A0, "A_W"), (W_B0, "B_W"), (W_C0, "C_W"), (W_D0, "D_W")):
                    act.dma_start(raw[:, slot + l, :], a["L0_attn_" + name][l]).then_inc(raw_in, 16)
            act.dma_start(raw[:, R_S:R_S + 2, :], a["L0_ffn_Ws"].rearrange("l s h d -> h (l s) d")).then_inc(raw_in, 16)
            act.dma_start(raw[:, R_R:R_R + 32, :], a["L0_ffn_Wr"].rearrange("l e h d -> h (l e) d")).then_inc(raw_in, 16)
            for p in range(HALF):
                act.dma_start(x_tok[:, :, p, :], a["x"][2 * p:2 * p + 2].rearrange("b r c f -> (b r) c f")).then_inc(x_in, 16)
            act.wait_ge(x_in, 16 * HALF)

        n_raw_act = (4 * LAYERS + 2) * 16

        @block.gpsimd
        def _(pool):
            pool.memset(m.big2[:, 0:W_IN * 128], 0.0).then_inc(cleared, 1)
            pool.memset(rows, 0.0).then_inc(cleared, 1)
            pool.memset(m.eps[:, :], EPS)
            pool.memset(m.ones[:, :], 1.0)

        I, S, M = ident, swap, cent
        def r(n):
            return raw[:, n, :]
        jobs = [[(r(n), I)] for n in range(W_C0)]
        jobs += [[(r(W_C0), M)], [(r(W_C1), M)], [(r(W_D0), M), (I, M)], [(r(W_D1), M), (I, M)],
                 [(r(W_Q), S)], [(r(W_K), S)], [(r(R_S), I), (I, I)], [(r(R_S + 1), I), (I, I)],
                 [(I, I)], [(I, I)]]
        jobs += [[(r(R_R + n), I)] for n in range(LAYERS * EXPERTS)]
        NG = len(jobs) // 4
        NGW = NW // 4

        @block.tensor
        def _(pe):
            pe.wait_ge(const_in, 16)
            pe.wait_ge(raw_in, N_RAW[0] + n_raw_act)
            for g in range(NG):
                if g >= 2:
                    pe.wait_ge(taken, g - 1)
                for n, job in enumerate(jobs[4 * g:4 * g + 4]):
                    for k, (w, mv) in enumerate(job):
                        last = pe.matmul(m.bank[g % 2][:, 128 * n:128 * n + 128], w, mv,
                                         start=(k == 0), stop=(k == len(job) - 1))
                last.then_inc(turned, 1)
            pe.wait_ge(vec_in, N_VEC[0])
            pe.matmul(m.bank[2][:, 0:64], rows, ident[0:64, 0:64], start=True, stop=True).then_inc(small, 1)
            pe.wait_ge(small_out, 1)
            pe.wait_ge(taken, NG)
            v = lambda n: m.vec[:, n:n + 1]
            w = lambda n: m.wt[:, n, :]
            sums = {D_PROJ: [(ident, v(V_PROJ)), (w(W_PROJ), v(V_BV))],
                    D_C0: [(cent, v(V_CB0)), (cent, v(V_DB0))],
                    D_C1: [(cent, v(V_CB1)), (cent, v(V_DB1)), (w(W_D1), v(V_LB0))],
                    D_B1: [(ident, v(V_BB1)), (w(W_B1), v(V_LB0))],
                    D_OUT: [(ident, v(V_OUT)), (w(W_OUT0), v(V_LB1)), (w(W_OUT1), v(V_LB1))],
                    D_QS: [(swap, v(V_BQ))], D_KS: [(swap, v(V_BK))]}
            for d, terms in sums.items():
                for k, (x, y) in enumerate(terms):
                    last = pe.matmul(m.bank[3][:, d:d + 1], x, y, start=(k == 0), stop=(k == len(terms) - 1))
            last.then_inc(small, 1)

        @block.vector
        def _(dve):
            for g in range(NG):
                dve.wait_ge(turned, g + 1)
                src = m.bank[g % 2][:, :].rearrange("p (n c) -> p n c", c=128)
                if g < NGW:
                    dve.tensor_copy(m.wt[:, 4 * g:4 * g + 4, :], src).then_inc(taken, 1)
                else:
                    if g == NGW:
                        dve.wait_ge(taken, g)
                    l, e = (4 * (g - NGW)) // EXPERTS, (4 * (g - NGW)) % EXPERTS
                    shared = m.wt[:, W_S0 + l, :].unsqueeze(1).broadcast_to([128, 4, 128])
                    dve.tensor_tensor(m.experts[:, l, e:e + 4, 0:HID], src, shared, ALU.add).then_inc(taken, 1)
            dve.wait_ge(small, 1)
            dve.tensor_copy(m.vec[:, :], m.bank[2][:, 0:64]).then_inc(small_out, 1)
            dve.wait_ge(small_out, 1)
            for l in range(LAYERS):
                dve.tensor_scalar(m.experts[:, l, 0:EXPERTS, HID:HID + 1],
                                  m.vec[:, V_BR + l * EXPERTS:V_BR + (l + 1) * EXPERTS].unsqueeze(2),
                                  m.vec[:, V_BS0 + l:V_BS0 + l + 1], None, ALU.add)
                dve.tensor_copy(m.experts[:, l, EXPERTS, HID:HID + 1], m.vec[:, V_BS0 + l:V_BS0 + l + 1])
                dve.tensor_copy(m.experts[:, l, EXPERTS, 0:HID], m.wt[:, W_S0 + l, :])
            dve.wait_ge(vec_in, N_VEC[0])
            dve.tensor_copy(route_f, route_raw).then_inc(routed, 1)
            dve.wait_ge(routed, 1)
            dve.tensor_scalar(valid, route_f, 0.0, None, ALU.is_ge).then_inc(routed, 1)
            dve.tensor_scalar(valid2, route_f, float(EXPERTS), None, ALU.is_lt).then_inc(routed, 1)
            dve.wait_ge(routed, 3)
            dve.tensor_tensor(valid, valid, valid2, ALU.mult).then_inc(routed, 1)
            dve.wait_ge(routed, 4)
            dve.scalar_tensor_tensor(route_f, route_f, -float(EXPERTS), valid, ALU.add, ALU.mult).then_inc(routed, 1)
            dve.wait_ge(routed, 5)
            dve.tensor_scalar(m.route[:, :], route_f, float(EXPERTS), None, ALU.add)
            dve.memset(m.entry[:, :, 0:1], 0.0)
            dve.wait_ge(small, 2)
            dve.tensor_copy(m.dvec[:, 0:5], m.bank[3][:, 0:5]).then_inc(small_out, 1)
            dve.tensor_copy(m.dvec[:, D_QS:D_QS + 2], m.bank[3][:, D_QS:D_QS + 2]).then_inc(small_out, 1)
            dve.wait_ge(small_out, 3)
            dve.tensor_tensor(m.dvec[:, D_WC0:D_WC0 + 2], m.dvec[:, D_C0:D_C0 + 2], m.vec[:, V_LW0:V_LW0 + 2], ALU.mult)


def transpose_input(m):
    nc, sem = m.nc, m.sem
    x_tok = m.big1[:, 0:HALF * COLS * FEAT].rearrange("p (c h f) -> p c h f", h=HALF, f=FEAT)
    m.x_t = m.big1[:, HALF * COLS * FEAT:2 * HALF * COLS * FEAT].rearrange("p (w n) -> p w n", n=NPOS)
    ident = m.const[:, C_IDENT:C_IDENT + 128]
    flipped, by_dve, by_act = sem("flipped"), sem("flip_dve"), sem("flip_act")
    NG = COLS // 4

    def dest(g):
        wc, j0 = (4 * g) // WIN, (4 * g) % WIN
        v = m.x_t.rearrange("p (t w) (i j) -> p w j t i", w=WIN, j=WIN)
        return v[:, wc, j0:j0 + 4, :, :]

    def src(g):
        return m.bank[g % 4][:, :].rearrange("p (j t i) -> p j t i", j=4, i=WIN)

    with nc.Block() as block:
        @block.tensor
        def _(pe):
            for g in range(NG):
                if g >= 4:
                    pe.wait_ge(by_dve if g % 2 == 0 else by_act, 4 * ((g - 4) // 2 + 1))
                for n in range(4):
                    last = pe.transpose(m.bank[g % 4][:, 128 * n:128 * n + 128], x_tok[:, 4 * g + n, :, :].rearrange("p h f -> p (h f)"), ident)
                last.then_inc(flipped, 1)

        @block.vector
        def _(dve):
            for g in range(0, NG, 2):
                dve.wait_ge(flipped, g + 1)
                for j in range(4):
                    dve.tensor_copy(dest(g)[:, j], src(g)[:, j]).then_inc(by_dve, 1)

        @block.scalar
        def _(act):
            for g in range(1, NG, 2):
                act.wait_ge(flipped, g + 1)
                for j in range(4):
                    act.activation(dest(g)[:, j], src(g)[:, j], m.ACT.Copy).then_inc(by_act, 1)


def window_attention(m):
    nc, sem, ALU, ACT, AX = m.nc, m.sem, m.ALU, m.ACT, m.AX
    cur = [0]

    def buf(*shape):
        n = int(np.prod(shape))
        v = m.big2[:, cur[0]:cur[0] + n]
        cur[0] += n
        assert cur[0] <= CHUNKS * COLS
        if len(shape) == 1:
            return v
        names = "abcde"[:len(shape)]
        return v.rearrange("p (" + " ".join(names) + ") -> p " + " ".join(names),
                           **{c: s for c, s in zip(names, shape)})

    x_now = buf(2, PPT, 2, NPOS)
    rot = buf(4, NT)
    q_bd = buf(2, PPT, 128)
    k_rot = buf(2, PPT, NPOS)
    k_mask = buf(4, HEADS, NPOS)
    shifted = buf(2, HEADS, NPOS)
    probs = buf(2, NT)
    probs_t = buf(2, 4, 128)
    v_aug = buf(2, PPT * HALF, HEADS, HD + 1)
    top = buf(2, HEADS)
    inv = buf(4, HEADS)
    o_bd = buf(PPT, 128)
    o_t = buf(NT)

    b_s, b_pt, b_o, b_x, b_h = m.bank[0:2], m.bank[2:4], m.bank[4:6], m.bank[6], m.bank[7]
    bo_psum = [b[:, :].rearrange("p (n s) -> p n s", s=256) for b in b_o]
    cst = lambda c, n: m.const[:, c:c + n]

    S = Names()
    S.zeroed, S.x_ready, S.x_mm, S.rope, S.v_copied = (sem("at_" + n) for n in ("zeroed", "x_ready", "x_mm", "rope", "v_copied"))
    S.q_ready, S.krot, S.kmask, S.scores, S.maxed = (sem("at_" + n) for n in ("q_ready", "krot", "kmask", "scores", "maxed"))
    S.shifted, S.probs, S.pt, S.pt_copied, S.av = (sem("at_" + n) for n in ("shifted", "probs", "pt", "pt_copied", "av"))
    S.inv, S.normed, S.ot, S.ot_copied, S.proj = (sem("at_" + n) for n in ("inv", "normed", "ot", "ot_copied", "proj"))
    S.h, = (sem("at_" + n) for n in ("h",))
    def over_tiles(eng, tile):
        tile(0, 0, "first")
        tile(1, 1, "mid")
        tile(2, 0, "mid")
        with eng.Fori(1, (TILES - 2) // 2) as u:
            tile(u * 2 + 1, 1, "mid")
            tile(u * 2 + 2, 0, "mid")
        tile(TILES - 1, (TILES - 1) % 2, "last")
        tile(TILES, TILES % 2, "drain")

    def flags(kind):
        return kind != "drain", kind in ("first", "mid"), kind != "first"

    with nc.Block() as block:
        @block.tensor
        def _(pe):
            def product(t, par, n):
                at_least(pe, S.x_ready, t * 2 + 2)
                if n < 4:
                    at_least(pe, S.rope, t * 4 + n)
                    if n == 0:
                        at_least(pe, S.v_copied, t * 4)
                    pe.matmul(b_x[:, :], m.wt[:, (W_Q, W_QS, W_K, W_KS)[n], :], x_now[:, par, :, 0, :],
                              start=True, stop=True).then_inc(S.x_mm, 1)
                else:
                    at_least(pe, S.rope, t * 4 + 4)
                    at_least(pe, S.v_copied, t * 4 + 2 * (n - 4))
                    for k in range(4):
                        pr = 4 * (n - 4) + k
                        tok = x_now[:, par, pr, :, :].rearrange("p a n -> p (a n)")
                        last = pe.matmul(b_x[:, 128 * k:128 * k + 128], tok, m.wt[:, W_V, :], start=True, stop=True)
                    last.then_inc(S.x_mm, 1)

            def scores(i, par, j):
                at_least(pe, S.kmask, i + 1)
                at_least(pe, S.shifted, i - 1)
                pe.matmul(b_s[j % 2][:, :], q_bd[:, par, j, :], k_mask[:, j % 4].rearrange("p h n -> p (h n)"),
                          start=True, stop=True).then_inc(S.scores, 1)

            def tile(t, par, kind):
                now, nxt, prev = flags(kind)
                for j in range(PPT):
                    i = t * PPT + j
                    if now and j < PPT - 1:
                        scores(i + 1, par, j + 1)
                    if nxt and j == PPT - 1:
                        at_least(pe, S.q_ready, t * 2 + 4)
                        scores(i + 1, 1 - par, 0)
                    if nxt and 1 <= j < 7:
                        product(t + 1, 1 - par, j - 1)
                    if prev and j == 4:
                        at_least(pe, S.normed, t * 4)
                        at_least(pe, S.h, t - 1)
                        for pr in range(PPT):
                            last = pe.matmul(b_h[:, NPOS * pr:NPOS * (pr + 1)], o_bd[:, pr, :], cst(C_STACK, NPOS),
                                             start=True, stop=True)
                        last.then_inc(S.ot, 1)
                    if prev and j == 6:
                        at_least(pe, S.ot_copied, t)
                        pe.matmul(b_h[:, :], m.wt[:, W_PROJ, :], o_t, start=True, stop=True).then_inc(S.proj, 1)
                    if (now and j >= 1) or (prev and j < 1):
                        at_least(pe, S.probs, i)
                        at_least(pe, S.pt_copied, i - 2)
                        for c in range(4):
                            last = pe.transpose(b_pt[(j + 1) % 2][:, 128 * c:128 * c + 128],
                                                probs[:, (j + 1) % 2, 128 * c:128 * c + 128], cst(C_IDENT, 128))
                        last.then_inc(S.pt, 1)
                    if (now and j >= 2) or (prev and j < 2):
                        jj = (j - 2) % PPT
                        vpar = par if j >= 2 else 1 - par
                        at_least(pe, S.pt_copied, i - 1)
                        if jj % 4 == 0:
                            at_least(pe, S.v_copied, (t * 4 if j >= 2 else t * 4 - 4) + 2 * (jj // 4 + 1))
                            at_least(pe, S.normed, (t * 4 if j >= 2 else t * 4 - 4) + 2 * (jj // 4))
                        dst = bo_psum[(jj % 4) // 2][:, jj % 2, 0:144].rearrange("p (h k d) -> p h k d", h=HALF, k=4)
                        for c in range(4):
                            last = pe.matmul(dst[:, :, c, :], probs_t[:, j % 2, c, :],
                                             v_aug[:, vpar, HALF * jj:HALF * jj + 2, 2 * c:2 * c + 2, :]
                                             .rearrange("p a h d -> p a (h d)"), start=True, stop=True)
                        last.then_inc(S.av, 1)

            for n in range(6):
                product(0, 0, n)
            at_least(pe, S.q_ready, 2)
            scores(0, 0, 0)
            over_tiles(pe, tile)

        @block.vector
        def _(dve):
            def rope(t, n):
                at_least(dve, S.x_mm, t * 6 + n + 1)
                if n < 2:
                    at_least(dve, S.q_ready, t * 2)
                else:
                    at_least(dve, S.krot, t)
                bias = (m.vec[:, V_BQ:V_BQ + 1], m.dvec[:, D_QS:D_QS + 1], m.vec[:, V_BK:V_BK + 1],
                        m.dvec[:, D_KS:D_KS + 1])[n]
                table = cst((C_COSQ, C_SINQ, C_COSK, C_SINK)[n], NPOS).unsqueeze(1).broadcast_to([128, PPT, NPOS])
                dve.scalar_tensor_tensor(rot[:, n, :].rearrange("p (w n) -> p w n", n=NPOS),
                                         b_x[:, :].rearrange("p (w n) -> p w n", n=NPOS), bias, table,
                                         ALU.add, ALU.mult).then_inc(S.rope, 1)

            def tile(t, par, kind):
                now, nxt, prev = flags(kind)
                for j in range(PPT):
                    i = t * PPT + j
                    if now:
                        at_least(dve, S.scores, i + 1)
                        at_least(dve, S.shifted, i - 1)
                        sc = b_s[j % 2][:, :].rearrange("p (h n) -> p h n", n=NPOS)
                        dve.tensor_reduce(top[:, j % 2, :], sc, AX.X, ALU.max).then_inc(S.maxed, 1)
                        dve.wait_ge(S.maxed, i + 1)
                        at_least(dve, S.probs, i - 1)
                        dve.tensor_tensor(shifted[:, j % 2], sc, top[:, j % 2, :].unsqueeze(2)
                                          .broadcast_to([128, HEADS, NPOS]), ALU.subtract).then_inc(S.shifted, 1)
                    if nxt and 1 <= j < 5:
                        rope(t + 1, j - 1)
                    for when, back, go in ((2, 4, prev), (6, 0, now)):
                        if j != when or not go:
                            continue
                        g4 = t * PPT - back
                        n0 = (t * 4 - 2) if back else t * 4
                        at_least(dve, S.av, g4 + 4)
                        if back == 0:
                            at_least(dve, S.ot, t)
                        for p in range(HALF):
                            s = slice(64 * p, 64 * p + 64)
                            for b in range(2):
                                o = bo_psum[b][s, :, 72 * p:72 * p + 72].rearrange("p n (h d) -> p n h d", d=HD + 1)
                                dve.reciprocal(inv[s, 2 * b:2 * b + 2, :], o[:, :, :, HD]).then_inc(S.inv, 1)
                        dve.wait_ge(S.inv, n0 * 2 + 4)
                        for p in range(HALF):
                            s = slice(64 * p, 64 * p + 64)
                            for b in range(2):
                                o = bo_psum[b][s, :, 72 * p:72 * p + 72].rearrange("p n (h d) -> p n h d", d=HD + 1)
                                at = (4 if back else 0) + 2 * b
                                last = dve.tensor_tensor(
                                    o_bd[s, at:at + 2, 64 * p:64 * p + 64].rearrange("p n (h d) -> p n h d", d=HD),
                                    o[:, :, :, 0:HD],
                                    inv[s, 2 * b:2 * b + 2, :].unsqueeze(3).broadcast_to([64, 2, HEADS, HD]),
                                    ALU.mult)
                            last.then_inc(S.normed, 1)

            dve.memset(q_bd[:, :, :, :], 0.0).then_inc(S.zeroed, 1)
            dve.memset(o_bd[:, :, :], 0.0).then_inc(S.zeroed, 1)
            dve.memset(v_aug[:, :, :, :, :], 0.0).then_inc(S.zeroed, 1)
            dve.wait_ge(S.zeroed, 3)
            va = v_aug.rearrange("p a b (c k) d -> p (a b) c k d", k=2)
            for k in range(2):
                dve.memset(va[64 * k:64 * k + 64, :, :, k, HD], 1.0).then_inc(S.zeroed, 1)
            dve.wait_ge(S.zeroed, 5)
            for n in range(4):
                rope(0, n)
            over_tiles(dve, tile)

        @block.scalar
        def _(act):
            def v_copy(t, par, n):
                at_least(act, S.x_mm, t * 6 + 5 + n)
                at_least(act, S.av, t * PPT - PPT)
                src = b_x[:, :].rearrange("p (a c k d) -> p a c k d", a=8, c=4, k=2)
                dst = v_aug[:, par, 8 * n:8 * n + 8, :, :].rearrange("p a (c k) d -> p a c k d", k=2)
                for k in range(2):
                    s = slice(64 * k, 64 * k + 64)
                    act.activation(dst[s, :, :, k, 0:HD], src[s, :, :, k, :], ACT.Copy).then_inc(S.v_copied, 1)

            def tile(t, par, kind):
                now, nxt, prev = flags(kind)
                for j in range(PPT):
                    i = t * PPT + j
                    if now:
                        at_least(act, S.shifted, i + 1)
                        at_least(act, S.pt, i - 1)
                        act.activation(probs[:, j % 2, :], shifted[:, j % 2].rearrange("p h n -> p (h n)"),
                                       ACT.Exp).then_inc(S.probs, 1)
                    if (now and j >= 1) or (prev and j < 1):
                        at_least(act, S.pt, i)
                        at_least(act, S.av, i - 2)
                        act.activation(probs_t[:, (j + 1) % 2].rearrange("p c n -> p (c n)"),
                                       b_pt[(j + 1) % 2][:, :], ACT.Copy).then_inc(S.pt_copied, 1)
                    if nxt and j in (5, 6):
                        v_copy(t + 1, 1 - par, j - 5)
                    if prev and j == 5:
                        at_least(act, S.ot, t)
                        at_least(act, S.proj, t - 1)
                        act.activation(o_t, b_h[:, :], ACT.Copy).then_inc(S.ot_copied, 1)
                    if prev and j == 7:
                        at_least(act, S.proj, t)
                        act.activation(m.h[:, bass.ds(t * WIN - WIN, WIN), :].rearrange("p i (w j) -> p w i j", j=WIN),
                                       b_h[:, :].rearrange("p (w i j) -> p w i j", w=WIN, j=WIN),
                                       ACT.Identity, bias=m.dvec[:, D_PROJ:D_PROJ + 1]).then_inc(S.h, 1)

            act.wait_ge(S.zeroed, 5)
            for n in range(2):
                v_copy(0, 0, n)
            over_tiles(act, tile)

        @block.gpsimd
        def _(pool):
            def mask(i, par, jj):
                at_least(pool, S.scores, i - 3)
                pool.tensor_tensor(k_mask[:, jj % 4], k_rot[:, par, jj, :].unsqueeze(1).broadcast_to([128, HEADS, NPOS]),
                                   cst(C_MASK, HEADS).unsqueeze(2).broadcast_to([128, HEADS, NPOS]),
                                   ALU.mult).then_inc(S.kmask, 1)

            def load_x(t, par):
                at_least(pool, S.x_mm, t * 6 - 6)
                stand_apart(pool, m.apart)
                for k in range(2):
                    pool.tensor_copy(x_now[:, par, :, k, :], m.x_t[:, bass.ds(t * PPT, PPT), :]).then_inc(S.x_ready, 1)

            def add_q(t, par):
                at_least(pool, S.rope, t * 4 + 2)
                at_least(pool, S.scores, t * PPT - PPT)
                at_least(pool, S.kmask, t * PPT - 2)
                at_least(pool, S.x_ready, t * 2 + 2)
                for p in range(HALF):
                    s = slice(64 * p, 64 * p + 64)
                    at_least(pool, S.q_ready, t * 2 + p)
                    pool.tensor_tensor(q_bd[s, par, :, 64 * p:64 * p + 64],
                                       rot[s, 0, :].rearrange("p (w n) -> p w n", n=NPOS),
                                       rot[s, 1, :].rearrange("p (w n) -> p w n", n=NPOS), ALU.add).then_inc(S.q_ready, 1)
                at_least(pool, S.q_ready, t * 2 + 2)

            def add_k(t, par):
                at_least(pool, S.rope, t * 4 + 4)
                at_least(pool, S.kmask, t * PPT - PPT)
                pool.tensor_tensor(k_rot[:, par].rearrange("p w n -> p (w n)"), rot[:, 2, :], rot[:, 3, :],
                                   ALU.add).then_inc(S.krot, 1)
                pool.wait_ge(S.krot, t + 1)

            def tile(t, par, kind):
                now, nxt, prev = flags(kind)
                for j in range(PPT):
                    i = t * PPT + j
                    if nxt and j == 0:
                        load_x(t + 1, 1 - par)
                    if nxt and j == 3:
                        add_q(t + 1, 1 - par)
                    if nxt and j == PPT - 3:
                        add_k(t + 1, 1 - par)
                    if now and j < PPT - 3:
                        mask(i + 3, par, j + 3)
                    elif nxt:
                        mask(i + 3, 1 - par, j + 3 - PPT)

            pool.wait_ge(S.zeroed, 5)
            load_x(0, 0)
            add_q(0, 0)
            add_k(0, 0)
            for jj in range(3):
                mask(jj, 0, jj)
            over_tiles(pool, tile)


def norm_and_project(m, kind):
    sem, ALU, ACT = m.sem, m.ALU, m.ACT
    m.x1 = m.big1[:, :].rearrange("p (c n) -> p c n", n=CHUNKS)
    m.y = m.big1[:, 0:BROWS * COLS]
    h = m.h[:, :, :].rearrange("p r c -> p (r c)")
    buf = m.big2[:, 0:8 * NT].rearrange("p (n c) -> p n c", c=NT)
    square, dev, rstd, u = buf[:, 0:2], buf[:, 2:4], buf[:, 4:6], buf[:, 6:8]
    N = Names()
    N.centred, N.squared, N.variance, N.deviation, N.rstd = (sem(f"{kind}_" + n) for n in ("centred", "squared", "variance", "deviation", "rstd"))
    N.scaled, N.product, N.copied0, N.copied1 = (sem(f"{kind}_" + n) for n in ("scaled", "product", "copied0", "copied1"))
    b_c, b_v, b_p = m.bank[0:2], m.bank[2:4], m.bank[4:8]
    w = lambda c: m.const[:, c:c + 128]
    project = kind == "in"

    with m.nc.Block() as block:
        @block.tensor
        def _(pe):
            def centre(t, par):
                at_least(pe, N.scaled, t - 1)
                pe.matmul(b_c[par][:, :], w(C_CENT64), h[:, bass.ds(t * NT, NT)], start=True, stop=True)\
                    .then_inc(N.centred, 1)

            def tile(t, par, first=False, last=False):
                if not last:
                    centre(t + 1, 1 - par)
                at_least(pe, N.squared, t + 1)
                at_least(pe, N.deviation, t - 1)
                pe.matmul(b_v[par][:, :], w(C_MEAN64), square[:, par, :], start=True, stop=True)\
                    .then_inc(N.variance, 1)
                if project and not first:
                    in_product(t - 1, 1 - par)

            def in_product(t, par):
                at_least(pe, N.scaled, t + 1)
                at_least(pe, N.copied0, t - 1)
                at_least(pe, N.copied1, t - 1)
                for p in range(HALF):
                    s = slice(64 * p, 64 * p + 64)
                    pe.matmul(b_p[2 * par + p][:, :], m.wt[s, W_IN, :], u[s, par, :], start=True, stop=True)\
                        .then_inc(N.product, 1)

            centre(0, 0)
            tile(0, 0, first=True)
            tile(1, 1)
            tile(2, 0)
            with pe.Fori(1, (TILES - 2) // 2) as k:
                tile(k * 2 + 1, 1)
                tile(k * 2 + 2, 0)
            tile(TILES - 1, 1, last=True)
            if project:
                in_product(TILES - 1, 1)

        def copy_in(t, p):
            return (m.x1[:, :, bass.ds(t * WIN + p * BROWS, WIN)].rearrange("p c i -> p i c"),
                    lambda par: b_p[2 * par + p][:, :].rearrange("p (i c) -> p i c", c=COLS))

        @block.scalar
        def _(act):
            def tile(t, par, first=False):
                at_least(act, N.centred, t + 1)
                at_least(act, N.variance, t - 1)
                act.activation(square[:, par, :], b_c[par][:, :], ACT.Square).then_inc(N.squared, 1)
                at_least(act, N.variance, t + 1)
                at_least(act, N.rstd, t - 1)
                act.activation(dev[:, par, :], b_v[par][:, :], ACT.Sqrt, bias=m.eps[:, :]).then_inc(N.deviation, 1)
                if project and not first:
                    copied(t - 1, 1 - par)

            def copied(t, par):
                at_least(act, N.product, t * 2 + 1)
                dst, src = copy_in(t, 0)
                act.activation(dst, src(par), ACT.Identity, bias=m.vec[:, V_IN:V_IN + 1]).then_inc(N.copied0, 1)

            tile(0, 0, first=True)
            tile(1, 1)
            tile(2, 0)
            with act.Fori(1, (TILES - 2) // 2) as k:
                tile(k * 2 + 1, 1)
                tile(k * 2 + 2, 0)
            tile(TILES - 1, 1)
            if project:
                copied(TILES - 1, 1)

        @block.vector
        def _(dve):
            def tile(t, par, first=False):
                at_least(dve, N.deviation, t + 1)
                dve.reciprocal(rstd[:, par, :], dev[:, par, :]).then_inc(N.rstd, 1)
                dve.wait_ge(N.rstd, t + 1)
                if project:
                    at_least(dve, N.product, t * 2 - 2)
                dst = u[:, par, :] if project else m.y[:, bass.ds(t * NT, NT)]
                dve.tensor_tensor(dst, b_c[par][:, :], rstd[:, par, :], ALU.mult).then_inc(N.scaled, 1)
                if project and not first:
                    copied(t - 1, 1 - par)

            def copied(t, par):
                at_least(dve, N.product, t * 2 + 2)
                dst, src = copy_in(t, 1)
                dve.tensor_scalar(dst, src(par), m.vec[:, V_IN:V_IN + 1], None, ALU.add).then_inc(N.copied1, 1)

            tile(0, 0, first=True)
            tile(1, 1)
            tile(2, 0)
            with dve.Fori(1, (TILES - 2) // 2) as k:
                tile(k * 2 + 1, 1)
                tile(k * 2 + 2, 0)
            tile(TILES - 1, 1)
            if project:
                copied(TILES - 1, 1)


def recurrence(m, layer):
    sem, ALU, ACT = m.sem, m.ALU, m.ACT
    x1 = m.x1
    hs = m.hs = m.big2[:, :].rearrange("p (c n) -> p c n", n=CHUNKS)
    GROUPS, GB = 2, BATCH // 2
    GC = CHUNKS // GROUPS
    w_a, w_b = m.wt[:, W_A0 + layer, :], m.wt[:, W_B0 + layer, :]
    bias = m.vec[:, V_BB0:V_BB0 + 1] if layer == 0 else m.dvec[:, D_B1:D_B1 + 1]
    cols = [slice(GC * g, GC * g + GC) for g in range(GROUPS)]
    bank = [[m.bank[2 * g + k][:, 0:GC] for k in range(2)] for g in range(GROUPS)]
    T = f"l{layer}_"
    summed = [sem(T + f"summed{g}") for g in range(GROUPS)]
    stepped = [sem(T + f"stepped{g}") for g in range(GROUPS)]
    again_summed = [sem(T + f"again_summed{g}") for g in range(GROUPS)]
    again_stepped = [sem(T + f"again_stepped{g}") for g in range(GROUPS)]
    again_first, cleared, compared, counted = (sem(T + n) for n in ("again_first", "cleared", "compared", "counted"))
    warm = [m.warm[:, k, :] for k in range(2)]
    entry = [m.entry[:, GB * g:GB * g + GB, 0:ROWS] for g in range(GROUPS)]
    ending = [m.entry[:, GB * g:GB * g + GB, 1:ROWS + 1] for g in range(GROUPS)]
    by_row = lambda v: v.rearrange("p (b r) -> p b r", r=ROWS)
    MAIN = COLS + 1

    with m.nc.Block() as block:
        @block.vector
        def _(dve):
            dve.memset(warm[1], 0.0).then_inc(cleared, 1)
            for g in range(GROUPS):
                dve.wait_ge(stepped[g], WARM + MAIN)
                dve.tensor_tensor(by_row(m.gap[:, cols[g]]), by_row(hs[:, COLS - 1, cols[g]]), ending[g],
                                  ALU.subtract).then_inc(compared, 1)
            dve.wait_ge(compared, GROUPS)
            dve.tensor_tensor(m.gap[:, :], m.gap[:, :], m.gap[:, :], ALU.mult).then_inc(compared, 1)
            dve.wait_ge(compared, GROUPS + 1)
            dve.tensor_scalar(m.gap[:, :], m.gap[:, :], TOL * TOL, None, ALU.is_le).then_inc(compared, 1)
            dve.wait_ge(compared, GROUPS + 2)
            dve.tensor_reduce(m.agree[:, :], m.gap[:, :].rearrange("p (b r) -> p b r", r=ROWS)[:, :, 0:ROWS - 1],
                              m.AX.XY, ALU.min).then_inc(compared, 1)
            dve.wait_ge(counted, 1)
            dve.tensor_copy(m.flag[:, :], m.bank[7][0:1, 0:1])

        def step_a(pe, g, k, state, done, ready, count):
            pe.wait_ge(ready[g], count)
            pe.matmul(bank[g][k % 2], w_a, state, start=False, stop=True).then_inc(done[g], 1)

        def step_b(pe, g, par, c):
            x = x1[:, c, cols[g]] if isinstance(c, int) else \
                x1[:, bass.ds(c, 1), cols[g]].rearrange("p a n -> p (a n)")
            pe.matmul(bank[g][par], w_b, x, start=True, stop=False)

        def state_at(c, g):
            return hs[:, c, cols[g]] if isinstance(c, int) else \
                hs[:, bass.ds(c, 1), cols[g]].rearrange("p a n -> p (a n)")

        def main_pass(pe, done, ready, base, last_b=True):
            for g in range(GROUPS):
                step_a(pe, g, 0, entry[g], done, ready, base + 1)
                step_b(pe, g, 1, 1)
            with pe.Fori(0, (COLS - 2) // 2) as u:
                for k in (1, 2):
                    for g in range(GROUPS):
                        step_a(pe, g, k, state_at(u * 2 + (k - 1), g), done, ready, u * 2 + (base + 1 + k))
                        step_b(pe, g, (k + 1) % 2, u * 2 + (k + 1))
            for g in range(GROUPS):
                step_a(pe, g, COLS - 1, state_at(COLS - 2, g), done, ready, base + COLS)

        def main_states(act, done, ready, base):
            def step(k, par):
                for g in range(GROUPS):
                    act.wait_ge(done[g], base + 1 + k if isinstance(k, int) else k + (base + 1))
                    act.activation(state_at(k, g), bank[g][par], ACT.Tanh, bias=bias).then_inc(ready[g], 1)
            with act.Fori(0, COLS // 2) as u:
                step(u * 2, 0)
                step(u * 2 + 1, 1)

        @block.tensor
        def _(pe):
            C0 = COLS - WARM
            pe.wait_ge(cleared, 1)
            for g in range(GROUPS):
                step_b(pe, g, 0, C0)
            for g in range(GROUPS):
                pe.matmul(bank[g][0], w_a, warm[1][:, cols[g]], start=False, stop=True).then_inc(summed[g], 1)
                step_b(pe, g, 1, C0 + 1)
            with pe.Fori(0, (WARM - 2) // 2) as u:
                for k in (1, 2):
                    for g in range(GROUPS):
                        step_a(pe, g, k, warm[(k + 1) % 2][:, cols[g]], summed, stepped, u * 2 + k)
                        step_b(pe, g, (k + 1) % 2, u * 2 + (C0 + k + 1))
            for g in range(GROUPS):
                step_a(pe, g, WARM - 1, warm[0][:, cols[g]], summed, stepped, WARM - 1)
                step_b(pe, g, 0, 0)
            main_pass(pe, summed, stepped, WARM)
            pe.wait_ge(compared, GROUPS + 3)
            pe.matmul(m.bank[7][0:1, 0:1], m.agree[:, :], m.ones[:, :], start=True, stop=True).then_inc(counted, 1)

        @block.scalar
        def _(act):
            with act.Fori(0, WARM // 2) as u:
                for k in range(2):
                    for g in range(GROUPS):
                        act.wait_ge(summed[g], u * 2 + (k + 1))
                        act.activation(warm[k][:, cols[g]], bank[g][k], ACT.Tanh, bias=bias).then_inc(stepped[g], 1)
            for g in range(GROUPS):
                act.wait_ge(stepped[g], WARM)
                act.activation(ending[g], by_row(warm[1][:, cols[g]]), ACT.Copy).then_inc(stepped[g], 1)
            main_states(act, summed, stepped, WARM)

    with m.nc.Block() as block:
        @block.tensor
        def _(pe):
            agreeing = pe.value_load(m.flag[0:1, 0:1], min_val=0, max_val=128)
            with pe.If(agreeing < 128):
                with pe.Fori(0, ROWS - 1) as rep:
                    for g in range(GROUPS):
                        at = rep * MAIN + 1
                        pe.wait_ge(again_stepped[g], at)
                        step_b(pe, g, 0, 0)
                    main_pass(pe, again_summed, again_stepped, rep * MAIN)

        @block.scalar
        def _(act):
            agreeing = act.value_load(m.flag[0:1, 0:1], min_val=0, max_val=128)
            with act.If(agreeing < 128):
                with act.Fori(0, ROWS - 1) as rep:
                    for g in range(GROUPS):
                        act.activation(ending[g], by_row(hs[:, COLS - 1, cols[g]]), ACT.Copy)\
                            .then_inc(again_stepped[g], 1)
                    main_states(act, again_summed, again_stepped, rep * COLS)
                    for g in range(GROUPS):
                        act.wait_ge(again_stepped[g], rep * MAIN + MAIN)


def mix_and_norm(m, layer):
    sem, ALU, ACT = m.sem, m.ALU, m.ACT
    STEPS = CHUNKS * COLS // NT
    hs, x = m.big2, m.big1
    b_y, b_v = m.bank[0:2], m.bank[2:4]
    w_c, w_d = m.wt[:, W_C0 + layer, :], m.wt[:, W_D0 + layer, :]
    scale = m.vec[:, V_LW0 + layer:V_LW0 + layer + 1]
    b_scaled = m.dvec[:, D_WC0 + layer:D_WC0 + layer + 1]
    b_plain = m.dvec[:, D_C0 + layer:D_C0 + layer + 1]
    M = Names()
    M.mixed, M.squared, M.weighted, M.variance, M.deviation = (sem(f"mix{layer}_" + n) for n in ("mixed", "squared", "weighted", "variance", "deviation"))
    M.rstd, M.written = (sem(f"mix{layer}_" + n) for n in ("rstd", "written"))
    square = dev = rstd = m.ring[:, 0:2, :]
    weighted = m.ring[:, 2:4, :]

    def over_tiles(eng, tile, tail=None):
        for t in range(3):
            tile(t, t % 2)
        with eng.Fori(1, (STEPS - 2) // 2) as k:
            tile(k * 2 + 1, 1)
            tile(k * 2 + 2, 0)
        tile(STEPS - 1, 1, last=True)

    with m.nc.Block() as block:
        @block.tensor
        def _(pe):
            def mix(t, par):
                at_least(pe, M.squared, t - 1)
                at_least(pe, M.weighted, t - 1)
                pe.matmul(b_y[par][:, :], w_c, hs[:, bass.ds(t * NT, NT)], start=True, stop=False)
                pe.matmul(b_y[par][:, :], w_d, x[:, bass.ds(t * NT, NT)], start=False, stop=True).then_inc(M.mixed, 1)

            def tile(t, par, last=False):
                if not last:
                    mix(t + 1, 1 - par)
                at_least(pe, M.squared, t + 1)
                at_least(pe, M.deviation, t - 1)
                pe.matmul(b_v[par][:, :], m.const[:, C_MEAN128:C_MEAN128 + 128], square[:, par, :],
                          start=True, stop=True).then_inc(M.variance, 1)
            mix(0, 0)
            over_tiles(pe, tile)

        @block.scalar
        def _(act):
            def tile(t, par, last=False):
                at_least(act, M.mixed, t + 1)
                at_least(act, M.written, t - 1)
                act.activation(square[:, par, :], b_y[par][:, :], ACT.Square, bias=b_plain).then_inc(M.squared, 1)
                at_least(act, M.variance, t + 1)
                act.activation(dev[:, par, :], b_v[par][:, :], ACT.Sqrt, bias=m.eps[:, :]).then_inc(M.deviation, 1)
            over_tiles(act, tile)

        @block.vector
        def _(dve):
            def tile(t, par, last=False):
                at_least(dve, M.mixed, t + 1)
                at_least(dve, M.squared, t + 1)
                at_least(dve, M.written, t - 1)
                dve.tensor_scalar(weighted[:, par, :], b_y[par][:, :], scale, b_scaled, ALU.mult, ALU.add)\
                    .then_inc(M.weighted, 1)
                at_least(dve, M.deviation, t + 1)
                dve.reciprocal(rstd[:, par, :], dev[:, par, :]).then_inc(M.rstd, 1)
            over_tiles(dve, tile)

        @block.gpsimd
        def _(pool):
            def tile(t, par, last=False):
                at_least(pool, M.weighted, t + 1)
                at_least(pool, M.rstd, t + 1)
                stand_apart(pool, m.apart)
                pool.tensor_tensor(x[:, bass.ds(t * NT, NT)], weighted[:, par, :], rstd[:, par, :], ALU.mult)\
                    .then_inc(M.written, 1)
            over_tiles(pool, tile)


def add_recurrent_output(m):
    summed, added = m.sem("out_summed"), m.sem("out_added")

    with m.nc.Block() as block:
        @block.tensor
        def _(pe):
            def tile(t, par):
                at_least(pe, added, t - 1)
                for p in range(HALF):
                    last = pe.matmul(m.bank[par][:, :], m.wt[:, W_OUT0 + p, :],
                                     m.x1[:, :, bass.ds(t * WIN + p * BROWS, WIN)],
                                     start=(p == 0), stop=(p == HALF - 1))
                last.then_inc(summed, 1)
            tile(0, 0)
            tile(1, 1)
            with pe.Fori(1, TILES // 2) as k:
                tile(k * 2, 0)
                tile(k * 2 + 1, 1)

        @block.vector
        def _(dve):
            with dve.Fori(0, TILES // 2) as k:
                for par in range(2):
                    t = k * 2 + par
                    dve.wait_ge(summed, t + 1)
                    h = m.h[:, bass.ds(t * WIN, WIN), :].rearrange("p i c -> p c i")
                    dve.scalar_tensor_tensor(h, m.bank[par][:, :].rearrange("p (c i) -> p c i", i=WIN),
                                             m.dvec[:, D_OUT:D_OUT + 1], h, m.ALU.add, m.ALU.add).then_inc(added, 1)


def routed_ffn(m):
    sem, ALU, ACT = m.sem, m.ALU, m.ACT
    cur = [0]

    def buf(*shape):
        n = int(np.prod(shape))
        v = m.big2[:, cur[0]:cur[0] + n]
        cur[0] += n
        names = "abcde"[:len(shape)]
        return v if len(shape) == 1 else v.rearrange(
            "p (" + " ".join(names) + ") -> p " + " ".join(names), **{c: s for c, s in zip(names, shape)})

    act1, act2, act3, held, result = (buf(2, NT) for _ in range(5))
    result = result[:, :, 0:4 * FEAT]
    expert = buf(LAYERS, 2, 2, HID + 1)
    h = m.h[:, :, :].rearrange("p r c -> p (r c)")
    out = m.out.rearrange("b s f -> (b s) f")
    R = Names()
    R.expert0, R.expert1, R.mm1, R.relu1, R.mm2 = (sem("ffn_" + n) for n in ("expert0", "expert1", "mm1", "relu1", "mm2"))
    R.relu2, R.mm3, R.relu3, R.held, R.mm4 = (sem("ffn_" + n) for n in ("relu2", "mm3", "relu3", "held", "mm4"))
    R.result, R.stored = (sem("ffn_" + n) for n in ("result", "stored"))
    b1, b2, b3, b4 = (m.bank[2 * n:2 * n + 2] for n in range(4))

    def over_units(eng, unit):
        for u in range(4):
            unit(u // 2, u % 2, range(u + 1))
        with eng.Fori(2, TILES) as t:
            unit(t, 0, range(4))
            unit(t, 1, range(4))
        for u in range(2 * TILES, 2 * TILES + 3):
            unit(u // 2, u % 2, range(u - 2 * TILES + 1, 4))


    with m.nc.Block() as block:
        @block.tensor
        def _(pe):
            def unit(t, par, stages):
                u = t * 2 + par
                if 0 in stages:
                    at_least(pe, R.relu1, u - 1)
                    pe.matmul(b1[par][:, :], m.wt[:, W_FIN0 + par, :], m.y[:, bass.ds(t * NT, NT)],
                              start=True, stop=True).then_inc(R.mm1, 1)
                for st, src, dst, ready, free, done, have in (
                        (1, act1, b2, R.relu1, R.relu2, R.mm2, R.expert0), (2, act2, b3, R.relu2, R.relu3, R.mm3, R.expert1)):
                    if st in stages:
                        k, kp = u - st, (par + st) % 2
                        at_least(pe, ready, k + 1)
                        at_least(pe, free, k - 1)
                        at_least(pe, have, k * 2 + 2)
                        for s in range(2):
                            last = pe.matmul(dst[kp][:, SEG * s:SEG * s + SEG], expert[:, st - 1, kp, s, 0:HID],
                                             src[:, kp, SEG * s:SEG * s + SEG], start=True, stop=True)
                        last.then_inc(done, 1)
                if 3 in stages:
                    k, kp = u - 3, (par + 3) % 2
                    at_least(pe, R.relu3, k + 1)
                    at_least(pe, R.held, k + 1)
                    at_least(pe, R.result, k - 1)
                    for s in range(4):
                        o = b4[kp][:, FEAT * s:FEAT * s + FEAT]
                        pe.matmul(o, act3[:, kp, s:NT:4], m.wt[:, W_FOUT, 0:FEAT], start=True, stop=False)
                        last = pe.matmul(o, held[:, kp, s:NT:4], m.const[:, C_IDENT + 64 * kp:C_IDENT + 64 * kp + 64],
                                         start=False, stop=True)
                    last.then_inc(R.mm4, 1)
            over_units(pe, unit)

        @block.scalar
        def _(act):
            def unit(t, par, stages):
                u = t * 2 + par
                if 0 in stages:
                    at_least(act, R.mm1, u + 1)
                    at_least(act, R.mm2, u - 1)
                    act.activation(act1[:, par, :], b1[par][:, :], ACT.Relu, bias=m.vec[:, V_FI:V_FI + 1]).then_inc(R.relu1, 1)
                if 1 in stages:
                    k, kp = u - 1, 1 - par
                    at_least(act, R.mm2, k + 1)
                    at_least(act, R.mm3, k - 1)
                    for s in range(2):
                        c = slice(SEG * s, SEG * s + SEG)
                        last = act.activation(act2[:, kp, c], b2[kp][:, c], ACT.Relu, bias=expert[:, 0, kp, s, HID:HID + 1])
                    last.then_inc(R.relu2, 1)
            over_units(act, unit)

        @block.vector
        def _(dve):
            def unit(t, par, stages):
                u = t * 2 + par
                if 2 in stages:
                    k, kp = u - 2, par
                    at_least(dve, R.mm3, k + 1)
                    at_least(dve, R.mm4, k - 1)
                    for s in range(2):
                        c = slice(SEG * s, SEG * s + SEG)
                        last = dve.tensor_scalar(act3[:, kp, c], b3[kp][:, c], expert[:, 1, kp, s, HID:HID + 1], 0.0,
                                                 ALU.add, ALU.max)
                    last.then_inc(R.relu3, 1)
                if 3 in stages:
                    k, kp = u - 3, 1 - par
                    at_least(dve, R.mm4, k + 1)
                    at_least(dve, R.stored, k * 16 - 16)
                    dve.tensor_tensor(result[:, kp, :].rearrange("p (s f) -> p s f", f=FEAT),
                                      b4[kp][:, 0:4 * FEAT].rearrange("p (s f) -> p s f", f=FEAT),
                                      m.bo[:, :].unsqueeze(1).broadcast_to([128, 4, FEAT]), ALU.add).then_inc(R.result, 1)
            over_units(dve, unit)

        @block.gpsimd
        def _(pool):
            def unit(t, par, stages):
                u = t * 2 + par
                if 0 in stages:
                    for l, have, used in ((0, R.expert0, R.relu2), (1, R.expert1, R.relu3)):
                        at_least(pool, used, u - 1)
                        if not isinstance(u, int):
                            stand_apart(pool, m.apart)
                        for s in range(2):
                            e = pool.value_load(m.route[0:1, bass.ds(t * 2 + (par * SEGS // 2 + s), 1)],
                                                min_val=0, max_val=EXPERTS)
                            pool.tensor_copy(expert[:, l, par, s, :],
                                             m.experts[:, l, bass.ds(e, 1), :].rearrange("p a c -> p (a c)"))\
                                .then_inc(have, 1)
                    at_least(pool, R.mm4, u - 1)
                    if not isinstance(u, int):
                        stand_apart(pool, m.apart)
                    pool.tensor_copy(held[:, par, :], h[:, bass.ds(t * NT, NT)]).then_inc(R.held, 1)
            over_units(pool, unit)

        @block.sync
        def _(sp):
            def unit(t, par, stages):
                u = t * 2 + par
                if 3 in stages:
                    k, kp = u - 3, 1 - par
                    tk = t - 2 + par
                    at_least(sp, R.result, k + 1)
                    stand_apart(sp, m.apart)
                    at_least(sp, R.stored, k * 16)
                    stand_apart(sp, m.apart)
                    sp.dma_start(out[bass.ds(tk * NT + kp * (BATCH // HALF) * ROWS * COLS, NT), :]
                                 .rearrange("(i s) f -> i (s f)", s=4), result[:, kp, :]).then_inc(R.stored, 16)
            over_units(sp, unit)
            sp.wait_ge(R.stored, 2 * TILES * 16)


_INS = ["x", "L0_tok_qkv_w", "L0_tok_qkv_b", "L0_tok_proj_w", "L0_tok_proj_b", "L0_attn_in_W", "L0_attn_in_b",
        "L0_attn_A_W", "L0_attn_B_W", "L0_attn_B_b", "L0_attn_C_W", "L0_attn_C_b", "L0_attn_D_W", "L0_attn_D_b",
        "L0_attn_ln_w", "L0_attn_ln_b", "L0_attn_out_W", "L0_attn_out_b", "L0_ffn_route_id", "L0_ffn_Wi",
        "L0_ffn_bi", "L0_ffn_Wr", "L0_ffn_br", "L0_ffn_Ws", "L0_ffn_bs", "L0_ffn_Wo", "L0_ffn_bo"]


def kernel(**inputs):
    import concourse.bacc as _bacc
    from concourse.bass_utils import run_bass_kernel_spmd as _run

    nc = _bacc.Bacc("TRN2", target_bir_lowering=False, num_devices=1)
    arrays, a = {}, {}
    for name in _INS:
        v = np.ascontiguousarray(inputs[name])
        arrays["in_" + name] = v
        a[name] = nc.dram_tensor("in_" + name, v.shape, mybir.dt.from_np(v.dtype), kind="ExternalInput").ap()
    c = shape_constants()
    arrays["in_consts"] = c
    a["consts"] = nc.dram_tensor("in_consts", c.shape, mybir.dt.float32, kind="ExternalInput").ap()
    out = nc.dram_tensor("out", (BATCH, ROWS * COLS, FEAT), mybir.dt.float32, kind="ExternalOutput").ap()
    program(nc, a, out)
    r = _run(nc, [arrays], core_ids=[0])
    return r.results[0]["out"]
```

```python
import numpy as np
import concourse.bass as bass
from concourse import mybir
from contextlib import ExitStack


class Names:
    pass


BATCH, ROWS, COLS, FEAT = 4, 64, 64, 64
HALF = 2
BROWS = (BATCH // HALF) * ROWS
WIN = 8
NPOS = WIN * WIN
HEADS, HD = 8, 8
PAIRS = (BROWS // WIN) * (COLS // WIN)
TILES = BROWS // WIN
PPT = PAIRS // TILES
HID = 128
LAYERS = 2
EXPERTS = 16
CHUNKS = BATCH * ROWS
WARM = 24
TOL = 2.0 ** -20
SEGS = 64
SEG = BATCH * ROWS * COLS // SEGS
SEG_ROWS = SEG // COLS
EPS = 1e-5
NT = 512

C_IDENT, C_CENT64, C_MEAN64, C_CENT128, C_MEAN128, C_SWAP = (128 * n for n in range(6))
C_STACK = 768
C_MASK = C_STACK + NPOS
C_COSQ = C_MASK + HEADS
C_SINQ, C_COSK, C_SINK = C_COSQ + 64, C_COSQ + 128, C_COSQ + 192
C_END = C_COSQ + 256


def shape_constants():
    c = np.zeros((128, C_END), np.float32)
    eye = np.eye(128, dtype=np.float32)
    bd = np.kron(np.eye(2), np.ones((64, 64))).astype(np.float32) / 64
    c[:, C_IDENT:C_IDENT + 128] = eye
    c[:, C_CENT64:C_CENT64 + 128] = eye - bd
    c[:, C_MEAN64:C_MEAN64 + 128] = bd
    c[:, C_CENT128:C_CENT128 + 128] = eye - 1.0 / 128
    c[:, C_MEAN128:C_MEAN128 + 128] = 1.0 / 128
    c[np.arange(128), C_SWAP + (np.arange(128) ^ 1)] = 1.0
    c[:, C_STACK:C_STACK + 64] = np.vstack([np.eye(64), np.eye(64)])
    f = np.arange(128) % 64
    c[np.arange(128), C_MASK + f // HD] = 1.0
    half = HD // 2
    inv = (1.0 / np.float32(10000.0) ** (np.arange(0, half, 2, dtype=np.float32) / half)).astype(np.float32)
    pos = np.arange(NPOS)
    d = f % HD
    where = np.where((d // half)[:, None] == 0, (pos // WIN)[None, :], (pos % WIN)[None, :]).astype(np.float32)
    ang = where * inv[(d % half) // 2][:, None]
    cos, sin = np.cos(ang), np.sin(ang) * np.where(d % 2 == 0, -1.0, 1.0)[:, None]
    scale = HD ** -0.5
    c[:, C_COSQ:C_COSQ + 64] = cos * scale
    c[:, C_SINQ:C_SINQ + 64] = sin * scale
    c[:, C_COSK:C_COSK + 64] = cos
    c[:, C_SINK:C_SINK + 64] = sin
    return c


(W_Q, W_K, W_V, W_PROJ, W_FIN0, W_FIN1, W_OUT0, W_OUT1, W_FOUT, W_IN, W_A0, W_A1, W_B0, W_B1, W_C0, W_C1,
 W_D0, W_D1, W_S0, W_S1, W_QS, W_KS) = range(22)
NW = 22
(V_BQ, V_BK, V_BV, V_PROJ, V_IN, V_BB0, V_BB1, V_CB0, V_CB1, V_DB0, V_DB1, V_LW0, V_LW1, V_LB0, V_LB1,
 V_OUT, V_FI, V_BO, V_BS0, V_BS1, V_BR) = range(21)
NV = V_BR + LAYERS * EXPERTS
(D_PROJ, D_C0, D_C1, D_B1, D_OUT, D_WC0, D_WC1, D_QS, D_KS) = range(9)


def at_least(eng, sem, count):
    if isinstance(count, int) and count <= 0:
        return
    eng.wait_ge(sem, count)


def stand_apart(eng, sem):
    eng.sem_inc(sem, 1)


def program(nc, a, out):
    F32, I32 = mybir.dt.float32, mybir.dt.int32
    ctx = ExitStack()
    with ctx:
        def sb(name, shape, dt=F32):
            return ctx.enter_context(nc.sbuf_tensor(name, shape, dt))

        def sem(name):
            return ctx.enter_context(nc.semaphore(name))

        m = Names()
        m.nc, m.a, m.out, m.sem, m.F32, m.I32 = nc, a, out, sem, F32, I32
        m.ALU, m.ACT, m.AX = mybir.AluOpType, mybir.ActivationFunctionType, mybir.AxisListType
        m.apart = sem("apart")
        m.const = sb("const", [128, C_END])
        m.wt = sb("wt", [128, NW, 128])
        m.experts = sb("experts", [128, LAYERS, EXPERTS + 1, HID + 1])
        m.route = sb("route", [1, SEGS], I32)
        m.entry = sb("entry", [128, BATCH, ROWS + 1])
        m.vec = sb("vec", [128, 64])
        m.dvec = sb("dvec", [128, 12])
        m.eps = sb("eps", [128, 1])
        m.h = sb("h", [128, BROWS, COLS])
        m.big1 = sb("big1", [128, CHUNKS * COLS])
        m.big2 = sb("big2", [128, CHUNKS * COLS])
        m.bank = [ctx.enter_context(nc.psum_tensor(f"bank{n}", [128, NT], F32)) for n in range(8)]
        m.warm = sb("warm", [128, 2, CHUNKS])
        m.gap = sb("gap", [128, CHUNKS])
        m.agree = sb("agree", [128, 1])
        m.ones = sb("ones", [128, 1])
        m.flag = sb("flag", [1, 1], I32)
        m.ring = sb("ring", [128, 4, NT])
        prepare(m)
        window_attention(m)
        prepare_rest(m)
        norm_and_project(m, "in")
        for layer in range(LAYERS):
            recurrence(m, layer)
            mix_and_norm(m, layer)
        add_recurrent_output(m)
        norm_and_project(m, "ffn")
        routed_ffn(m)


def prepare(m):
    a, sem, ALU, ACT = m.a, m.sem, m.ALU, m.ACT
    rows = m.ring[0:64, 0, 0:128]
    x_tok = m.big1[:, 0:HALF * COLS * FEAT].rearrange("p (c h f) -> p c h f", h=HALF, f=FEAT)
    m.x_t = m.big1[:, HALF * COLS * FEAT:2 * HALF * COLS * FEAT].rearrange("p (w n) -> p w n", n=NPOS)
    ident = m.const[:, C_IDENT:C_IDENT + 128]
    swap = m.const[:, C_SWAP:C_SWAP + 128]
    m.route_raw = m.ring[0:1, 1, 0:SEGS].bitcast(m.I32)
    zeroed, const_in, attn_in, vec_in = (sem(n) for n in ("zeroed", "const_in", "attn_in", "vec_in"))
    turned, taken, small, small_out = (sem(n) for n in ("turned", "taken", "small", "small_out"))
    flipped, by_dve, by_act, m.rest_in = (sem(n) for n in ("flipped", "flip_dve", "flip_act", "rest_in"))
    XCH = 4
    x_in = [sem(f"x_in{n}") for n in range(XCH)]
    NG = COLS // 4
    n_attn, n_vec, n_rest = [0], [0], [0]

    def load(eng, slot, src, rows_at=0, cols_at=0, into=None):
        n, c = src.shape
        dst = m.wt[rows_at:rows_at + n, slot, cols_at:cols_at + c]
        if slot <= W_PROJ:
            eng.dma_start(dst, src).then_inc(attn_in, 16)
            n_attn[0] += 16
        else:
            eng.dma_start(dst, src).then_inc(m.rest_in, 16)
            n_rest[0] += 16

    def flip_dest(g):
        wc, j0 = (4 * g) // WIN, (4 * g) % WIN
        v = m.x_t.rearrange("p (t w) (i j) -> p w j t i", w=WIN, j=WIN)
        return v[:, wc, j0:j0 + 4, :, :]

    def flip_src(g):
        return m.bank[4 + g % 4][:, :].rearrange("p (j t i) -> p j t i", j=4, i=WIN)

    with m.nc.Block() as block:
        @block.sync
        def _(sp):
            sp.wait_ge(zeroed, 2)
            for p in range(HALF):
                for n, slot in enumerate((W_Q, W_K, W_V)):
                    load(sp, slot, a["L0_tok_qkv_w"][64 * n:64 * n + 64, :], 64 * p, 64 * p)
                load(sp, W_PROJ, a["L0_tok_proj_w"], 64 * p, 64 * p)

            def vector(row, src, at=0):
                c = src.shape[1]
                sp.dma_start(rows[row:row + src.shape[0], at:at + c], src).then_inc(vec_in, 16)
                n_vec[0] += 16

            for p in range(HALF):
                for n, row in enumerate((V_BQ, V_BK, V_BV)):
                    vector(row, a["L0_tok_qkv_b"][64 * n:64 * n + 64].rearrange("(a n) -> a n", a=1), 64 * p)
                vector(V_PROJ, a["L0_tok_proj_b"].rearrange("(a n) -> a n", a=1), 64 * p)
                vector(V_OUT, a["L0_attn_out_b"].rearrange("(a n) -> a n", a=1), 64 * p)
                vector(V_BO, a["L0_ffn_bo"].rearrange("(a n) -> a n", a=1), 64 * p)
            for row, name in ((V_IN, "L0_attn_in_b"), (V_FI, "L0_ffn_bi")):
                vector(row, a[name].rearrange("(a n) -> a n", a=1))
            for row, name in ((V_BB0, "B_b"), (V_CB0, "C_b"), (V_DB0, "D_b"), (V_LW0, "ln_w"), (V_LB0, "ln_b")):
                vector(row, a["L0_attn_" + name])
            vector(V_BS0, a["L0_ffn_bs"].rearrange("l s h -> (l s) h"))
            vector(V_BR, a["L0_ffn_br"].rearrange("l e h -> (l e) h"))
            for p in range(HALF):
                load(sp, W_IN, a["L0_attn_in_W"], 0, 64 * p)
                load(sp, W_FIN0 + p, a["L0_ffn_Wi"], 0, 64 * p)
                load(sp, W_OUT0 + p, a["L0_attn_out_W"], 64 * p, 0)
            load(sp, W_FOUT, a["L0_ffn_Wo"])
            for l in range(LAYERS):
                for slot, name in ((W_A0, "A_W"), (W_B0, "B_W"), (W_C0, "C_W"), (W_D0, "D_W")):
                    load(sp, slot + l, a["L0_attn_" + name][l])
                load(sp, W_S0 + l, a["L0_ffn_Ws"][l, 0])
            sp.dma_start(m.route_raw, a["L0_ffn_route_id"].rearrange("(a n) -> a n", a=1)).then_inc(m.rest_in, 16)
            for l in range(LAYERS):
                sp.dma_start(m.experts[:, l, 0:EXPERTS, 0:HID], a["L0_ffn_Wr"][l].rearrange("e h d -> h e d"))\
                    .then_inc(m.rest_in, 16)
            n_rest[0] += 16 * (1 + LAYERS)

        @block.scalar
        def _(act):
            act.dma_start(m.const[:, :], a["consts"]).then_inc(const_in, 16)
            for n in range(XCH):
                for p in range(HALF):
                    c = slice(COLS // XCH * n, COLS // XCH * (n + 1))
                    act.dma_start(x_tok[:, c, p, :], a["x"][2 * p:2 * p + 2, :, c, :].rearrange("b r c f -> (b r) c f"))\
                        .then_inc(x_in[n], 16)
            for g in range(1, NG, 2):
                act.wait_ge(flipped, g + 1)
                for j in range(4):
                    act.activation(flip_dest(g)[:, j], flip_src(g)[:, j], ACT.Copy).then_inc(by_act, 1)

        @block.gpsimd
        def _(pool):
            pool.memset(m.eps[:, :], EPS)
            pool.memset(m.ones[:, :], 1.0)

        @block.tensor
        def _(pe):
            pe.wait_ge(const_in, 16)
            pe.wait_ge(attn_in, n_attn[0])
            for n, (w, mv) in enumerate(((W_Q, ident), (W_K, ident), (W_V, ident), (W_PROJ, ident))):
                last = pe.matmul(m.bank[0][:, 128 * n:128 * n + 128], m.wt[:, w, :], mv, start=True, stop=True)
            last.then_inc(turned, 1)
            for n, w in enumerate((W_Q, W_K)):
                last = pe.matmul(m.bank[1][:, 128 * n:128 * n + 128], m.wt[:, w, :], swap, start=True, stop=True)
            last.then_inc(turned, 1)
            pe.wait_ge(vec_in, n_vec[0])
            pe.matmul(m.bank[2][:, 0:64], rows, ident[0:64, 0:64], start=True, stop=True).then_inc(small, 1)
            for g in range(NG):
                if g % (NG // XCH) == 0:
                    pe.wait_ge(x_in[g // (NG // XCH)], 16 * HALF)
                if g >= 4:
                    pe.wait_ge(by_dve if g % 2 == 0 else by_act, 4 * ((g - 4) // 2 + 1))
                for n in range(4):
                    last = pe.transpose(m.bank[4 + g % 4][:, 128 * n:128 * n + 128],
                                        x_tok[:, 4 * g + n, :, :].rearrange("p h f -> p (h f)"), ident)
                last.then_inc(flipped, 1)
            pe.wait_ge(taken, 2)
            pe.wait_ge(small_out, 1)
            product_sums(m, pe, m.bank[3], (D_PROJ, D_QS, D_KS)).then_inc(small, 1)

        @block.vector
        def _(dve):
            dve.memset(m.wt[:, 0:W_IN, :], 0.0).then_inc(zeroed, 1)
            dve.memset(rows, 0.0).then_inc(zeroed, 1)
            dve.memset(m.entry[:, :, 0:1], 0.0)
            dve.wait_ge(turned, 2)
            quad = lambda b, n: b[:, 0:128 * n].rearrange("p (n c) -> p n c", c=128)
            dve.tensor_copy(m.wt[:, W_Q:W_PROJ + 1, :], quad(m.bank[0], 4)).then_inc(taken, 1)
            dve.tensor_copy(m.wt[:, W_QS:W_KS + 1, :], quad(m.bank[1], 2)).then_inc(taken, 1)
            dve.wait_ge(small, 1)
            dve.tensor_copy(m.vec[:, :], m.bank[2][:, 0:64]).then_inc(small_out, 1)
            for g in range(0, NG, 2):
                dve.wait_ge(flipped, g + 1)
                for j in range(4):
                    dve.tensor_copy(flip_dest(g)[:, j], flip_src(g)[:, j]).then_inc(by_dve, 1)
            dve.wait_ge(small, 2)
            for d in (D_PROJ, D_QS, D_KS):
                dve.tensor_copy(m.dvec[:, d:d + 1], m.bank[3][:, d:d + 1])
    m.n_rest = n_rest[0]


def product_sums(m, pe, bank, which):
    ident, swap, cent = (m.const[:, c:c + 128] for c in (C_IDENT, C_SWAP, C_CENT128))
    v = lambda n: m.vec[:, n:n + 1]
    w = lambda n: m.wt[:, n, :]
    sums = {D_PROJ: [(ident, v(V_PROJ)), (w(W_PROJ), v(V_BV))],
            D_C0: [(cent, v(V_CB0)), (cent, v(V_DB0))],
            D_C1: [(cent, v(V_CB1)), (cent, v(V_DB1)), (w(W_D1), v(V_LB0))],
            D_B1: [(ident, v(V_BB1)), (w(W_B1), v(V_LB0))],
            D_OUT: [(ident, v(V_OUT)), (w(W_OUT0), v(V_LB1)), (w(W_OUT1), v(V_LB1))],
            D_QS: [(swap, v(V_BQ))], D_KS: [(swap, v(V_BK))]}
    for d in which:
        for k, (x, y) in enumerate(sums[d]):
            last = pe.matmul(bank[:, d:d + 1], x, y, start=(k == 0), stop=(k == len(sums[d]) - 1))
    return last


def prepare_rest(m):
    sem, ALU = m.sem, m.ALU
    ident, cent = (m.const[:, c:c + 128] for c in (C_IDENT, C_CENT128))
    turned, taken, small, small_out, routed = (sem("rest_" + n) for n in ("turned", "taken", "small", "small_out", "routed"))
    route_raw = m.route_raw
    route_f, valid, valid2 = (m.ring[0:1, 1, SEGS * n:SEGS * (n + 1)] for n in (1, 2, 3))
    jobs = [(m.wt[:, n, :], ident, False) for n in range(W_FIN0, W_C0)]
    jobs += [(m.wt[:, n, :], cent, n >= W_D0) for n in range(W_C0, W_S0)]
    jobs += [(m.wt[:, n, :], ident, True) for n in (W_S0, W_S1)]
    NGW = len(jobs) // 4
    jobs += [(m.experts[:, l, e, 0:HID], ident, False) for l in range(LAYERS) for e in range(EXPERTS)]
    NG, NB = len(jobs) // 4, 6

    with m.nc.Block() as block:
        @block.tensor
        def _(pe):
            pe.wait_ge(m.rest_in, m.n_rest)
            for g in range(NG):
                if g >= NB:
                    pe.wait_ge(taken, g - NB + 1)
                for n, (w, mv, plus) in enumerate(jobs[4 * g:4 * g + 4]):
                    dst = m.bank[g % NB][:, 128 * n:128 * n + 128]
                    last = pe.matmul(dst, w, mv, start=True, stop=not plus)
                    if plus:
                        last = pe.matmul(dst, ident, mv, start=False, stop=True)
                last.then_inc(turned, 1)
            pe.wait_ge(taken, NGW)
            product_sums(m, pe, m.bank[NB], (D_C0, D_C1, D_B1, D_OUT)).then_inc(small, 1)

        @block.vector
        def _(dve):
            for g in range(NG):
                dve.wait_ge(turned, g + 1)
                src = m.bank[g % NB][:, :].rearrange("p (n c) -> p n c", c=128)
                if g < NGW:
                    at = W_FIN0 + 4 * g
                    dve.tensor_copy(m.wt[:, at:at + 4, :], src).then_inc(taken, 1)
                else:
                    if g == NGW:
                        dve.wait_ge(taken, g)
                    l, e = (4 * (g - NGW)) // EXPERTS, (4 * (g - NGW)) % EXPERTS
                    shared = m.wt[:, W_S0 + l, :].unsqueeze(1).broadcast_to([128, 4, 128])
                    dve.tensor_tensor(m.experts[:, l, e:e + 4, 0:HID], src, shared, ALU.add).then_inc(taken, 1)
            for l in range(LAYERS):
                shared = m.vec[:, V_BS0 + l:V_BS0 + l + 1]
                dve.tensor_scalar(m.experts[:, l, 0:EXPERTS, HID:HID + 1],
                                  m.vec[:, V_BR + l * EXPERTS:V_BR + (l + 1) * EXPERTS].unsqueeze(2),
                                  shared, None, ALU.add)
                dve.tensor_copy(m.experts[:, l, EXPERTS, HID:HID + 1], shared)
                dve.tensor_copy(m.experts[:, l, EXPERTS, 0:HID], m.wt[:, W_S0 + l, :])
            dve.tensor_copy(route_f, route_raw).then_inc(routed, 1)
            dve.wait_ge(routed, 1)
            dve.tensor_scalar(valid, route_f, 0.0, None, ALU.is_ge).then_inc(routed, 1)
            dve.tensor_scalar(valid2, route_f, float(EXPERTS), None, ALU.is_lt).then_inc(routed, 1)
            dve.wait_ge(routed, 3)
            dve.tensor_tensor(valid, valid, valid2, ALU.mult).then_inc(routed, 1)
            dve.wait_ge(routed, 4)
            dve.scalar_tensor_tensor(route_f, route_f, -float(EXPERTS), valid, ALU.add, ALU.mult).then_inc(routed, 1)
            dve.wait_ge(routed, 5)
            dve.tensor_scalar(m.route[:, :], route_f, float(EXPERTS), None, ALU.add)
            dve.wait_ge(small, 1)
            dve.tensor_copy(m.dvec[:, D_C0:D_OUT + 1], m.bank[NB][:, D_C0:D_OUT + 1]).then_inc(small_out, 1)
            dve.wait_ge(small_out, 1)
            dve.tensor_tensor(m.dvec[:, D_WC0:D_WC0 + 2], m.dvec[:, D_C0:D_C0 + 2], m.vec[:, V_LW0:V_LW0 + 2], ALU.mult)


def window_attention(m):
    nc, sem, ALU, ACT, AX = m.nc, m.sem, m.ALU, m.ACT, m.AX
    cur = [0]

    def buf(*shape):
        n = int(np.prod(shape))
        v = m.big2[:, cur[0]:cur[0] + n]
        cur[0] += n
        assert cur[0] <= CHUNKS * COLS
        if len(shape) == 1:
            return v
        names = "abcde"[:len(shape)]
        return v.rearrange("p (" + " ".join(names) + ") -> p " + " ".join(names),
                           **{c: s for c, s in zip(names, shape)})

    x_now = buf(2, PPT, 2, NPOS)
    rot = buf(4, NT)
    q_bd = buf(2, PPT, 128)
    k_rot = buf(2, PPT, NPOS)
    k_mask = buf(4, HEADS, NPOS)
    shifted = buf(2, HEADS, NPOS)
    probs = buf(2, NT)
    probs_t = buf(2, 4, 128)
    v_aug = buf(2, PPT * HALF, HEADS, HD + 1)
    top = buf(2, HEADS)
    inv = buf(4, HEADS)
    o_bd = buf(PPT, 128)
    o_t = buf(NT)

    b_s, b_pt, b_o, b_x, b_h = m.bank[0:2], m.bank[2:4], m.bank[4:6], m.bank[6], m.bank[7]
    bo_psum = [b[:, :].rearrange("p (n s) -> p n s", s=256) for b in b_o]
    cst = lambda c, n: m.const[:, c:c + n]

    x_ready = [sem(f"at_x_ready{n}") for n in range(2)]
    S = Names()
    S.zeroed, S.x_mm, S.rope, S.v_copied = (sem("at_" + n) for n in ("zeroed", "x_mm", "rope", "v_copied"))
    S.q_ready, S.krot, S.kmask, S.scores, S.maxed = (sem("at_" + n) for n in ("q_ready", "krot", "kmask", "scores", "maxed"))
    S.shifted, S.probs, S.pt, S.pt_copied, S.av = (sem("at_" + n) for n in ("shifted", "probs", "pt", "pt_copied", "av"))
    S.inv, S.normed, S.ot, S.ot_copied, S.proj = (sem("at_" + n) for n in ("inv", "normed", "ot", "ot_copied", "proj"))
    S.h, = (sem("at_" + n) for n in ("h",))
    def over_tiles(eng, tile):
        tile(0, 0, "first")
        tile(1, 1, "mid")
        tile(2, 0, "mid")
        with eng.Fori(1, (TILES - 2) // 2) as u:
            tile(u * 2 + 1, 1, "mid")
            tile(u * 2 + 2, 0, "mid")
        tile(TILES - 1, (TILES - 1) % 2, "last")
        tile(TILES, TILES % 2, "drain")

    def flags(kind):
        return kind != "drain", kind in ("first", "mid"), kind != "first"

    with nc.Block() as block:
        @block.tensor
        def _(pe):
            def product(t, par, n):
                at_least(pe, x_ready[par], (t - par) * 16 + 32)
                if n < 4:
                    at_least(pe, S.rope, t * 4 + n)
                    if n == 0:
                        at_least(pe, S.v_copied, t * 4)
                    pe.matmul(b_x[:, :], m.wt[:, (W_Q, W_QS, W_K, W_KS)[n], :], x_now[:, par, :, 0, :],
                              start=True, stop=True).then_inc(S.x_mm, 1)
                else:
                    at_least(pe, S.rope, t * 4 + 4)
                    at_least(pe, S.v_copied, t * 4 + 2 * (n - 4))
                    for k in range(4):
                        pr = 4 * (n - 4) + k
                        tok = x_now[:, par, pr, :, :].rearrange("p a n -> p (a n)")
                        last = pe.matmul(b_x[:, 128 * k:128 * k + 128], tok, m.wt[:, W_V, :], start=True, stop=True)
                    last.then_inc(S.x_mm, 1)

            def scores(i, par, j):
                at_least(pe, S.kmask, i + 1)
                at_least(pe, S.shifted, i - 1)
                pe.matmul(b_s[j % 2][:, :], q_bd[:, par, j, :], k_mask[:, j % 4].rearrange("p h n -> p (h n)"),
                          start=True, stop=True).then_inc(S.scores, 1)

            def tile(t, par, kind):
                now, nxt, prev = flags(kind)
                for j in range(PPT):
                    i = t * PPT + j
                    if now and j < PPT - 1:
                        scores(i + 1, par, j + 1)
                    if nxt and j == PPT - 1:
                        at_least(pe, S.q_ready, t * 2 + 4)
                        scores(i + 1, 1 - par, 0)
                    if prev and j == 4:
                        at_least(pe, S.normed, t * 8)
                        at_least(pe, S.h, t - 1)
                        for pr in range(PPT):
                            last = pe.matmul(b_h[:, NPOS * pr:NPOS * (pr + 1)], o_bd[:, pr, :], cst(C_STACK, NPOS),
                                             start=True, stop=True)
                        last.then_inc(S.ot, 1)
                    if prev and j == 6:
                        at_least(pe, S.ot_copied, t)
                        pe.matmul(b_h[:, :], m.wt[:, W_PROJ, :], o_t, start=True, stop=True).then_inc(S.proj, 1)
                    if (now and j >= 1) or (prev and j < 1):
                        at_least(pe, S.probs, i)
                        at_least(pe, S.pt_copied, i - 2)
                        for c in range(4):
                            last = pe.transpose(b_pt[(j + 1) % 2][:, 128 * c:128 * c + 128],
                                                probs[:, (j + 1) % 2, 128 * c:128 * c + 128], cst(C_IDENT, 128))
                        last.then_inc(S.pt, 1)
                    if (now and j >= 2) or (prev and j < 2):
                        jj = (j - 2) % PPT
                        vpar = par if j >= 2 else 1 - par
                        at_least(pe, S.pt_copied, i - 1)
                        if jj % 4 == 0:
                            at_least(pe, S.v_copied, (t * 4 if j >= 2 else t * 4 - 4) + 2 * (jj // 4 + 1))
                        if jj % 2 == 0:
                            at_least(pe, S.normed, (t * 8 if j >= 2 else t * 8 - 8) + jj - 2)
                        dst = bo_psum[(jj % 4) // 2][:, jj % 2, 0:144].rearrange("p (h k d) -> p h k d", h=HALF, k=4)
                        for c in range(4):
                            last = pe.matmul(dst[:, :, c, :], probs_t[:, j % 2, c, :],
                                             v_aug[:, vpar, HALF * jj:HALF * jj + 2, 2 * c:2 * c + 2, :]
                                             .rearrange("p a h d -> p a (h d)"), start=True, stop=True)
                        last.then_inc(S.av, 1)
                    if nxt and j < 6:
                        product(t + 1, 1 - par, j)

            for n in range(6):
                product(0, 0, n)
            at_least(pe, S.q_ready, 2)
            scores(0, 0, 0)
            over_tiles(pe, tile)

        @block.vector
        def _(dve):
            def rope(t, n):
                at_least(dve, S.x_mm, t * 6 + n + 1)
                if n < 2:
                    at_least(dve, S.q_ready, t * 2)
                else:
                    at_least(dve, S.krot, t)
                bias = (m.vec[:, V_BQ:V_BQ + 1], m.dvec[:, D_QS:D_QS + 1], m.vec[:, V_BK:V_BK + 1],
                        m.dvec[:, D_KS:D_KS + 1])[n]
                table = cst((C_COSQ, C_SINQ, C_COSK, C_SINK)[n], NPOS).unsqueeze(1).broadcast_to([128, PPT, NPOS])
                dve.scalar_tensor_tensor(rot[:, n, :].rearrange("p (w n) -> p w n", n=NPOS),
                                         b_x[:, :].rearrange("p (w n) -> p w n", n=NPOS), bias, table,
                                         ALU.add, ALU.mult).then_inc(S.rope, 1)

            def tile(t, par, kind):
                now, nxt, prev = flags(kind)
                for j in range(PPT):
                    i = t * PPT + j
                    if now:
                        at_least(dve, S.scores, i + 1)
                        at_least(dve, S.shifted, i - 1)
                        sc = b_s[j % 2][:, :].rearrange("p (h n) -> p h n", n=NPOS)
                        dve.tensor_reduce(top[:, j % 2, :], sc, AX.X, ALU.max).then_inc(S.maxed, 1)
                        dve.wait_ge(S.maxed, i + 1)
                        at_least(dve, S.probs, i - 1)
                        dve.tensor_tensor(shifted[:, j % 2], sc, top[:, j % 2, :].unsqueeze(2)
                                          .broadcast_to([128, HEADS, NPOS]), ALU.subtract).then_inc(S.shifted, 1)
                    if (now and j in (4, 6)) or (prev and j in (0, 2)):
                        jj = (j - 4) % PPT
                        b = (jj // 2) % 2
                        n0 = t * 8 + (j - 4)
                        at_least(dve, S.av, i - 2)
                        if jj == 0:
                            at_least(dve, S.ot, t)
                        halves = [(slice(64 * p, 64 * p + 64), slice(72 * p, 72 * p + 72)) for p in range(HALF)]
                        outs = [bo_psum[b][s, :, c].rearrange("p n (h d) -> p n h d", d=HD + 1) for s, c in halves]
                        for p, (s, c) in enumerate(halves):
                            dve.reciprocal(inv[s, 2 * b:2 * b + 2, :], outs[p][:, :, :, HD]).then_inc(S.inv, 1)
                        for p, (s, c) in enumerate(halves):
                            dve.wait_ge(S.inv, n0 + 1 + p)
                            dve.tensor_tensor(
                                o_bd[s, jj:jj + 2, 64 * p:64 * p + 64].rearrange("p n (h d) -> p n h d", d=HD),
                                outs[p][:, :, :, 0:HD],
                                inv[s, 2 * b:2 * b + 2, :].unsqueeze(3).broadcast_to([64, 2, HEADS, HD]),
                                ALU.mult).then_inc(S.normed, 1)
                    if nxt and j < 4:
                        rope(t + 1, j)

            dve.memset(q_bd[:, :, :, :], 0.0).then_inc(S.zeroed, 1)
            dve.memset(o_bd[:, :, :], 0.0).then_inc(S.zeroed, 1)
            dve.memset(v_aug[:, :, :, :, :], 0.0).then_inc(S.zeroed, 1)
            dve.wait_ge(S.zeroed, 3)
            va = v_aug.rearrange("p a b (c k) d -> p (a b) c k d", k=2)
            for k in range(2):
                dve.memset(va[64 * k:64 * k + 64, :, :, k, HD], 1.0).then_inc(S.zeroed, 1)
            dve.wait_ge(S.zeroed, 5)
            for n in range(4):
                rope(0, n)
            over_tiles(dve, tile)

        @block.scalar
        def _(act):
            def v_copy(t, par, n):
                at_least(act, S.x_mm, t * 6 + 5 + n)
                at_least(act, S.av, t * PPT - PPT)
                src = b_x[:, :].rearrange("p (a c k d) -> p a c k d", a=8, c=4, k=2)
                dst = v_aug[:, par, 8 * n:8 * n + 8, :, :].rearrange("p a (c k) d -> p a c k d", k=2)
                for k in range(2):
                    s = slice(64 * k, 64 * k + 64)
                    act.activation(dst[s, :, :, k, 0:HD], src[s, :, :, k, :], ACT.Copy).then_inc(S.v_copied, 1)

            def tile(t, par, kind):
                now, nxt, prev = flags(kind)
                for j in range(PPT):
                    i = t * PPT + j
                    if now:
                        at_least(act, S.shifted, i + 1)
                        at_least(act, S.pt, i - 1)
                        act.activation(probs[:, j % 2, :], shifted[:, j % 2].rearrange("p h n -> p (h n)"),
                                       ACT.Exp).then_inc(S.probs, 1)
                    if (now and j >= 1) or (prev and j < 1):
                        at_least(act, S.pt, i)
                        at_least(act, S.av, i - 2)
                        act.activation(probs_t[:, (j + 1) % 2].rearrange("p c n -> p (c n)"),
                                       b_pt[(j + 1) % 2][:, :], ACT.Copy).then_inc(S.pt_copied, 1)
                    if nxt and j in (4, 5):
                        v_copy(t + 1, 1 - par, j - 4)
                    if prev and j == 5:
                        at_least(act, S.ot, t)
                        at_least(act, S.proj, t - 1)
                        act.activation(o_t, b_h[:, :], ACT.Copy).then_inc(S.ot_copied, 1)
                    if prev and j == 7:
                        at_least(act, S.proj, t)
                        act.activation(m.h[:, bass.ds(t * WIN - WIN, WIN), :].rearrange("p i (w j) -> p w i j", j=WIN),
                                       b_h[:, :].rearrange("p (w i j) -> p w i j", w=WIN, j=WIN),
                                       ACT.Identity, bias=m.dvec[:, D_PROJ:D_PROJ + 1]).then_inc(S.h, 1)

            act.wait_ge(S.zeroed, 5)
            for n in range(2):
                v_copy(0, 0, n)
            over_tiles(act, tile)

        @block.gpsimd
        def _(pool):
            def mask(i, par, jj):
                at_least(pool, S.scores, i - 3)
                pool.tensor_tensor(k_mask[:, jj % 4], k_rot[:, par, jj, :].unsqueeze(1).broadcast_to([128, HEADS, NPOS]),
                                   cst(C_MASK, HEADS).unsqueeze(2).broadcast_to([128, HEADS, NPOS]),
                                   ALU.mult).then_inc(S.kmask, 1)

            def add_q(t, par):
                at_least(pool, S.rope, t * 4 + 2)
                at_least(pool, S.scores, t * PPT - PPT)
                at_least(pool, S.kmask, t * PPT - 2)
                for p in range(HALF):
                    s = slice(64 * p, 64 * p + 64)
                    at_least(pool, S.q_ready, t * 2 + p)
                    pool.tensor_tensor(q_bd[s, par, :, 64 * p:64 * p + 64],
                                       rot[s, 0, :].rearrange("p (w n) -> p w n", n=NPOS),
                                       rot[s, 1, :].rearrange("p (w n) -> p w n", n=NPOS), ALU.add).then_inc(S.q_ready, 1)
                at_least(pool, S.q_ready, t * 2 + 2)

            def add_k(t, par):
                at_least(pool, S.rope, t * 4 + 4)
                at_least(pool, S.kmask, t * PPT - PPT)
                pool.tensor_tensor(k_rot[:, par].rearrange("p w n -> p (w n)"), rot[:, 2, :], rot[:, 3, :],
                                   ALU.add).then_inc(S.krot, 1)
                pool.wait_ge(S.krot, t + 1)

            def tile(t, par, kind):
                now, nxt, prev = flags(kind)
                for j in range(PPT):
                    i = t * PPT + j
                    if nxt and j == 3:
                        add_q(t + 1, 1 - par)
                    if nxt and j == PPT - 3:
                        add_k(t + 1, 1 - par)
                    if now and j < PPT - 3:
                        mask(i + 3, par, j + 3)
                    elif nxt:
                        mask(i + 3, 1 - par, j + 3 - PPT)

            pool.wait_ge(S.zeroed, 5)
            add_q(0, 0)
            add_k(0, 0)
            for jj in range(3):
                mask(jj, 0, jj)
            over_tiles(pool, tile)

        @block.sync
        def _(sp):
            def load_x(t, par):
                at_least(sp, S.x_mm, t * 6 - 6)
                stand_apart(sp, m.apart)
                for k in range(2):
                    sp.dma_start(x_now[:, par, :, k, :], m.x_t[:, bass.ds(t * PPT, PPT), :]).then_inc(x_ready[par], 16)
            load_x(0, 0)
            load_x(1, 1)
            with sp.Fori(1, TILES // 2) as k:
                load_x(k * 2, 0)
                load_x(k * 2 + 1, 1)


def norm_and_project(m, kind):
    sem, ALU, ACT = m.sem, m.ALU, m.ACT
    m.x1 = m.big1[:, :].rearrange("p (c n) -> p c n", n=CHUNKS)
    m.y = m.big1[:, 0:BROWS * COLS]
    h = m.h[:, :, :].rearrange("p r c -> p (r c)")
    buf = m.big2[:, 0:8 * NT].rearrange("p (n c) -> p n c", c=NT)
    square, log, rstd, u = buf[:, 0:2], buf[:, 2:4], buf[:, 4:6], buf[:, 6:8]
    N = Names()
    N.centred, N.squared, N.variance, N.log, N.rstd = (sem(f"{kind}_" + n) for n in ("centred", "squared", "variance", "log", "rstd"))
    N.scaled, N.product, N.copied0, N.copied1 = (sem(f"{kind}_" + n) for n in ("scaled", "product", "copied0", "copied1"))
    b_c, b_v, b_p = m.bank[0:2], m.bank[2:4], m.bank[4:8]
    w = lambda c: m.const[:, c:c + 128]
    project = kind == "in"

    with m.nc.Block() as block:
        @block.tensor
        def _(pe):
            def centre(t, par):
                at_least(pe, N.scaled, t - 1)
                pe.matmul(b_c[par][:, :], w(C_CENT64), h[:, bass.ds(t * NT, NT)], start=True, stop=True)\
                    .then_inc(N.centred, 1)

            def tile(t, par, first=False, last=False):
                if not last:
                    centre(t + 1, 1 - par)
                at_least(pe, N.squared, t + 1)
                at_least(pe, N.log, t - 1)
                pe.matmul(b_v[par][:, :], w(C_MEAN64), square[:, par, :], start=True, stop=True)\
                    .then_inc(N.variance, 1)
                if project and not first:
                    in_product(t - 1, 1 - par)

            def in_product(t, par):
                at_least(pe, N.scaled, t + 1)
                at_least(pe, N.copied0, t - 1)
                at_least(pe, N.copied1, t - 1)
                for p in range(HALF):
                    s = slice(64 * p, 64 * p + 64)
                    pe.matmul(b_p[2 * par + p][:, :], m.wt[s, W_IN, :], u[s, par, :], start=True, stop=True)\
                        .then_inc(N.product, 1)

            centre(0, 0)
            tile(0, 0, first=True)
            tile(1, 1)
            tile(2, 0)
            with pe.Fori(1, (TILES - 2) // 2) as k:
                tile(k * 2 + 1, 1)
                tile(k * 2 + 2, 0)
            tile(TILES - 1, 1, last=True)
            if project:
                in_product(TILES - 1, 1)

        def copy_in(t, p):
            return (m.x1[:, :, bass.ds(t * WIN + p * BROWS, WIN)].rearrange("p c i -> p i c"),
                    lambda par: b_p[2 * par + p][:, :].rearrange("p (i c) -> p i c", c=COLS))

        @block.scalar
        def _(act):
            def tile(t, par, first=False):
                at_least(act, N.centred, t + 1)
                at_least(act, N.variance, t - 1)
                act.activation(square[:, par, :], b_c[par][:, :], ACT.Square).then_inc(N.squared, 1)
                at_least(act, N.variance, t + 1)
                act.activation(log[:, par, :], b_v[par][:, :], ACT.Ln, bias=m.eps[:, :]).then_inc(N.log, 1)
                act.wait_ge(N.log, t + 1)
                at_least(act, N.scaled, t - 1)
                act.activation(rstd[:, par, :], log[:, par, :], ACT.Exp, scale=-0.5).then_inc(N.rstd, 1)
                if project and not first:
                    copied(t - 1, 1 - par)

            def copied(t, par):
                at_least(act, N.product, t * 2 + 1)
                dst, src = copy_in(t, 0)
                act.activation(dst, src(par), ACT.Identity, bias=m.vec[:, V_IN:V_IN + 1]).then_inc(N.copied0, 1)

            act.preload_act_table_set("natural_log_exp_and_others")
            tile(0, 0, first=True)
            tile(1, 1)
            tile(2, 0)
            with act.Fori(1, (TILES - 2) // 2) as k:
                tile(k * 2 + 1, 1)
                tile(k * 2 + 2, 0)
            tile(TILES - 1, 1)
            if project:
                copied(TILES - 1, 1)

        @block.vector
        def _(dve):
            def tile(t, par, first=False):
                at_least(dve, N.rstd, t + 1)
                if project:
                    at_least(dve, N.product, t * 2 - 2)
                dst = u[:, par, :] if project else m.y[:, bass.ds(t * NT, NT)]
                dve.tensor_tensor(dst, b_c[par][:, :], rstd[:, par, :], ALU.mult).then_inc(N.scaled, 1)
                if project and not first:
                    copied(t - 1, 1 - par)

            def copied(t, par):
                at_least(dve, N.product, t * 2 + 2)
                dst, src = copy_in(t, 1)
                dve.tensor_scalar(dst, src(par), m.vec[:, V_IN:V_IN + 1], None, ALU.add).then_inc(N.copied1, 1)

            tile(0, 0, first=True)
            tile(1, 1)
            tile(2, 0)
            with dve.Fori(1, (TILES - 2) // 2) as k:
                tile(k * 2 + 1, 1)
                tile(k * 2 + 2, 0)
            tile(TILES - 1, 1)
            if project:
                copied(TILES - 1, 1)


def recurrence(m, layer):
    sem, ALU, ACT = m.sem, m.ALU, m.ACT
    x1 = m.x1
    hs = m.hs = m.big2[:, :].rearrange("p (c n) -> p c n", n=CHUNKS)
    GROUPS, GB = 2, BATCH // 2
    GC = CHUNKS // GROUPS
    w_a, w_b = m.wt[:, W_A0 + layer, :], m.wt[:, W_B0 + layer, :]
    bias = m.vec[:, V_BB0:V_BB0 + 1] if layer == 0 else m.dvec[:, D_B1:D_B1 + 1]
    cols = [slice(GC * g, GC * g + GC) for g in range(GROUPS)]
    bank = [[m.bank[2 * g + k][:, 0:GC] for k in range(2)] for g in range(GROUPS)]
    T = f"l{layer}_"
    summed = [sem(T + f"summed{g}") for g in range(GROUPS)]
    stepped = [sem(T + f"stepped{g}") for g in range(GROUPS)]
    again_summed = [sem(T + f"again_summed{g}") for g in range(GROUPS)]
    again_stepped = [sem(T + f"again_stepped{g}") for g in range(GROUPS)]
    again_first, cleared, compared, counted = (sem(T + n) for n in ("again_first", "cleared", "compared", "counted"))
    warm = [m.warm[:, k, :] for k in range(2)]
    entry = [m.entry[:, GB * g:GB * g + GB, 0:ROWS] for g in range(GROUPS)]
    ending = [m.entry[:, GB * g:GB * g + GB, 1:ROWS + 1] for g in range(GROUPS)]
    by_row = lambda v: v.rearrange("p (b r) -> p b r", r=ROWS)
    MAIN = COLS + 1

    with m.nc.Block() as block:
        @block.vector
        def _(dve):
            dve.memset(warm[1], 0.0).then_inc(cleared, 1)
            for g in range(GROUPS):
                dve.wait_ge(stepped[g], WARM + MAIN)
                dve.tensor_tensor(by_row(m.gap[:, cols[g]]), by_row(hs[:, COLS - 1, cols[g]]), ending[g],
                                  ALU.subtract).then_inc(compared, 1)
            dve.wait_ge(compared, GROUPS)
            dve.tensor_tensor(m.gap[:, :], m.gap[:, :], m.gap[:, :], ALU.mult).then_inc(compared, 1)
            dve.wait_ge(compared, GROUPS + 1)
            dve.tensor_scalar(m.gap[:, :], m.gap[:, :], TOL * TOL, None, ALU.is_le).then_inc(compared, 1)
            dve.wait_ge(compared, GROUPS + 2)
            dve.tensor_reduce(m.agree[:, :], m.gap[:, :].rearrange("p (b r) -> p b r", r=ROWS)[:, :, 0:ROWS - 1],
                              m.AX.XY, ALU.min).then_inc(compared, 1)
            dve.wait_ge(counted, 1)
            dve.tensor_copy(m.flag[:, :], m.bank[7][0:1, 0:1])

        def step_a(pe, g, k, state, done, ready, count):
            pe.wait_ge(ready[g], count)
            pe.matmul(bank[g][k % 2], w_a, state, start=False, stop=True).then_inc(done[g], 1)

        def step_b(pe, g, par, c):
            x = x1[:, c, cols[g]] if isinstance(c, int) else \
                x1[:, bass.ds(c, 1), cols[g]].rearrange("p a n -> p (a n)")
            pe.matmul(bank[g][par], w_b, x, start=True, stop=False)

        def state_at(c, g):
            return hs[:, c, cols[g]] if isinstance(c, int) else \
                hs[:, bass.ds(c, 1), cols[g]].rearrange("p a n -> p (a n)")

        def main_pass(pe, done, ready, base, last_b=True):
            for g in range(GROUPS):
                step_a(pe, g, 0, entry[g], done, ready, base + 1)
                step_b(pe, g, 1, 1)
            with pe.Fori(0, (COLS - 2) // 2) as u:
                for k in (1, 2):
                    for g in range(GROUPS):
                        step_a(pe, g, k, state_at(u * 2 + (k - 1), g), done, ready, u * 2 + (base + 1 + k))
                        step_b(pe, g, (k + 1) % 2, u * 2 + (k + 1))
            for g in range(GROUPS):
                step_a(pe, g, COLS - 1, state_at(COLS - 2, g), done, ready, base + COLS)

        def main_states(act, done, ready, base):
            def step(k, par):
                for g in range(GROUPS):
                    act.wait_ge(done[g], base + 1 + k if isinstance(k, int) else k + (base + 1))
                    act.activation(state_at(k, g), bank[g][par], ACT.Tanh, bias=bias).then_inc(ready[g], 1)
            with act.Fori(0, COLS // 2) as u:
                step(u * 2, 0)
                step(u * 2 + 1, 1)

        @block.tensor
        def _(pe):
            C0 = COLS - WARM
            pe.wait_ge(cleared, 1)
            for g in range(GROUPS):
                step_b(pe, g, 0, C0)
            for g in range(GROUPS):
                pe.matmul(bank[g][0], w_a, warm[1][:, cols[g]], start=False, stop=True).then_inc(summed[g], 1)
                step_b(pe, g, 1, C0 + 1)
            with pe.Fori(0, (WARM - 2) // 2) as u:
                for k in (1, 2):
                    for g in range(GROUPS):
                        step_a(pe, g, k, warm[(k + 1) % 2][:, cols[g]], summed, stepped, u * 2 + k)
                        step_b(pe, g, (k + 1) % 2, u * 2 + (C0 + k + 1))
            for g in range(GROUPS):
                step_a(pe, g, WARM - 1, warm[0][:, cols[g]], summed, stepped, WARM - 1)
                step_b(pe, g, 0, 0)
            main_pass(pe, summed, stepped, WARM)
            pe.wait_ge(compared, GROUPS + 3)
            pe.matmul(m.bank[7][0:1, 0:1], m.agree[:, :], m.ones[:, :], start=True, stop=True).then_inc(counted, 1)

        @block.scalar
        def _(act):
            act.preload_act_table(ACT.Tanh)
            with act.Fori(0, WARM // 2) as u:
                for k in range(2):
                    for g in range(GROUPS):
                        act.wait_ge(summed[g], u * 2 + (k + 1))
                        act.activation(warm[k][:, cols[g]], bank[g][k], ACT.Tanh, bias=bias).then_inc(stepped[g], 1)
            for g in range(GROUPS):
                act.wait_ge(stepped[g], WARM)
                act.activation(ending[g], by_row(warm[1][:, cols[g]]), ACT.Copy).then_inc(stepped[g], 1)
            main_states(act, summed, stepped, WARM)

    with m.nc.Block() as block:
        @block.tensor
        def _(pe):
            agreeing = pe.value_load(m.flag[0:1, 0:1], min_val=0, max_val=128)
            with pe.If(agreeing < 128):
                with pe.Fori(0, ROWS - 1) as rep:
                    for g in range(GROUPS):
                        at = rep * MAIN + 1
                        pe.wait_ge(again_stepped[g], at)
                        step_b(pe, g, 0, 0)
                    main_pass(pe, again_summed, again_stepped, rep * MAIN)

        @block.scalar
        def _(act):
            agreeing = act.value_load(m.flag[0:1, 0:1], min_val=0, max_val=128)
            with act.If(agreeing < 128):
                with act.Fori(0, ROWS - 1) as rep:
                    for g in range(GROUPS):
                        act.activation(ending[g], by_row(hs[:, COLS - 1, cols[g]]), ACT.Copy)\
                            .then_inc(again_stepped[g], 1)
                    main_states(act, again_summed, again_stepped, rep * COLS)
                    for g in range(GROUPS):
                        act.wait_ge(again_stepped[g], rep * MAIN + MAIN)


def mix_and_norm(m, layer):
    sem, ALU, ACT = m.sem, m.ALU, m.ACT
    STEPS = CHUNKS * COLS // NT
    hs, x = m.big2, m.big1
    b_y, b_v = m.bank[0:2], m.bank[2:4]
    w_c, w_d = m.wt[:, W_C0 + layer, :], m.wt[:, W_D0 + layer, :]
    scale = m.vec[:, V_LW0 + layer:V_LW0 + layer + 1]
    b_scaled = m.dvec[:, D_WC0 + layer:D_WC0 + layer + 1]
    b_plain = m.dvec[:, D_C0 + layer:D_C0 + layer + 1]
    M = Names()
    M.mixed, M.squared, M.weighted, M.variance, M.log = (sem(f"mix{layer}_" + n) for n in ("mixed", "squared", "weighted", "variance", "log"))
    M.rstd, M.written = (sem(f"mix{layer}_" + n) for n in ("rstd", "written"))
    square = log = rstd = m.ring[:, 0:2, :]
    weighted = m.ring[:, 2:4, :]

    def over_tiles(eng, tile, tail=None):
        for t in range(3):
            tile(t, t % 2)
        with eng.Fori(1, (STEPS - 2) // 2) as k:
            tile(k * 2 + 1, 1)
            tile(k * 2 + 2, 0)
        tile(STEPS - 1, 1, last=True)

    with m.nc.Block() as block:
        @block.tensor
        def _(pe):
            def mix(t, par):
                at_least(pe, M.squared, t - 1)
                at_least(pe, M.weighted, t - 1)
                pe.matmul(b_y[par][:, :], w_c, hs[:, bass.ds(t * NT, NT)], start=True, stop=False)
                pe.matmul(b_y[par][:, :], w_d, x[:, bass.ds(t * NT, NT)], start=False, stop=True).then_inc(M.mixed, 1)

            def tile(t, par, last=False):
                if not last:
                    mix(t + 1, 1 - par)
                at_least(pe, M.squared, t + 1)
                at_least(pe, M.log, t - 1)
                pe.matmul(b_v[par][:, :], m.const[:, C_MEAN128:C_MEAN128 + 128], square[:, par, :],
                          start=True, stop=True).then_inc(M.variance, 1)
            mix(0, 0)
            over_tiles(pe, tile)

        @block.scalar
        def _(act):
            def tile(t, par, last=False):
                at_least(act, M.mixed, t + 1)
                at_least(act, M.written, t - 1)
                act.activation(square[:, par, :], b_y[par][:, :], ACT.Square, bias=b_plain).then_inc(M.squared, 1)
                at_least(act, M.variance, t + 1)
                act.activation(log[:, par, :], b_v[par][:, :], ACT.Ln, bias=m.eps[:, :]).then_inc(M.log, 1)
                act.wait_ge(M.log, t + 1)
                act.activation(rstd[:, par, :], log[:, par, :], ACT.Exp, scale=-0.5).then_inc(M.rstd, 1)
            act.preload_act_table_set("natural_log_exp_and_others")
            over_tiles(act, tile)

        @block.vector
        def _(dve):
            def tile(t, par, last=False):
                at_least(dve, M.mixed, t + 1)
                at_least(dve, M.squared, t + 1)
                at_least(dve, M.written, t - 1)
                dve.tensor_scalar(weighted[:, par, :], b_y[par][:, :], scale, b_scaled, ALU.mult, ALU.add)\
                    .then_inc(M.weighted, 1)
                dve.wait_ge(M.weighted, t + 1)
                at_least(dve, M.rstd, t + 1)
                dve.tensor_tensor(x[:, bass.ds(t * NT, NT)], weighted[:, par, :], rstd[:, par, :], ALU.mult)\
                    .then_inc(M.written, 1)
            over_tiles(dve, tile)


def add_recurrent_output(m):
    summed, added = m.sem("out_summed"), m.sem("out_added")

    with m.nc.Block() as block:
        @block.tensor
        def _(pe):
            def tile(t, par):
                at_least(pe, added, t - 1)
                for p in range(HALF):
                    last = pe.matmul(m.bank[par][:, :], m.wt[:, W_OUT0 + p, :],
                                     m.x1[:, :, bass.ds(t * WIN + p * BROWS, WIN)],
                                     start=(p == 0), stop=(p == HALF - 1))
                last.then_inc(summed, 1)
            tile(0, 0)
            tile(1, 1)
            with pe.Fori(1, TILES // 2) as k:
                tile(k * 2, 0)
                tile(k * 2 + 1, 1)

        @block.vector
        def _(dve):
            with dve.Fori(0, TILES // 2) as k:
                for par in range(2):
                    t = k * 2 + par
                    dve.wait_ge(summed, t + 1)
                    h = m.h[:, bass.ds(t * WIN, WIN), :].rearrange("p i c -> p c i")
                    dve.scalar_tensor_tensor(h, m.bank[par][:, :].rearrange("p (c i) -> p c i", i=WIN),
                                             m.dvec[:, D_OUT:D_OUT + 1], h, m.ALU.add, m.ALU.add).then_inc(added, 1)


def routed_ffn(m):
    sem, ALU, ACT = m.sem, m.ALU, m.ACT
    cur = [0]

    def buf(*shape):
        n = int(np.prod(shape))
        v = m.big2[:, cur[0]:cur[0] + n]
        cur[0] += n
        names = "abcde"[:len(shape)]
        return v if len(shape) == 1 else v.rearrange(
            "p (" + " ".join(names) + ") -> p " + " ".join(names), **{c: s for c, s in zip(names, shape)})

    act1, act2 = buf(2, NT), buf(2, NT)
    RING = 4
    act3 = buf(RING, NT)
    expert = buf(LAYERS, RING, 2, HID + 1)
    final = buf(NT)
    result = buf(2, HALF, 4 * FEAT)
    h = m.h[:, :, :].rearrange("p r c -> p (r c)")
    out = m.out.rearrange("b s f -> (b s) f")
    stored = [sem(f"ffn_stored{k}") for k in range(2)]
    R = Names()
    R.expert, R.mm1, R.relu1, R.mm2 = (sem("ffn_" + n) for n in ("expert", "mm1", "relu1", "mm2"))
    R.relu2, R.mm3, R.relu3, R.mm4 = (sem("ffn_" + n) for n in ("relu2", "mm3", "relu3", "mm4"))
    R.final, R.turned, R.result = (sem("ffn_" + n) for n in ("final", "turned", "result"))
    b1, b2, b3, b_final, b_turned = m.bank[0:2], m.bank[2:4], m.bank[4:6], m.bank[6], m.bank[7]
    UNITS = HALF * TILES

    def over_units(eng, unit):
        for u in range(2 * RING):
            unit(u // 2, u % RING)
        with eng.Fori(2, TILES // 2) as v:
            for q in range(RING):
                unit(v * 2 + q // 2, q)
        for u in range(UNITS, UNITS + RING):
            unit(u // 2, u % RING)

    def runs(u, stage):
        return not isinstance(u, int) or 0 <= u - stage < UNITS

    with m.nc.Block() as block:
        @block.tensor
        def _(pe):
            def unit(t, q):
                par = q % 2
                u = t * 2 + par
                if runs(u, 0):
                    at_least(pe, R.relu1, u - 1)
                    pe.matmul(b1[par][:, :], m.wt[:, W_FIN0 + par, :], m.y[:, bass.ds(t * NT, NT)],
                              start=True, stop=True).then_inc(R.mm1, 1)
                for st, src, dst, ready, free, done in (
                        (1, act1[:, 1 - par], b2, R.relu1, R.relu2, R.mm2),
                        (2, act2[:, par], b3, R.relu2, R.relu3, R.mm3)):
                    if runs(u, st):
                        k = u - st
                        at_least(pe, ready, k + 1)
                        at_least(pe, free, k - 1)
                        at_least(pe, R.expert, k * 2 + 2)
                        for s in range(2):
                            c = slice(SEG * s, SEG * s + SEG)
                            last = pe.matmul(dst[(q - st) % 2][:, c], expert[:, st - 1, (q - st) % RING, s, 0:HID],
                                             src[:, c], start=True, stop=True)
                        last.then_inc(done, 1)
                if runs(u, 3):
                    at_least(pe, R.relu3, u - 2)
                    if par == 1:
                        at_least(pe, R.final, t - 1)
                    p = 1 - par
                    pe.matmul(b_final[64 * p:64 * p + 64, :], m.wt[:, W_FOUT, 0:FEAT], act3[:, (q - 3) % RING],
                              start=True, stop=True).then_inc(R.mm4, 1)
                if par == 1 and runs(u, 5):
                    at_least(pe, R.final, t - 1)
                    at_least(pe, R.result, t - 2)
                    for s in range(4):
                        last = pe.transpose(b_turned[:, 128 * s:128 * s + 128], final[:, s:NT:4],
                                            m.const[:, C_IDENT:C_IDENT + 128])
                    last.then_inc(R.turned, 1)
            over_units(pe, unit)

        @block.scalar
        def _(act):
            def unit(t, q):
                par = q % 2
                u = t * 2 + par
                if runs(u, 0):
                    at_least(act, R.mm1, u + 1)
                    at_least(act, R.mm2, u - 1)
                    act.activation(act1[:, par, :], b1[par][:, :], ACT.Relu, bias=m.vec[:, V_FI:V_FI + 1]).then_inc(R.relu1, 1)
                if runs(u, 1):
                    at_least(act, R.mm2, u)
                    at_least(act, R.mm3, u - 2)
                    for s in range(2):
                        c = slice(SEG * s, SEG * s + SEG)
                        last = act.activation(act2[:, 1 - par, c], b2[1 - par][:, c], ACT.Relu,
                                              bias=expert[:, 0, (q - 1) % RING, s, HID:HID + 1])
                    last.then_inc(R.relu2, 1)
            over_units(act, unit)

        @block.vector
        def _(dve):
            def unit(t, q):
                par = q % 2
                u = t * 2 + par
                if runs(u, 2):
                    k = u - 2
                    at_least(dve, R.mm3, k + 1)
                    at_least(dve, R.mm4, k - RING + 1)
                    for s in range(2):
                        c = slice(SEG * s, SEG * s + SEG)
                        last = dve.tensor_scalar(act3[:, (q - 2) % RING, c], b3[par][:, c],
                                                 expert[:, 1, (q - 2) % RING, s, HID:HID + 1], 0.0, ALU.add, ALU.max)
                    last.then_inc(R.relu3, 1)
                if par == 0 and runs(u, 4):
                    at_least(dve, R.mm4, u - 2)
                    at_least(dve, R.turned, t - 2)
                    dve.scalar_tensor_tensor(final, b_final[:, :], m.vec[:, V_BO:V_BO + 1],
                                             h[:, bass.ds((t - 2) * NT, NT)], ALU.add, ALU.add).then_inc(R.final, 1)
                if par == 1 and runs(u, 5):
                    slot = q // 2
                    at_least(dve, R.turned, t - 1)
                    at_least(dve, stored[slot], (t - 2 - slot) * 16)
                    dve.tensor_copy(result[:, slot].rearrange("i p (s f) -> i p s f", f=FEAT),
                                    b_turned[:, :].rearrange("i (s p f) -> i p s f", p=HALF, f=FEAT)).then_inc(R.result, 1)
            over_units(dve, unit)

        @block.gpsimd
        def _(pool):
            def unit(t, q):
                par = q % 2
                u = t * 2 + par
                if runs(u, 0):
                    at_least(pool, R.relu3, u - RING + 1)
                    if not isinstance(u, int):
                        stand_apart(pool, m.apart)
                    for s in range(2):
                        e = pool.value_load(m.route[0:1, bass.ds(t * 2 + (par * SEGS // 2 + s), 1)],
                                            min_val=0, max_val=EXPERTS)
                        pool.tensor_copy(expert[:, :, q, s, :],
                                         m.experts[:, :, bass.ds(e, 1), :].rearrange("p l a c -> p l (a c)"))\
                            .then_inc(R.expert, 1)
            over_units(pool, unit)

        @block.sync
        def _(sp):
            def unit(t, q):
                if q % 2 == 1 and runs(t * 2 + 1, 5):
                    slot = q // 2
                    at_least(sp, R.result, t - 1)
                    stand_apart(sp, m.apart)
                    for p in range(HALF):
                        sp.dma_start(out[bass.ds((t - 2) * NT + p * BROWS * COLS, NT), :]
                                     .rearrange("(i s) f -> i (s f)", s=4), result[:, slot, p]).then_inc(stored[slot], 16)
            over_units(sp, unit)
            for slot in range(2):
                sp.wait_ge(stored[slot], TILES * 16)


_INS = ["x", "L0_tok_qkv_w", "L0_tok_qkv_b", "L0_tok_proj_w", "L0_tok_proj_b", "L0_attn_in_W", "L0_attn_in_b",
        "L0_attn_A_W", "L0_attn_B_W", "L0_attn_B_b", "L0_attn_C_W", "L0_attn_C_b", "L0_attn_D_W", "L0_attn_D_b",
        "L0_attn_ln_w", "L0_attn_ln_b", "L0_attn_out_W", "L0_attn_out_b", "L0_ffn_route_id", "L0_ffn_Wi",
        "L0_ffn_bi", "L0_ffn_Wr", "L0_ffn_br", "L0_ffn_Ws", "L0_ffn_bs", "L0_ffn_Wo", "L0_ffn_bo"]


def kernel(**inputs):
    import concourse.bacc as _bacc
    from concourse.bass_utils import run_bass_kernel_spmd as _run

    nc = _bacc.Bacc("TRN2", target_bir_lowering=False, num_devices=1)
    arrays, a = {}, {}
    for name in _INS:
        v = np.ascontiguousarray(inputs[name])
        arrays["in_" + name] = v
        a[name] = nc.dram_tensor("in_" + name, v.shape, mybir.dt.from_np(v.dtype), kind="ExternalInput").ap()
    c = shape_constants()
    arrays["in_consts"] = c
    a["consts"] = nc.dram_tensor("in_consts", c.shape, mybir.dt.float32, kind="ExternalInput").ap()
    out = nc.dram_tensor("out", (BATCH, ROWS * COLS, FEAT), mybir.dt.float32, kind="ExternalOutput").ap()
    program(nc, a, out)
    r = _run(nc, [arrays], core_ids=[0])
    return r.results[0]["out"]
```

```python
import numpy as np
import concourse.bass as bass
from concourse import mybir
from contextlib import ExitStack


class Names:
    pass


BATCH, ROWS, COLS, FEAT = 4, 64, 64, 64
HALF = 2
BROWS = (BATCH // HALF) * ROWS
WIN = 8
NPOS = WIN * WIN
HEADS, HD = 8, 8
PAIRS = (BROWS // WIN) * (COLS // WIN)
TILES = BROWS // WIN
PPT = PAIRS // TILES
HID = 128
LAYERS = 2
EXPERTS = 16
CHUNKS = BATCH * ROWS
WARM = 24
TOL = 2.0 ** -20
SEGS = 64
SEG = BATCH * ROWS * COLS // SEGS
SEG_ROWS = SEG // COLS
EPS = 1e-5
NT = 512

C_IDENT, C_CENT64, C_MEAN64, C_CENT128, C_MEAN128 = (128 * n for n in range(5))
C_MASK = 640
C_COSQ = C_MASK + HEADS
C_SINQ, C_COSK, C_SINK = C_COSQ + 64, C_COSQ + 128, C_COSQ + 192
C_END = C_COSQ + 256


def shape_constants():
    c = np.zeros((128, C_END), np.float32)
    eye = np.eye(128, dtype=np.float32)
    bd = np.kron(np.eye(2), np.ones((64, 64))).astype(np.float32) / 64
    c[:, C_IDENT:C_IDENT + 128] = eye
    c[:, C_CENT64:C_CENT64 + 128] = eye - bd
    c[:, C_MEAN64:C_MEAN64 + 128] = bd
    c[:, C_CENT128:C_CENT128 + 128] = eye - 1.0 / 128
    c[:, C_MEAN128:C_MEAN128 + 128] = 1.0 / 128
    f = np.arange(128) % 64
    c[np.arange(128), C_MASK + f // HD] = 1.0
    half = HD // 2
    inv = (1.0 / np.float32(10000.0) ** (np.arange(0, half, 2, dtype=np.float32) / half)).astype(np.float32)
    pos = np.arange(NPOS)
    d = f % HD
    where = np.where((d // half)[:, None] == 0, (pos // WIN)[None, :], (pos % WIN)[None, :]).astype(np.float32)
    ang = where * inv[(d % half) // 2][:, None]
    cos, sin = np.cos(ang), np.sin(ang) * np.where(d % 2 == 0, -1.0, 1.0)[:, None]
    scale = HD ** -0.5
    c[:, C_COSQ:C_COSQ + 64] = cos * scale
    c[:, C_SINQ:C_SINQ + 64] = sin * scale
    c[:, C_COSK:C_COSK + 64] = cos
    c[:, C_SINK:C_SINK + 64] = sin
    return c


(W_Q, W_K, W_V, W_PROJ, W_FIN0, W_FIN1, W_OUT0, W_OUT1, W_FOUT, W_IN, W_A0, W_A1, W_B0, W_B1, W_C0, W_C1,
 W_D0, W_D1, W_S0, W_S1) = range(20)
NW = 20
(V_BQ, V_BK, V_BV, V_PROJ, V_IN, V_BB0, V_BB1, V_CB0, V_CB1, V_DB0, V_DB1, V_LW0, V_LW1, V_LB0, V_LB1,
 V_OUT, V_FI, V_BO, V_BS0, V_BS1, V_BR) = range(21)
NV = V_BR + LAYERS * EXPERTS
(D_PROJ, D_C0, D_C1, D_B1, D_OUT) = range(5)


def at_least(eng, sem, count):
    if isinstance(count, int) and count <= 0:
        return
    eng.wait_ge(sem, count)


def over_slots(eng, count, slot, before, after):
    for s in range(-before, 4):
        slot(s, s % 4)
    with eng.Fori(1, count // 4 - 1) as v:
        for q in range(4):
            slot(v * 4 + q, q)
    for s in range(count - 4, count + after):
        slot(s, s % 4)


def within(t, count):
    return not isinstance(t, int) or 0 <= t < count


def stand_apart(eng, sem):
    eng.sem_inc(sem, 1)


def program(nc, a, out):
    F32, I32 = mybir.dt.float32, mybir.dt.int32
    ctx = ExitStack()
    with ctx:
        def sb(name, shape, dt=F32):
            return ctx.enter_context(nc.sbuf_tensor(name, shape, dt))

        def sem(name):
            return ctx.enter_context(nc.semaphore(name))

        m = Names()
        m.nc, m.a, m.out, m.sem, m.F32, m.I32 = nc, a, out, sem, F32, I32
        m.ALU, m.ACT, m.AX = mybir.AluOpType, mybir.ActivationFunctionType, mybir.AxisListType
        m.apart = sem("apart")
        m.const = sb("const", [128, C_END])
        m.wt = sb("wt", [128, NW, 128])
        m.experts = sb("experts", [128, LAYERS, EXPERTS + 1, HID + 1])
        m.route = sb("route", [1, SEGS], I32)
        m.entry = sb("entry", [128, BATCH, ROWS + 1])
        m.vec = sb("vec", [128, 64])
        m.dvec = sb("dvec", [128, 12])
        m.eps = sb("eps", [128, 1])
        m.h = sb("h", [128, BROWS, COLS])
        m.big1 = sb("big1", [128, CHUNKS * COLS])
        m.big2 = sb("big2", [128, CHUNKS * COLS])
        m.bank = [ctx.enter_context(nc.psum_tensor(f"bank{n}", [128, NT], F32)) for n in range(8)]
        m.agree = sb("agree", [128, 1])
        m.ones = sb("ones", [128, 1])
        m.flag = sb("flag", [1, 1], I32)
        m.ring = sb("ring", [128, 2, NT])
        m.warm = m.ring[:, 0, :].rearrange("p (k n) -> p k n", n=CHUNKS)
        m.gap = m.ring[:, 1, 0:CHUNKS]
        m.mean_r = sb("mean_r", [128, 2, 128], mybir.dt.float32r)
        m.halves = sb("halves", [128, 2, 2, NT], mybir.dt.float32r)
        buffers = attention_buffers(m)
        prepare(m, buffers)
        window_attention(m, buffers)
        fold_weights(m)
        norm_and_project(m, "in")
        for layer in range(LAYERS):
            recurrence(m, layer)
            mix_and_norm(m, layer)
        norm_and_project(m, "ffn")
        routed_ffn(m)


def row_of(vector):
    return vector.rearrange("(a n) -> a n", a=1)


def prepare(m, B):
    a, sem = m.a, m.sem
    m.rows = m.ring[0:64, 0, 0:128]
    ident = m.const[:, C_IDENT:C_IDENT + 128]
    zeroed, const_in, attn_in, vec_in = (sem(n) for n in ("zeroed", "const_in", "attn_in", "vec_in"))
    turned, taken, small, small_out = (sem(n) for n in ("turned", "taken", "small", "small_out"))
    m.x_ready = [sem(f"at_x_ready{n}") for n in range(2)]

    with m.nc.Block() as block:
        @block.sync
        def _(sp):
            for t in range(2):
                load_x(m, B, sp, t, t)
            sp.wait_ge(zeroed, 2)
            for p in range(HALF):
                half = slice(64 * p, 64 * p + 64)
                sp.dma_start(m.wt[half, W_Q:W_V + 1, half], a["L0_tok_qkv_w"].rearrange("(n r) c -> r n c", n=3))\
                    .then_inc(attn_in, 16)
                sp.dma_start(m.wt[half, W_PROJ, half], a["L0_tok_proj_w"]).then_inc(attn_in, 16)
                sp.dma_start(m.rows[V_BQ:V_BV + 1, half], a["L0_tok_qkv_b"].rearrange("(n c) -> n c", n=3))\
                    .then_inc(vec_in, 16)
                sp.dma_start(m.rows[V_PROJ:V_PROJ + 1, half], row_of(a["L0_tok_proj_b"])).then_inc(vec_in, 16)

        @block.scalar
        def _(act):
            act.dma_start(m.const[:, :], a["consts"]).then_inc(const_in, 16)

        @block.gpsimd
        def _(pool):
            pool.memset(m.eps[:, :], EPS)
            pool.memset(m.ones[:, :], 1.0)

        @block.tensor
        def _(pe):
            pe.wait_ge(const_in, 16)
            pe.wait_ge(attn_in, 16 * 2 * HALF)
            for n, w in enumerate((W_Q, W_K, W_V, W_PROJ)):
                last = pe.transpose(m.bank[0][:, 128 * n:128 * n + 128], m.wt[:, w, :], ident)
            last.then_inc(turned, 1)
            pe.wait_ge(vec_in, 16 * 2 * HALF)
            pe.matmul(m.bank[2][:, 0:64], m.rows, ident[0:64, 0:64], start=True, stop=True).then_inc(small, 1)
            pe.wait_ge(taken, 1)
            pe.wait_ge(small_out, 1)
            product_sums(m, pe, m.bank[3], (D_PROJ,)).then_inc(small, 1)

        @block.vector
        def _(dve):
            dve.memset(m.wt[:, 0:W_IN, :], 0.0).then_inc(zeroed, 1)
            dve.memset(m.rows, 0.0).then_inc(zeroed, 1)
            dve.memset(m.entry[:, :, 0:1], 0.0)
            dve.memset(B.q_bd[:, :, :, :], 0.0)
            dve.memset(B.o_bd[:, :, :], 0.0)
            dve.memset(B.v_aug[:, :, :, :, :], 0.0).then_inc(zeroed, 1)
            dve.wait_ge(zeroed, 3)
            v_heads = B.v_aug.rearrange("p a b (c k) d -> p (a b) c k d", k=2)
            for k in range(2):
                dve.memset(v_heads[64 * k:64 * k + 64, :, :, k, HD], 1.0)
            dve.wait_ge(const_in, 16)
            for n, c in enumerate((C_MEAN64, C_MEAN128)):
                dve.tensor_copy(m.mean_r[:, n, :], m.const[:, c:c + 128])
            dve.wait_ge(turned, 1)
            dve.tensor_copy(m.wt[:, W_Q:W_PROJ + 1, :].rearrange("p n c -> p (n c)"), m.bank[0][:, :]).then_inc(taken, 1)
            dve.wait_ge(small, 1)
            dve.tensor_copy(m.vec[:, :], m.bank[2][:, 0:64]).then_inc(small_out, 1)
            dve.wait_ge(small, 2)
            dve.tensor_copy(m.dvec[:, D_PROJ:D_PROJ + 1], m.bank[3][:, D_PROJ:D_PROJ + 1])


def load_x(m, B, sp, t, par):
    for p in range(HALF):
        src = m.a["x"][2 * p:2 * p + 2].rearrange("b r c f -> (b r c) f")[bass.ds(t * NT, NT), :]
        sp.dma_start(B.x_tok[:, par, :, p, :], src.rearrange("(n q) f -> q n f", q=128)).then_inc(m.x_ready[par], 16)


def load_rest(m, sp):
    a = m.a
    m.rest_in, m.n_rest = m.sem("rest_in"), 0
    m.route_raw = m.ring[0:1, 1, 0:SEGS].bitcast(m.I32)

    def load(dst, src):
        sp.dma_start(dst, src).then_inc(m.rest_in, 16)
        m.n_rest += 16

    for p in range(HALF):
        half = slice(64 * p, 64 * p + 64)
        load(m.rows[V_OUT:V_OUT + 1, half], row_of(a["L0_attn_out_b"]))
        load(m.rows[V_BO:V_BO + 1, half], row_of(a["L0_ffn_bo"]))
        load(m.wt[:, W_IN, half], a["L0_attn_in_W"])
        load(m.wt[:, W_FIN0 + p, half], a["L0_ffn_Wi"])
        load(m.wt[half, W_OUT0 + p, :], a["L0_attn_out_W"])
    load(m.wt[0:FEAT, W_FOUT, :], a["L0_ffn_Wo"])
    for slot, name in ((W_A0, "A_W"), (W_B0, "B_W"), (W_C0, "C_W"), (W_D0, "D_W")):
        load(m.wt[:, slot:slot + LAYERS, :], a["L0_attn_" + name].rearrange("l h d -> h l d"))
    load(m.wt[:, W_S0:W_S0 + LAYERS, :], a["L0_ffn_Ws"].rearrange("l s h d -> h (l s) d"))
    for row, name in ((V_IN, "L0_attn_in_b"), (V_FI, "L0_ffn_bi")):
        load(m.rows[row:row + 1, :], row_of(a[name]))
    for row, name in ((V_BB0, "B_b"), (V_CB0, "C_b"), (V_DB0, "D_b"), (V_LW0, "ln_w"), (V_LB0, "ln_b")):
        load(m.rows[row:row + LAYERS, :], a["L0_attn_" + name])
    load(m.rows[V_BS0:V_BS0 + LAYERS, :], a["L0_ffn_bs"].rearrange("l s h -> (l s) h"))
    load(m.rows[V_BR:V_BR + LAYERS * EXPERTS, :], a["L0_ffn_br"].rearrange("l e h -> (l e) h"))
    load(m.route_raw, row_of(a["L0_ffn_route_id"]))


def fold_weights(m):
    sem, ALU, ACT = m.sem, m.ALU, m.ACT
    ident, cent = (m.const[:, c:c + 128] for c in (C_IDENT, C_CENT128))
    turned, weights, small, small_out = (sem("rest_" + n) for n in ("turned", "weights", "small", "small_out"))
    jobs = [(m.wt[:, n, :], ident, False) for n in range(W_FIN0, W_C0)]
    jobs += [(m.wt[:, n, :], cent, n >= W_D0) for n in range(W_C0, W_S0)]
    jobs += [(m.wt[:, n, :], ident, True) for n in (W_S0, W_S1)]
    NGW = len(jobs) // 4

    with m.nc.Block() as block:
        @block.tensor
        def _(pe):
            pe.wait_ge(m.rest_in, m.n_rest)
            pe.matmul(m.bank[NGW][:, 0:64], m.rows, ident[0:64, 0:64], start=True, stop=True).then_inc(small, 1)
            for g in range(NGW):
                for n, (w, mv, plus) in enumerate(jobs[4 * g:4 * g + 4]):
                    dst = m.bank[g][:, 128 * n:128 * n + 128]
                    if mv is ident and not plus:
                        last = pe.transpose(dst, w, ident)
                        continue
                    last = pe.matmul(dst, w, mv, start=True, stop=not plus)
                    if plus:
                        last = pe.matmul(dst, ident, mv, start=False, stop=True)
                last.then_inc(turned, 1)
            pe.wait_ge(small_out, 1)
            pe.wait_ge(weights, NGW)
            product_sums(m, pe, m.bank[NGW + 1], (D_C0, D_C1, D_B1, D_OUT)).then_inc(small, 1)

        @block.scalar
        def _(act):
            for g in range(NGW):
                act.wait_ge(turned, g + 1)
                at = W_FIN0 + 4 * g
                act.activation(m.wt[:, at:at + 4, :].rearrange("p n c -> p (n c)"), m.bank[g][:, :], ACT.Copy)\
                    .then_inc(weights, 1)

        @block.vector
        def _(dve):
            dve.wait_ge(small, 1)
            dve.tensor_copy(m.vec[:, :], m.bank[NGW][:, 0:64]).then_inc(small_out, 1)
            dve.wait_ge(small, 2)
            dve.tensor_copy(m.dvec[:, D_C0:D_OUT + 1], m.bank[NGW + 1][:, D_C0:D_OUT + 1])
            for slot, scale in ((W_B1, V_LW0), (W_D1, V_LW0), (W_OUT0, V_LW1), (W_OUT1, V_LW1)):
                dve.tensor_scalar(m.wt[:, slot, :], m.wt[:, slot, :], m.vec[:, scale:scale + 1], None, ALU.mult)


def prepare_experts(m, dve):
    ALU = m.ALU
    route = m.sem("route")
    route_f, valid, valid2 = (m.ring[0:1, 1, SEGS * n:SEGS * (n + 1)] for n in (1, 2, 3))
    dve.tensor_copy(route_f, m.route_raw).then_inc(route, 1)
    dve.wait_ge(route, 1)
    dve.tensor_scalar(valid, route_f, 0.0, None, ALU.is_ge).then_inc(route, 1)
    dve.tensor_scalar(valid2, route_f, float(EXPERTS), None, ALU.is_lt).then_inc(route, 1)
    dve.wait_ge(route, 3)
    dve.tensor_tensor(valid, valid, valid2, ALU.mult).then_inc(route, 1)
    dve.wait_ge(route, 4)
    dve.scalar_tensor_tensor(route_f, route_f, -float(EXPERTS), valid, ALU.add, ALU.mult).then_inc(route, 1)
    dve.wait_ge(route, 5)
    dve.tensor_scalar(m.route[:, :], route_f, float(EXPERTS), None, ALU.add).then_inc(route, 1)
    dve.wait_ge(route, 6)
    for l in range(LAYERS):
        shared = m.vec[:, V_BS0 + l:V_BS0 + l + 1]
        dve.tensor_scalar(m.experts[:, l, 0:EXPERTS, HID:HID + 1],
                          m.vec[:, V_BR + l * EXPERTS:V_BR + (l + 1) * EXPERTS].unsqueeze(2),
                          shared, None, ALU.add)
        dve.tensor_copy(m.experts[:, l, EXPERTS, HID:HID + 1], shared)
        dve.tensor_copy(m.experts[:, l, EXPERTS, 0:HID], m.wt[:, W_S0 + l, :])
        of_layer = m.experts[:, l, 0:EXPERTS, 0:HID]
        dve.tensor_tensor(of_layer, of_layer, m.wt[:, W_S0 + l, :].unsqueeze(1)
                          .broadcast_to([128, EXPERTS, 128]), ALU.add)


def product_sums(m, pe, bank, which):
    ident, cent = (m.const[:, c:c + 128] for c in (C_IDENT, C_CENT128))
    v = lambda n: m.vec[:, n:n + 1]
    w = lambda n: m.wt[:, n, :]
    sums = {D_PROJ: [(ident, v(V_PROJ)), (w(W_PROJ), v(V_BV))],
            D_C0: [(cent, v(V_CB0)), (cent, v(V_DB0))],
            D_C1: [(cent, v(V_CB1)), (cent, v(V_DB1)), (w(W_D1), v(V_LB0))],
            D_B1: [(ident, v(V_BB1)), (w(W_B1), v(V_LB0))],
            D_OUT: [(ident, v(V_OUT)), (w(W_OUT0), v(V_LB1)), (w(W_OUT1), v(V_LB1))]}
    for d in which:
        for k, (x, y) in enumerate(sums[d]):
            last = pe.matmul(bank[:, d:d + 1], x, y, start=(k == 0), stop=(k == len(sums[d]) - 1))
    return last


def attention_buffers(m):
    B = Names()
    B.x_tok = m.big1[:, 0:2 * NT].rearrange("p (s n h f) -> p s n h f", s=2, h=HALF, f=FEAT)
    cur = [0]

    def buf(*shape):
        n = int(np.prod(shape))
        v = m.big2[:, cur[0]:cur[0] + n]
        cur[0] += n
        assert cur[0] <= CHUNKS * COLS
        if len(shape) == 1:
            return v
        names = "abcde"[:len(shape)]
        return v.rearrange("p (" + " ".join(names) + ") -> p " + " ".join(names),
                           **{c: s for c, s in zip(names, shape)})

    B.x_now = buf(2, PPT, 2, NPOS)
    B.rot = buf(4, NT)
    B.q_bd = buf(2, PPT, 128)
    B.k_rot = buf(2, PPT, NPOS)
    B.k_mask = buf(4, HEADS, NPOS)
    B.shifted = buf(2, HEADS, NPOS)
    B.probs = buf(2, NT)
    B.probs_t = buf(2, 4, 128)
    B.v_aug = buf(2, PPT * HALF, HEADS, HD + 1)
    B.top = buf(2, HEADS)
    B.inv = buf(4, HEADS)
    B.o_bd = buf(PPT, 128)
    B.o_t = buf(NT)
    return B


def window_attention(m, B):
    nc, sem, ALU, ACT, AX = m.nc, m.sem, m.ALU, m.ACT, m.AX
    x_now, rot, q_bd, k_rot, k_mask, shifted = B.x_now, B.rot, B.q_bd, B.k_rot, B.k_mask, B.shifted
    probs, probs_t, v_aug, top, inv, o_bd, o_t = B.probs, B.probs_t, B.v_aug, B.top, B.inv, B.o_bd, B.o_t
    b_s, b_pt, b_o, b_h = m.bank[0:2], m.bank[2:4], m.bank[4:6], m.bank[7]
    first_banks = (m.bank[6], b_s[0], b_o[1], b_h)
    bo_psum = [b[:, :].rearrange("p (n s) -> p n s", s=256) for b in b_o]
    cst = lambda c, n: m.const[:, c:c + n]
    table = lambda c: cst(c, NPOS).unsqueeze(1).broadcast_to([128, PPT, NPOS])

    x_ready = m.x_ready
    experts_in = [sem(f"experts_in{l}") for l in range(LAYERS)]
    S = Names()
    S.turned, S.added = sem("at_experts_turned"), sem("at_experts_added")
    S.x_turned, S.x_placed, S.x_placed_too = (sem("at_" + n) for n in ("x_turned", "x_placed", "x_placed_too"))
    b_e = (*b_s, m.bank[6])
    fours = [(l, e) for l in range(LAYERS) for e in range(0, EXPERTS, 4)]
    S.x_mm, S.copied, S.v_copied = (sem("at_" + n) for n in ("x_mm", "copied", "v_copied"))
    S.swapped, S.sin_done, S.cos_done, S.first_cos = (sem("at_" + n) for n in ("swapped", "sin_done", "cos_done", "first_cos"))
    S.q_ready, S.krot, S.kmask, S.scores, S.maxed = (sem("at_" + n) for n in ("q_ready", "krot", "kmask", "scores", "maxed"))
    S.shifted, S.probs, S.pt, S.pt_copied, S.av = (sem("at_" + n) for n in ("shifted", "probs", "pt", "pt_copied", "av"))
    S.inv, S.normed, S.ot, S.ot_copied, S.proj = (sem("at_" + n) for n in ("inv", "normed", "ot", "ot_copied", "proj"))
    S.h = sem("at_h")

    def over_tiles(eng, tile):
        tile(0, 0, "first")
        tile(1, 1, "mid")
        tile(2, 0, "mid")
        with eng.Fori(1, (TILES - 2) // 2) as u:
            tile(u * 2 + 1, 1, "mid")
            tile(u * 2 + 2, 0, "mid")
        tile(TILES - 1, (TILES - 1) % 2, "last")
        tile(TILES, TILES % 2, "drain")

    def flags(kind):
        return kind != "drain", kind in ("first", "mid"), kind != "first"

    with nc.Block() as block:
        @block.tensor
        def _(pe):
            def turn_x(t, par):
                at_least(pe, x_ready[par], (t - par) * 16 + 32)
                if isinstance(t, int) and t == 1:
                    pe.wait_ge(S.v_copied, 4)
                at_least(pe, S.h, t - 2)
                for n in range(4):
                    last = pe.transpose(b_h[:, 128 * n:128 * n + 128],
                                        B.x_tok[:, par, n, :, :].rearrange("p h f -> p (h f)"), cst(C_IDENT, 128))
                last.then_inc(S.x_turned, 1)

            def product(t, par, n):
                first = isinstance(t, int) and t == 0
                b_x = first_banks[n] if first else m.bank[6]
                if n == 0:
                    at_least(pe, S.x_placed, t + 1)
                if n == 2:
                    at_least(pe, S.x_placed_too, t + 1)
                if not first:
                    if n == 0:
                        at_least(pe, S.v_copied, t * 4)
                    elif n < 3:
                        at_least(pe, S.copied, t * 2 + n)
                    else:
                        at_least(pe, S.v_copied, t * 4 + 2)
                if n < 2:
                    pe.matmul(b_x[:, :], m.wt[:, (W_Q, W_K)[n], :], x_now[:, par, :, 0, :],
                              start=True, stop=True).then_inc(S.x_mm, 1)
                else:
                    for k in range(4):
                        pr = 4 * (n - 2) + k
                        tok = x_now[:, par, pr, :, :].rearrange("p a n -> p (a n)")
                        last = pe.matmul(b_x[:, 128 * k:128 * k + 128], tok, m.wt[:, W_V, :], start=True, stop=True)
                    last.then_inc(S.x_mm, 1)

            def scores(i, par, j):
                at_least(pe, S.kmask, i + 1)
                at_least(pe, S.shifted, i - 1)
                pe.matmul(b_s[j % 2][:, :], q_bd[:, par, j, :], k_mask[:, j % 4].rearrange("p h n -> p (h n)"),
                          start=True, stop=True).then_inc(S.scores, 1)

            def turn_experts(groups):
                for g in groups:
                    l, e = fours[g]
                    if g < 3:
                        pe.wait_ge(*((S.shifted, PAIRS) if g < 2 else (S.v_copied, 4 * TILES)))
                    else:
                        pe.wait_ge(S.added, g - 2)
                    pe.wait_ge(experts_in[l], 16)
                    for n in range(4):
                        last = pe.transpose(b_e[g % 3][:, 128 * n:128 * n + 128], m.experts[:, l, e + n, 0:HID],
                                            cst(C_IDENT, 128))
                    last.then_inc(S.turned, 1)

            def tile(t, par, kind):
                now, nxt, prev = flags(kind)
                for j in range(PPT):
                    i = t * PPT + j
                    if kind == "drain" and j in (3, 5):
                        turn_experts(range(3) if j == 3 else range(3, len(fours)))
                    if now and j < PPT - 1:
                        scores(i + 1, par, j + 1)
                    if nxt and j == PPT - 1:
                        at_least(pe, S.q_ready, t * 2 + 4)
                        scores(i + 1, 1 - par, 0)
                    if prev and j in (3, 4):
                        at_least(pe, S.normed, t * 8 + 4 * (j - 4))
                        if j == 3:
                            at_least(pe, S.h, t - 1)
                        else:
                            at_least(pe, S.ot_copied, t * 4 - 2)
                        for n in range(4):
                            last = pe.transpose(b_h[:, 128 * n:128 * n + 128], o_bd[:, 4 * (j - 3) + n, :],
                                                cst(C_IDENT, 128))
                        last.then_inc(S.ot, 1)
                    if (now and j >= 1) or (prev and j < 1):
                        at_least(pe, S.probs, i)
                        at_least(pe, S.pt_copied, i - 2)
                        for c in range(4):
                            last = pe.transpose(b_pt[(j + 1) % 2][:, 128 * c:128 * c + 128],
                                                probs[:, (j + 1) % 2, 128 * c:128 * c + 128], cst(C_IDENT, 128))
                        last.then_inc(S.pt, 1)
                    if (now and j >= 2) or (prev and j < 2):
                        jj = (j - 2) % PPT
                        vpar = par if j >= 2 else 1 - par
                        at_least(pe, S.pt_copied, i - 1)
                        if jj % 4 == 0:
                            at_least(pe, S.v_copied, (t * 4 if j >= 2 else t * 4 - 4) + 2 * (jj // 4 + 1))
                        if jj % 2 == 0:
                            at_least(pe, S.normed, (t * 8 if j >= 2 else t * 8 - 8) + jj - 2)
                        dst = bo_psum[(jj % 4) // 2][:, jj % 2, 0:144].rearrange("p (h k d) -> p h k d", h=HALF, k=4)
                        for c in range(4):
                            last = pe.matmul(dst[:, :, c, :], probs_t[:, j % 2, c, :],
                                             v_aug[:, vpar, HALF * jj:HALF * jj + 2, 2 * c:2 * c + 2, :]
                                             .rearrange("p a h d -> p a (h d)"), start=True, stop=True)
                        last.then_inc(S.av, 1)
                    if prev and j == 6:
                        at_least(pe, S.ot_copied, t * 4)
                        pe.matmul(b_h[:, :], m.wt[:, W_PROJ, :], o_t, start=True, stop=True).then_inc(S.proj, 1)
                    if nxt and j == 0:
                        turn_x(t + 1, 1 - par)
                    if nxt and j in (1, 2, 4, 5):
                        product(t + 1, 1 - par, (1, 2, 4, 5).index(j))

            turn_x(0, 0)
            for n in range(4):
                product(0, 0, n)
            at_least(pe, S.q_ready, 2)
            scores(0, 0, 0)
            over_tiles(pe, tile)

        @block.vector
        def _(dve):
            def place_x(t, par):
                dve.wait_ge(S.x_turned, t + 1)
                dve.tensor_copy(x_now[:, par, :, 0, :].rearrange("p w (i j) -> p w i j", j=WIN),
                                b_h[:, :].rearrange("p (i w j) -> p w i j", w=PPT, j=WIN)).then_inc(S.x_placed, 1)

            def sin_term(t, n):
                dve.wait_ge(S.copied, t * 2 + n + 1)
                stand_apart(dve, m.apart)
                dve.stream_shuffle(rot[:, 2 * n + 1, :], rot[:, 2 * n, :], [f ^ 1 for f in range(32)])\
                    .then_inc(S.swapped, 1)
                dve.wait_ge(S.swapped, t * 2 + n + 1)
                term = rot[:, 2 * n + 1, :].rearrange("p (w n) -> p w n", n=NPOS)
                dve.tensor_tensor(term, term, table((C_SINQ, C_SINK)[n]), ALU.mult).then_inc(S.sin_done, 1)

            def tile(t, par, kind):
                now, nxt, prev = flags(kind)
                for j in range(PPT):
                    i = t * PPT + j
                    if now:
                        at_least(dve, S.scores, i + 1)
                        at_least(dve, S.shifted, i - 1)
                        sc = b_s[j % 2][:, :].rearrange("p (h n) -> p h n", n=NPOS)
                        dve.tensor_reduce(top[:, j % 2, :], sc, AX.X, ALU.max).then_inc(S.maxed, 1)
                        dve.wait_ge(S.maxed, i + 1)
                        at_least(dve, S.probs, i - 1)
                        dve.tensor_tensor(shifted[:, j % 2], sc, top[:, j % 2, :].unsqueeze(2)
                                          .broadcast_to([128, HEADS, NPOS]), ALU.subtract).then_inc(S.shifted, 1)
                    if (now and j in (4, 6)) or (prev and j in (0, 2)):
                        jj = (j - 4) % PPT
                        b = (jj // 2) % 2
                        n0 = t * 8 + (j - 4)
                        at_least(dve, S.av, i - 2)
                        if jj == 0:
                            at_least(dve, S.ot, t * 2)
                        halves = [(slice(64 * p, 64 * p + 64), slice(72 * p, 72 * p + 72)) for p in range(HALF)]
                        outs = [bo_psum[b][s, :, c].rearrange("p n (h d) -> p n h d", d=HD + 1) for s, c in halves]
                        for p, (s, c) in enumerate(halves):
                            dve.reciprocal(inv[s, 2 * b:2 * b + 2, :], outs[p][:, :, :, HD]).then_inc(S.inv, 1)
                        for p, (s, c) in enumerate(halves):
                            dve.wait_ge(S.inv, n0 + 1 + p)
                            dve.tensor_tensor(
                                o_bd[s, jj:jj + 2, 64 * p:64 * p + 64].rearrange("p n (h d) -> p n h d", d=HD),
                                outs[p][:, :, :, 0:HD],
                                inv[s, 2 * b:2 * b + 2, :].unsqueeze(3).broadcast_to([64, 2, HEADS, HD]),
                                ALU.mult).then_inc(S.normed, 1)
                    if nxt and j == 0:
                        place_x(t + 1, 1 - par)
                    if nxt and j in (2, 3):
                        sin_term(t + 1, j - 2)
                    if kind == "drain" and j == 3:
                        for g, (l, e) in enumerate(fours):
                            dve.wait_ge(S.turned, g + 1)
                            dve.tensor_copy(m.experts[:, l, e:e + 4, 0:HID],
                                            b_e[g % 3][:, :].rearrange("p (n c) -> p n c", c=128)).then_inc(S.added, 1)

            place_x(0, 0)
            for n in range(2):
                sin_term(0, n)
            term = rot[:, 2, :].rearrange("p (w n) -> p w n", n=NPOS)
            dve.tensor_tensor(term, term, table(C_COSK), ALU.mult).then_inc(S.first_cos, 1)
            dve.wait_ge(S.sin_done, 2)
            dve.wait_ge(S.first_cos, 1)
            dve.tensor_tensor(k_rot[:, 0].rearrange("p w n -> p (w n)"), rot[:, 2, :], rot[:, 3, :], ALU.add)\
                .then_inc(S.krot, 1)
            over_tiles(dve, tile)

        @block.scalar
        def _(act):
            def place_x(t, par):
                act.wait_ge(S.x_placed, t + 1)
                act.activation(x_now[:, par, :, 1, :], x_now[:, par, :, 0, :], ACT.Copy).then_inc(S.x_placed_too, 1)

            def qk_copy(t, n):
                b_x = first_banks[n] if isinstance(t, int) and t == 0 else m.bank[6]
                at_least(act, S.x_mm, t * 4 + 1 + n)
                at_least(act, S.krot if n else S.q_ready, t if n else t * 2)
                act.activation(rot[:, 2 * n, :], b_x[:, :], ACT.Identity, bias=m.vec[:, V_BQ + n:V_BQ + n + 1])\
                    .then_inc(S.copied, 1)

            def v_copy(t, par, n):
                at_least(act, S.x_mm, t * 4 + 3 + n)
                b_x = first_banks[2 + n] if isinstance(t, int) and t == 0 else m.bank[6]
                at_least(act, S.av, t * PPT - PPT)
                src = b_x[:, :].rearrange("p (a c k d) -> p a c k d", a=8, c=4, k=2)
                dst = v_aug[:, par, 8 * n:8 * n + 8, :, :].rearrange("p a (c k) d -> p a c k d", k=2)
                for k in range(2):
                    s = slice(64 * k, 64 * k + 64)
                    act.activation(dst[s, :, :, k, 0:HD], src[s, :, :, k, :], ACT.Copy).then_inc(S.v_copied, 1)

            def tile(t, par, kind):
                now, nxt, prev = flags(kind)
                for j in range(PPT):
                    i = t * PPT + j
                    if now:
                        at_least(act, S.shifted, i + 1)
                        at_least(act, S.pt, i - 1)
                        act.activation(probs[:, j % 2, :], shifted[:, j % 2].rearrange("p h n -> p (h n)"),
                                       ACT.Exp).then_inc(S.probs, 1)
                    if (now and j >= 1) or (prev and j < 1):
                        at_least(act, S.pt, i)
                        at_least(act, S.av, i - 2)
                        act.activation(probs_t[:, (j + 1) % 2].rearrange("p c n -> p (c n)"),
                                       b_pt[(j + 1) % 2][:, :], ACT.Copy).then_inc(S.pt_copied, 1)
                    if nxt and j == 0:
                        place_x(t + 1, 1 - par)
                    if nxt and j in (1, 2):
                        qk_copy(t + 1, j - 1)
                    if nxt and j in (4, 5):
                        v_copy(t + 1, 1 - par, j - 4)
                    if prev and j in (3, 5):
                        four = j // 4
                        at_least(act, S.ot, t * 2 - 1 + four)
                        at_least(act, S.proj, t - 1)
                        for p in range(HALF):
                            half = slice(64 * p, 64 * p + 64)
                            act.activation(o_t[half, 4 * NPOS * four:4 * NPOS * (four + 1)].rearrange("p (n q) -> p n q", q=NPOS),
                                           b_h[half, :].rearrange("p (n q) -> p n q", q=128)[:, :, half], ACT.Copy)\
                                .then_inc(S.ot_copied, 1)
                    if prev and j == 7:
                        at_least(act, S.proj, t)
                        act.activation(m.h[:, bass.ds(t * WIN - WIN, WIN), :].rearrange("p i (w j) -> p w i j", j=WIN),
                                       b_h[:, :].rearrange("p (w i j) -> p w i j", w=WIN, j=WIN),
                                       ACT.Identity, bias=m.dvec[:, D_PROJ:D_PROJ + 1]).then_inc(S.h, 1)

            place_x(0, 0)
            for n in range(2):
                qk_copy(0, n)
            for n in range(2):
                v_copy(0, 0, n)
            over_tiles(act, tile)

        @block.gpsimd
        def _(pool):
            def mask(i, par, jj):
                at_least(pool, S.scores, i - 3)
                pool.tensor_tensor(k_mask[:, jj % 4], k_rot[:, par, jj, :].unsqueeze(1).broadcast_to([128, HEADS, NPOS]),
                                   cst(C_MASK, HEADS).unsqueeze(2).broadcast_to([128, HEADS, NPOS]),
                                   ALU.mult).then_inc(S.kmask, 1)

            def cos_term(t, n):
                pool.wait_ge(S.swapped, t * 2 + n + 1)
                term = rot[:, 2 * n, :].rearrange("p (w n) -> p w n", n=NPOS)
                pool.tensor_tensor(term, term, table((C_COSQ, C_COSK)[n]), ALU.mult).then_inc(S.cos_done, 1)

            def add_q(t, par):
                at_least(pool, S.cos_done, 1 if isinstance(t, int) and t == 0 else t * 2)
                pool.wait_ge(S.sin_done, t * 2 + 1)
                at_least(pool, S.scores, t * PPT - PPT)
                at_least(pool, S.kmask, t * PPT - 2)
                for p in range(HALF):
                    s = slice(64 * p, 64 * p + 64)
                    at_least(pool, S.q_ready, t * 2 + p)
                    pool.tensor_tensor(q_bd[s, par, :, 64 * p:64 * p + 64],
                                       rot[s, 0, :].rearrange("p (w n) -> p w n", n=NPOS),
                                       rot[s, 1, :].rearrange("p (w n) -> p w n", n=NPOS), ALU.add).then_inc(S.q_ready, 1)
                at_least(pool, S.q_ready, t * 2 + 2)

            def add_k(t, par):
                pool.wait_ge(S.cos_done, t * 2 + 1)
                pool.wait_ge(S.sin_done, t * 2 + 2)
                at_least(pool, S.kmask, t * PPT - PPT)
                pool.tensor_tensor(k_rot[:, par].rearrange("p w n -> p (w n)"), rot[:, 2, :], rot[:, 3, :],
                                   ALU.add).then_inc(S.krot, 1)
                pool.wait_ge(S.krot, t + 1)

            def tile(t, par, kind):
                now, nxt, prev = flags(kind)
                for j in range(PPT):
                    i = t * PPT + j
                    if nxt and j == 3:
                        cos_term(t + 1, 0)
                        add_q(t + 1, 1 - par)
                    if nxt and j == PPT - 3:
                        cos_term(t + 1, 1)
                        add_k(t + 1, 1 - par)
                    if now and j < PPT - 3:
                        mask(i + 3, par, j + 3)
                    elif nxt:
                        mask(i + 3, 1 - par, j + 3 - PPT)

            cos_term(0, 0)
            add_q(0, 0)
            pool.wait_ge(S.krot, 1)
            for jj in range(3):
                mask(jj, 0, jj)
            over_tiles(pool, tile)

        @block.sync
        def _(sp):
            load_rest(m, sp)
            for l in range(LAYERS):
                sp.dma_start(m.experts[:, l, 0:EXPERTS, 0:HID], m.a["L0_ffn_Wr"][l].rearrange("e h d -> h e d"))\
                    .then_inc(experts_in[l], 16)
            with sp.Fori(1, TILES // 2) as k:
                for par in range(2):
                    t = k * 2 + par
                    sp.wait_ge(S.x_turned, t - 1)
                    stand_apart(sp, m.apart)
                    load_x(m, B, sp, t, par)


def mean_product(m, pe, bank, which, slot):
    for n in range(2):
        last = pe.matmul(bank, m.mean_r[:, which, :], m.halves[:, n, slot, :], start=(n == 0), stop=(n == 1))
    return last


def norm_and_project(m, kind):
    sem, ALU, ACT = m.sem, m.ALU, m.ACT
    m.x1 = m.big1[:, :].rearrange("p (c n) -> p c n", n=CHUNKS)
    m.y = m.big2[:, CHUNKS * COLS - BROWS * COLS:]
    h = m.h[:, :, :].rearrange("p r c -> p (r c)")
    buf = m.big2[:, 0:6 * NT].rearrange("p (n c) -> p n c", c=NT)
    square, rstd, u = buf[:, 0:2], buf[:, 2:4], buf[:, 4:6]
    N = Names()
    N.centred, N.squared, N.variance, N.log, N.rstd = (sem(f"{kind}_" + n) for n in ("centred", "squared", "variance", "log", "rstd"))
    N.scaled, N.product, N.copied0, N.copied1 = (sem(f"{kind}_" + n) for n in ("scaled", "product", "copied0", "copied1"))
    N.summed, N.added, N.rounded, N.rest = (sem(f"{kind}_" + n) for n in ("summed", "added", "rounded", "rest"))
    b_c, b_v, b_x = m.bank[0:4], m.bank[4:6], m.bank[6:8]
    w = lambda c: m.const[:, c:c + 128]
    project, add = kind == "in", kind == "ffn"

    def over_tiles(eng, slot):
        over_slots(eng, TILES, slot, 3 if add else 2, 1 if project else 0)

    with m.nc.Block() as block:
        @block.tensor
        def _(pe):
            def out_product(t, q):
                at_least(pe, N.added, t - 1)
                for p in range(HALF):
                    last = pe.matmul(b_x[q % 2][:, :], m.wt[:, W_OUT0 + p, :],
                                     m.x1[:, :, bass.ds(t * WIN + p * BROWS, WIN)],
                                     start=(p == 0), stop=(p == HALF - 1))
                last.then_inc(N.summed, 1)

            def centre(t, q):
                if add:
                    at_least(pe, N.added, t + 1)
                at_least(pe, N.scaled, t - 3)
                pe.matmul(b_c[q][:, :], w(C_CENT64), h[:, bass.ds(t * NT, NT)], start=True, stop=True)\
                    .then_inc(N.centred, 1)

            def variance(t, q):
                at_least(pe, N.rest, t + 1)
                at_least(pe, N.log, t - 1)
                mean_product(m, pe, b_v[q % 2][:, :], 0, q % 2).then_inc(N.variance, 1)

            def in_product(t, q):
                at_least(pe, N.scaled, t + 1)
                at_least(pe, N.copied0, t)
                at_least(pe, N.copied1, t)
                for p in range(HALF):
                    half = slice(64 * p, 64 * p + 64)
                    pe.matmul(b_x[p][:, :], m.wt[half, W_IN, :], u[half, q % 2, :], start=True, stop=True)\
                        .then_inc(N.product, 1)

            def slot(s, q):
                if within(s, TILES):
                    variance(s, q)
                if add and within(s + 3, TILES):
                    out_product(s + 3, (q + 3) % 4)
                if within(s + 2, TILES):
                    centre(s + 2, (q + 2) % 4)
                if project and within(s - 1, TILES):
                    in_product(s - 1, (q - 1) % 4)
            over_tiles(pe, slot)

        def copy_in(t, p):
            return (m.x1[:, :, bass.ds(t * WIN + p * BROWS, WIN)].rearrange("p c i -> p i c"),
                    b_x[p][:, :].rearrange("p (i c) -> p i c", c=COLS))

        @block.scalar
        def _(act):
            def slot(s, q):
                if within(s, TILES):
                    at_least(act, N.variance, s + 1)
                    at_least(act, N.scaled, s - 1)
                    act.activation(rstd[:, q % 2, :], b_v[q % 2][:, :], ACT.Ln, bias=m.eps[:, :]).then_inc(N.log, 1)
                    act.wait_ge(N.log, s + 1)
                    act.activation(rstd[:, q % 2, :], rstd[:, q % 2, :], ACT.Exp, scale=-0.5).then_inc(N.rstd, 1)
                if within(s + 2, TILES):
                    at_least(act, N.centred, s + 3)
                    at_least(act, N.rest, s + 1)
                    act.activation(square[:, q % 2, :], b_c[(q + 2) % 4][:, :], ACT.Square).then_inc(N.squared, 1)
                if project and within(s - 1, TILES):
                    at_least(act, N.product, s * 2 - 1)
                    dst, src = copy_in(s - 1, 0)
                    act.activation(dst, src, ACT.Identity, bias=m.vec[:, V_IN:V_IN + 1]).then_inc(N.copied0, 1)

            act.preload_act_table_set("natural_log_exp_and_others")
            over_tiles(act, slot)

        @block.vector
        def _(dve):
            def slot(s, q):
                if within(s + 1, TILES):
                    at_least(dve, N.squared, s + 2)
                    at_least(dve, N.variance, s)
                    q1 = (q + 1) % 2
                    dve.tensor_copy(m.halves[:, 0, q1, :], square[:, q1, :]).then_inc(N.rounded, 1)
                    at_least(dve, N.rounded, s + 2)
                    dve.tensor_tensor(m.halves[:, 1, q1, :], square[:, q1, :], m.halves[:, 0, q1, :].bitcast(m.F32),
                                      ALU.subtract).then_inc(N.rest, 1)
                if within(s, TILES):
                    at_least(dve, N.rstd, s + 1)
                    if project:
                        at_least(dve, N.product, s * 2 - 2)
                    dst = u[:, q % 2, :] if project else m.y[:, bass.ds(s * NT, NT)]
                    dve.tensor_tensor(dst, b_c[q][:, :], rstd[:, q % 2, :], ALU.mult).then_inc(N.scaled, 1)
                if add and within(s + 3, TILES):
                    at_least(dve, N.summed, s + 4)
                    tile = m.h[:, bass.ds((s + 3) * WIN, WIN), :].rearrange("p i c -> p c i")
                    dve.scalar_tensor_tensor(tile, b_x[(q + 1) % 2][:, :].rearrange("p (c i) -> p c i", i=WIN),
                                             m.dvec[:, D_OUT:D_OUT + 1], tile, ALU.add, ALU.add).then_inc(N.added, 1)
                if project and within(s - 1, TILES):
                    at_least(dve, N.product, s * 2)
                    dst, src = copy_in(s - 1, 1)
                    dve.tensor_scalar(dst, src, m.vec[:, V_IN:V_IN + 1], None, ALU.add).then_inc(N.copied1, 1)
            over_tiles(dve, slot)


def recurrence(m, layer):
    sem, ALU, ACT = m.sem, m.ALU, m.ACT
    x1 = m.x1
    hs = m.hs = m.big2[:, :].rearrange("p (c n) -> p c n", n=CHUNKS)
    GROUPS, GB = 2, BATCH // 2
    GC = CHUNKS // GROUPS
    w_a, w_b = m.wt[:, W_A0 + layer, :], m.wt[:, W_B0 + layer, :]
    bias = m.vec[:, V_BB0:V_BB0 + 1] if layer == 0 else m.dvec[:, D_B1:D_B1 + 1]
    cols = [slice(GC * g, GC * g + GC) for g in range(GROUPS)]
    bank = [[m.bank[2 * g + k][:, 0:GC] for k in range(2)] for g in range(GROUPS)]
    T = f"l{layer}_"
    summed = [sem(T + f"summed{g}") for g in range(GROUPS)]
    stepped = [sem(T + f"stepped{g}") for g in range(GROUPS)]
    again_summed = [sem(T + f"again_summed{g}") for g in range(GROUPS)]
    again_stepped = [sem(T + f"again_stepped{g}") for g in range(GROUPS)]
    cleared, compared, counted = (sem(T + n) for n in ("cleared", "compared", "counted"))
    warm = [m.warm[:, k, :] for k in range(2)]
    entry = [m.entry[:, GB * g:GB * g + GB, 0:ROWS] for g in range(GROUPS)]
    ending = [m.entry[:, GB * g:GB * g + GB, 1:ROWS + 1] for g in range(GROUPS)]
    by_row = lambda v: v.rearrange("p (b r) -> p b r", r=ROWS)
    MAIN = COLS + 1

    with m.nc.Block() as block:
        @block.vector
        def _(dve):
            dve.memset(warm[1], 0.0).then_inc(cleared, 1)
            if layer == 0:
                prepare_experts(m, dve)
            for g in range(GROUPS):
                dve.wait_ge(stepped[g], WARM + MAIN)
                dve.tensor_tensor(by_row(m.gap[:, cols[g]]), by_row(hs[:, COLS - 1, cols[g]]), ending[g],
                                  ALU.subtract).then_inc(compared, 1)
            dve.wait_ge(compared, GROUPS)
            dve.tensor_tensor(m.gap, m.gap, m.gap, ALU.mult).then_inc(compared, 1)
            dve.wait_ge(compared, GROUPS + 1)
            dve.tensor_scalar(m.gap, m.gap, TOL * TOL, None, ALU.is_le).then_inc(compared, 1)
            dve.wait_ge(compared, GROUPS + 2)
            dve.tensor_reduce(m.agree[:, :], m.gap.rearrange("p (b r) -> p b r", r=ROWS)[:, :, 0:ROWS - 1],
                              m.AX.XY, ALU.min).then_inc(compared, 1)
            dve.wait_ge(counted, 1)
            dve.tensor_copy(m.flag[:, :], m.bank[7][0:1, 0:1])

        def step_a(pe, g, k, state, done, ready, count):
            pe.wait_ge(ready[g], count)
            pe.matmul(bank[g][k % 2], w_a, state, start=False, stop=True).then_inc(done[g], 1)

        def step_b(pe, g, par, c):
            x = x1[:, c, cols[g]] if isinstance(c, int) else \
                x1[:, bass.ds(c, 1), cols[g]].rearrange("p a n -> p (a n)")
            pe.matmul(bank[g][par], w_b, x, start=True, stop=False)

        def state_at(c, g):
            return hs[:, c, cols[g]] if isinstance(c, int) else \
                hs[:, bass.ds(c, 1), cols[g]].rearrange("p a n -> p (a n)")

        def over_steps(pe, count, step):
            with pe.Fori(0, count // 4) as u:
                for k in range(1, 5):
                    step(u * 4 + k, k % 2)
            for k in range(count - count % 4 + 1, count + 1):
                step(k, k % 2)

        def main_pass(pe, done, ready, base):
            def step(k, par):
                for g in range(GROUPS):
                    step_a(pe, g, par, state_at(k - 1, g), done, ready, k + (base + 1))
                    step_b(pe, g, 1 - par, k + 1)

            for g in range(GROUPS):
                step_a(pe, g, 0, entry[g], done, ready, base + 1)
                step_b(pe, g, 1, 1)
            over_steps(pe, COLS - 2, step)
            for g in range(GROUPS):
                step_a(pe, g, COLS - 1, state_at(COLS - 2, g), done, ready, base + COLS)

        def main_states(act, done, ready, base):
            def step(k, par):
                for g in range(GROUPS):
                    act.wait_ge(done[g], base + 1 + k if isinstance(k, int) else k + (base + 1))
                    act.activation(state_at(k, g), bank[g][par], ACT.Tanh, bias=bias).then_inc(ready[g], 1)
            with act.Fori(0, COLS // 4) as u:
                for k in range(4):
                    step(u * 4 + k, k % 2)

        @block.tensor
        def _(pe):
            C0 = COLS - WARM
            pe.wait_ge(cleared, 1)
            for g in range(GROUPS):
                step_b(pe, g, 0, C0)
            for g in range(GROUPS):
                pe.matmul(bank[g][0], w_a, warm[1][:, cols[g]], start=False, stop=True).then_inc(summed[g], 1)
                step_b(pe, g, 1, C0 + 1)

            def warm_step(k, par):
                for g in range(GROUPS):
                    step_a(pe, g, par, warm[1 - par][:, cols[g]], summed, stepped, k)
                    step_b(pe, g, 1 - par, k + (C0 + 1))
            over_steps(pe, WARM - 2, warm_step)
            for g in range(GROUPS):
                step_a(pe, g, WARM - 1, warm[0][:, cols[g]], summed, stepped, WARM - 1)
                step_b(pe, g, 0, 0)
            main_pass(pe, summed, stepped, WARM)
            pe.wait_ge(compared, GROUPS + 3)
            pe.matmul(m.bank[7][0:1, 0:1], m.agree[:, :], m.ones[:, :], start=True, stop=True).then_inc(counted, 1)

        @block.scalar
        def _(act):
            act.preload_act_table(ACT.Tanh)
            with act.Fori(0, WARM // 4) as u:
                for k in range(4):
                    for g in range(GROUPS):
                        act.wait_ge(summed[g], u * 4 + (k + 1))
                        act.activation(warm[k % 2][:, cols[g]], bank[g][k % 2], ACT.Tanh, bias=bias)\
                            .then_inc(stepped[g], 1)
            for g in range(GROUPS):
                act.wait_ge(stepped[g], WARM)
                act.activation(ending[g], by_row(warm[1][:, cols[g]]), ACT.Copy).then_inc(stepped[g], 1)
            main_states(act, summed, stepped, WARM)

    with m.nc.Block() as block:
        @block.tensor
        def _(pe):
            agreeing = pe.value_load(m.flag[0:1, 0:1], min_val=0, max_val=128)
            with pe.If(agreeing < 128):
                with pe.Fori(0, ROWS - 1) as rep:
                    for g in range(GROUPS):
                        at = rep * MAIN + 1
                        pe.wait_ge(again_stepped[g], at)
                        step_b(pe, g, 0, 0)
                    main_pass(pe, again_summed, again_stepped, rep * MAIN)

        @block.scalar
        def _(act):
            agreeing = act.value_load(m.flag[0:1, 0:1], min_val=0, max_val=128)
            with act.If(agreeing < 128):
                with act.Fori(0, ROWS - 1) as rep:
                    for g in range(GROUPS):
                        act.activation(ending[g], by_row(hs[:, COLS - 1, cols[g]]), ACT.Copy)\
                            .then_inc(again_stepped[g], 1)
                    main_states(act, again_summed, again_stepped, rep * COLS)
                    for g in range(GROUPS):
                        act.wait_ge(again_stepped[g], rep * MAIN + MAIN)


def mix_and_norm(m, layer):
    sem, ALU, ACT = m.sem, m.ALU, m.ACT
    STEPS = CHUNKS * COLS // NT
    hs, x = m.big2, m.big1
    b_y, b_v = m.bank[0:4], m.bank[4:6]
    w_c, w_d = m.wt[:, W_C0 + layer, :], m.wt[:, W_D0 + layer, :]
    bias = m.dvec[:, D_C0 + layer:D_C0 + layer + 1]
    M = Names()
    M.mixed, M.squared, M.variance, M.log = (sem(f"mix{layer}_" + n) for n in ("mixed", "squared", "variance", "log"))
    M.rstd, M.written, M.rounded, M.rest = (sem(f"mix{layer}_" + n) for n in ("rstd", "written", "rounded", "rest"))
    square = m.ring
    rstd = (m.wt[:, W_Q:W_PROJ + 1, :].rearrange("p n c -> p (n c)"), m.const[:, C_MEAN64:C_MEAN64 + NT])

    def over_tiles(eng, slot):
        over_slots(eng, STEPS, slot, 2, 0)

    with m.nc.Block() as block:
        @block.tensor
        def _(pe):
            def slot(s, q):
                if within(s, STEPS):
                    at_least(pe, M.rest, s + 1)
                    at_least(pe, M.log, s - 1)
                    mean_product(m, pe, b_v[q % 2][:, :], 1, q % 2).then_inc(M.variance, 1)
                if within(s + 2, STEPS):
                    y = b_y[(q + 2) % 4][:, :]
                    at_least(pe, M.written, s - 1)
                    pe.matmul(y, w_c, hs[:, bass.ds((s + 2) * NT, NT)], start=True, stop=False)
                    pe.matmul(y, w_d, x[:, bass.ds((s + 2) * NT, NT)], start=False, stop=True).then_inc(M.mixed, 1)
            over_tiles(pe, slot)

        @block.scalar
        def _(act):
            def slot(s, q):
                if within(s, STEPS):
                    at_least(act, M.variance, s + 1)
                    at_least(act, M.written, s - 1)
                    act.activation(rstd[q % 2], b_v[q % 2][:, :], ACT.Ln, bias=m.eps[:, :]).then_inc(M.log, 1)
                    act.wait_ge(M.log, s + 1)
                    act.activation(rstd[q % 2], rstd[q % 2], ACT.Exp, scale=-0.5).then_inc(M.rstd, 1)
                if within(s + 2, STEPS):
                    at_least(act, M.mixed, s + 3)
                    at_least(act, M.rest, s + 1)
                    act.activation(square[:, q % 2, :], b_y[(q + 2) % 4][:, :], ACT.Square, bias=bias).then_inc(M.squared, 1)
            act.preload_act_table_set("natural_log_exp_and_others")
            over_tiles(act, slot)

        @block.vector
        def _(dve):
            def slot(s, q):
                if within(s + 1, STEPS):
                    at_least(dve, M.squared, s + 2)
                    at_least(dve, M.variance, s)
                    q1 = (q + 1) % 2
                    dve.tensor_copy(m.halves[:, 0, q1, :], square[:, q1, :]).then_inc(M.rounded, 1)
                    at_least(dve, M.rounded, s + 2)
                    dve.tensor_tensor(m.halves[:, 1, q1, :], square[:, q1, :], m.halves[:, 0, q1, :].bitcast(m.F32),
                                      ALU.subtract).then_inc(M.rest, 1)
                if within(s, STEPS):
                    at_least(dve, M.rstd, s + 1)
                    dve.scalar_tensor_tensor(x[:, bass.ds(s * NT, NT)], b_y[q][:, :], bias, rstd[q % 2],
                                             ALU.add, ALU.mult).then_inc(M.written, 1)
            over_tiles(dve, slot)


def routed_ffn(m):
    sem, ALU, ACT = m.sem, m.ALU, m.ACT
    cur = [0]

    def buf(*shape):
        n = int(np.prod(shape))
        v = m.big2[:, cur[0]:cur[0] + n]
        cur[0] += n
        names = "abcde"[:len(shape)]
        return v if len(shape) == 1 else v.rearrange(
            "p (" + " ".join(names) + ") -> p " + " ".join(names), **{c: s for c, s in zip(names, shape)})

    act1, act2 = buf(2, NT), buf(2, NT)
    RING = 4
    act3 = buf(RING, NT)
    expert = buf(LAYERS, RING, 2, HID + 1)
    final = buf(NT)
    result = buf(2, HALF, 4 * FEAT)
    h = m.h[:, :, :].rearrange("p r c -> p (r c)")
    out = m.out.rearrange("b s f -> (b s) f")
    stored = [sem(f"ffn_stored{k}") for k in range(2)]
    R = Names()
    R.expert, R.mm1, R.relu1, R.mm2 = (sem("ffn_" + n) for n in ("expert", "mm1", "relu1", "mm2"))
    R.relu2, R.mm3, R.relu3, R.mm4 = (sem("ffn_" + n) for n in ("relu2", "mm3", "relu3", "mm4"))
    R.final, R.turned, R.result = (sem("ffn_" + n) for n in ("final", "turned", "result"))
    b1, b2, b3, b_final, b_turned = m.bank[0:2], m.bank[2:4], m.bank[4:6], m.bank[6], m.bank[7]
    UNITS = HALF * TILES

    def over_units(eng, unit):
        for u in range(2 * RING):
            unit(u // 2, u % RING)
        with eng.Fori(2, TILES // 2) as v:
            for q in range(RING):
                unit(v * 2 + q // 2, q)
        for u in range(UNITS, UNITS + RING):
            unit(u // 2, u % RING)

    def runs(u, stage):
        return not isinstance(u, int) or 0 <= u - stage < UNITS

    with m.nc.Block() as block:
        @block.tensor
        def _(pe):
            def unit(t, q):
                par = q % 2
                u = t * 2 + par
                if runs(u, 0):
                    at_least(pe, R.relu1, u - 1)
                    pe.matmul(b1[par][:, :], m.wt[:, W_FIN0 + par, :], m.y[:, bass.ds(t * NT, NT)],
                              start=True, stop=True).then_inc(R.mm1, 1)
                for st, src, dst, ready, free, done in (
                        (1, act1[:, 1 - par], b2, R.relu1, R.relu2, R.mm2),
                        (2, act2[:, par], b3, R.relu2, R.relu3, R.mm3)):
                    if runs(u, st):
                        k = u - st
                        at_least(pe, ready, k + 1)
                        at_least(pe, free, k - 1)
                        at_least(pe, R.expert, k * 2 + 2)
                        for s in range(2):
                            c = slice(SEG * s, SEG * s + SEG)
                            last = pe.matmul(dst[(q - st) % 2][:, c], expert[:, st - 1, (q - st) % RING, s, 0:HID],
                                             src[:, c], start=True, stop=True)
                        last.then_inc(done, 1)
                if runs(u, 3):
                    at_least(pe, R.relu3, u - 2)
                    if par == 1:
                        at_least(pe, R.final, t - 1)
                    p = 1 - par
                    pe.matmul(b_final[64 * p:64 * p + 64, :], m.wt[:, W_FOUT, 0:FEAT], act3[:, (q - 3) % RING],
                              start=True, stop=True).then_inc(R.mm4, 1)
                if par == 1 and runs(u, 5):
                    at_least(pe, R.final, t - 1)
                    at_least(pe, R.result, t - 2)
                    for s in range(4):
                        last = pe.transpose(b_turned[:, 128 * s:128 * s + 128], final[:, s:NT:4],
                                            m.const[:, C_IDENT:C_IDENT + 128])
                    last.then_inc(R.turned, 1)
            over_units(pe, unit)

        @block.scalar
        def _(act):
            def unit(t, q):
                par = q % 2
                u = t * 2 + par
                if runs(u, 0):
                    at_least(act, R.mm1, u + 1)
                    at_least(act, R.mm2, u - 1)
                    act.activation(act1[:, par, :], b1[par][:, :], ACT.Relu, bias=m.vec[:, V_FI:V_FI + 1]).then_inc(R.relu1, 1)
                if runs(u, 1):
                    at_least(act, R.mm2, u)
                    at_least(act, R.mm3, u - 2)
                    for s in range(2):
                        c = slice(SEG * s, SEG * s + SEG)
                        last = act.activation(act2[:, 1 - par, c], b2[1 - par][:, c], ACT.Relu,
                                              bias=expert[:, 0, (q - 1) % RING, s, HID:HID + 1])
                    last.then_inc(R.relu2, 1)
            over_units(act, unit)

        @block.vector
        def _(dve):
            def unit(t, q):
                par = q % 2
                u = t * 2 + par
                if runs(u, 2):
                    k = u - 2
                    at_least(dve, R.mm3, k + 1)
                    at_least(dve, R.mm4, k - RING + 1)
                    for s in range(2):
                        c = slice(SEG * s, SEG * s + SEG)
                        last = dve.tensor_scalar(act3[:, (q - 2) % RING, c], b3[par][:, c],
                                                 expert[:, 1, (q - 2) % RING, s, HID:HID + 1], 0.0, ALU.add, ALU.max)
                    last.then_inc(R.relu3, 1)
                if par == 0 and runs(u, 4):
                    at_least(dve, R.mm4, u - 2)
                    at_least(dve, R.turned, t - 2)
                    dve.scalar_tensor_tensor(final, b_final[:, :], m.vec[:, V_BO:V_BO + 1],
                                             h[:, bass.ds((t - 2) * NT, NT)], ALU.add, ALU.add).then_inc(R.final, 1)
                if par == 1 and runs(u, 5):
                    slot = q // 2
                    at_least(dve, R.turned, t - 1)
                    at_least(dve, stored[slot], (t - 2 - slot) * 16)
                    dve.tensor_copy(result[:, slot].rearrange("i p (s f) -> i p s f", f=FEAT),
                                    b_turned[:, :].rearrange("i (s p f) -> i p s f", p=HALF, f=FEAT)).then_inc(R.result, 1)
            over_units(dve, unit)

        @block.gpsimd
        def _(pool):
            def unit(t, q):
                par = q % 2
                u = t * 2 + par
                if runs(u, 0):
                    at_least(pool, R.relu3, u - RING + 1)
                    if not isinstance(u, int):
                        stand_apart(pool, m.apart)
                    for s in range(2):
                        e = pool.value_load(m.route[0:1, bass.ds(t * 2 + (par * SEGS // 2 + s), 1)],
                                            min_val=0, max_val=EXPERTS)
                        pool.tensor_copy(expert[:, :, q, s, :],
                                         m.experts[:, :, bass.ds(e, 1), :].rearrange("p l a c -> p l (a c)"))\
                            .then_inc(R.expert, 1)
            over_units(pool, unit)

        @block.sync
        def _(sp):
            def unit(t, q):
                if q % 2 == 1 and runs(t * 2 + 1, 5):
                    slot = q // 2
                    at_least(sp, R.result, t - 1)
                    stand_apart(sp, m.apart)
                    for p in range(HALF):
                        sp.dma_start(out[bass.ds((t - 2) * NT + p * BROWS * COLS, NT), :]
                                     .rearrange("(i s) f -> i (s f)", s=4), result[:, slot, p]).then_inc(stored[slot], 16)
            over_units(sp, unit)
            for slot in range(2):
                sp.wait_ge(stored[slot], TILES * 16)


_INS = ["x", "L0_tok_qkv_w", "L0_tok_qkv_b", "L0_tok_proj_w", "L0_tok_proj_b", "L0_attn_in_W", "L0_attn_in_b",
        "L0_attn_A_W", "L0_attn_B_W", "L0_attn_B_b", "L0_attn_C_W", "L0_attn_C_b", "L0_attn_D_W", "L0_attn_D_b",
        "L0_attn_ln_w", "L0_attn_ln_b", "L0_attn_out_W", "L0_attn_out_b", "L0_ffn_route_id", "L0_ffn_Wi",
        "L0_ffn_bi", "L0_ffn_Wr", "L0_ffn_br", "L0_ffn_Ws", "L0_ffn_bs", "L0_ffn_Wo", "L0_ffn_bo"]


def kernel(**inputs):
    import concourse.bacc as _bacc
    from concourse.bass_utils import run_bass_kernel_spmd as _run

    nc = _bacc.Bacc("TRN2", target_bir_lowering=False, num_devices=1)
    arrays, a = {}, {}
    for name in _INS:
        v = np.ascontiguousarray(inputs[name])
        arrays["in_" + name] = v
        a[name] = nc.dram_tensor("in_" + name, v.shape, mybir.dt.from_np(v.dtype), kind="ExternalInput").ap()
    c = shape_constants()
    arrays["in_consts"] = c
    a["consts"] = nc.dram_tensor("in_consts", c.shape, mybir.dt.float32, kind="ExternalInput").ap()
    out = nc.dram_tensor("out", (BATCH, ROWS * COLS, FEAT), mybir.dt.float32, kind="ExternalOutput").ap()
    program(nc, a, out)
    r = _run(nc, [arrays], core_ids=[0])
    return r.results[0]["out"]
```
